# Optimizing a Trainium2 kernel written in Bass

```python
import numpy as np
import jax
import jax.numpy as jnp

def _softmax(x, axis=-1):
    return jax.nn.softmax(x, axis=axis)

def _gelu(x):
    return jax.nn.gelu(x, approximate=True)

def _silu(x):
    return jax.nn.silu(x)

def _sigmoid(x):
    return jax.nn.sigmoid(x)

def _layernorm(x, axis=-1, eps=1e-05):
    m = jnp.mean(x, axis=axis, keepdims=True)
    v = jnp.var(x, axis=axis, keepdims=True)
    return (x - m) / jnp.sqrt(v + eps)

def _scatter_add(tgt, idx, src, axis=0):
    return tgt.at[idx].add(src)

def _segment_sum(src, seg, n):
    return jax.ops.segment_sum(src, seg, n)
kernel_name = 'mk_seq_postln_d2_jaxref_r4_e2aebb'

def setup_inputs(seed: int=0):
    np.random.seed(seed)
    _w = jnp.asarray

    def _L0_attn_setup():
        import jax, jax.numpy as jnp
        import numpy as np
        import math
        D_MODEL = 256
        N_HEADS = 16
        D_K = D_MODEL // N_HEADS
        BATCH = 4
        SEQ = 512
        TRAINING_PROGRESS = 0.25
        CONVERGENCE_PHASE = 0.5
        TENSION = abs(1.0 - 1.0)

        def _pos_encoding(seq_len, d, yellow):
            phase_mod = 0.1 * math.sin(2.0 * math.pi * TRAINING_PROGRESS)
            i_even = jnp.arange(0, d, 2, dtype=jnp.float32)
            denom = jnp.power(10000.0, 2.0 * i_even / d) * (1.0 + yellow * phase_mod)
            pos = jnp.arange(seq_len, dtype=jnp.float32)
            ang = pos[:, None] / denom[None, :]
            pe = jnp.zeros((seq_len, d), jnp.float32)
            pe = pe.at[:, 0::2].set(jnp.sin(ang))
            pe = pe.at[:, 1::2].set(jnp.cos(ang))
            return pe
        key = jax.random.key(seed)
        ks = jax.random.split(key, 8)
        x = jax.random.normal(ks[0], (BATCH, SEQ, D_MODEL), dtype=jnp.float32)
        rby = jax.random.uniform(ks[1], (3,), dtype=jnp.float32)
        s = 0.02
        Wq = jax.random.normal(ks[2], (D_MODEL, D_MODEL), dtype=jnp.float32) * s
        Wk = jax.random.normal(ks[3], (D_MODEL, D_MODEL), dtype=jnp.float32) * s
        Wv = jax.random.normal(ks[4], (D_MODEL, D_MODEL), dtype=jnp.float32) * s
        Wo = jax.random.normal(ks[5], (D_MODEL, D_MODEL), dtype=jnp.float32) * s
        bq = jnp.zeros((D_MODEL,), jnp.float32)
        bk = jnp.zeros((D_MODEL,), jnp.float32)
        bv = jnp.zeros((D_MODEL,), jnp.float32)
        bo = jnp.zeros((D_MODEL,), jnp.float32)
        ln_gamma = jnp.ones((D_MODEL,), jnp.float32)
        ln_beta = jnp.zeros((D_MODEL,), jnp.float32)
        return {'x': x, 'rby': rby, 'Wq': Wq, 'bq': bq, 'Wk': Wk, 'bk': bk, 'Wv': Wv, 'bv': bv, 'Wo': Wo, 'bo': bo, 'ln_gamma': ln_gamma, 'ln_beta': ln_beta}
    _L0_attn_in = _L0_attn_setup()

    def _L0_ffn_setup():
        import jax, jax.numpy as jnp
        import numpy as np
        import math
        BETA = 0.9
        THRESHOLD = 1.0
        NUM_STEPS = 5
        ALPHA = 2.0

        @jax.custom_vjp
        def spike_fn(u):
            return (u > 0).astype(u.dtype)

        def _spike_fwd(u):
            return (spike_fn(u), u)

        def _spike_bwd(u, g):
            s = jnp.pi / 2.0 * ALPHA * u
            return (g * (ALPHA / 2.0) / (1.0 + s * s),)
        spike_fn.defvjp(_spike_fwd, _spike_bwd)
        key = jax.random.key(seed)
        k1, k2, k3 = jax.random.split(key, 3)
        n_embd = 256
        x = jax.random.normal(k1, (4, 512, n_embd), dtype=jnp.float32)
        W_fc = jax.random.normal(k2, (4 * n_embd, n_embd), dtype=jnp.float32) / math.sqrt(n_embd)
        W_proj = jax.random.normal(k3, (n_embd, 4 * n_embd), dtype=jnp.float32) / math.sqrt(4 * n_embd)
        return {'x': x, 'W_fc': W_fc, 'W_proj': W_proj}
    _L0_ffn_in = _L0_ffn_setup()

    def _L1_attn_setup():
        import jax, jax.numpy as jnp
        import numpy as np
        B, T, D = (2, 1024, 256)
        H, DK, DV = (8, 128, 128)
        INTER = 1024
        CHUNK = 128
        EPS = 1e-05

        def rmsnorm(x, w, eps=EPS):
            return x * jax.lax.rsqrt(jnp.mean(x * x, axis=-1, keepdims=True) + eps) * w

        def linear_attention(x, Wq, Wk, Wv, Wo, out_norm_w):
            b, t, d = x.shape
            n = t // CHUNK
            q = (x @ Wq).reshape(b, t, H, DK).transpose(0, 2, 1, 3)
            k = (x @ Wk).reshape(b, t, H, DK).transpose(0, 2, 1, 3)
            v = (x @ Wv).reshape(b, t, H, DV).transpose(0, 2, 1, 3)
            qc = q.reshape(b, H, n, CHUNK, DK).transpose(2, 0, 1, 3, 4)
            kc = k.reshape(b, H, n, CHUNK, DK).transpose(2, 0, 1, 3, 4)
            vc = v.reshape(b, H, n, CHUNK, DV).transpose(2, 0, 1, 3, 4)
            causal = jnp.tril(jnp.ones((CHUNK, CHUNK), dtype=bool))

            def step(S, qkv):
                qb, kb, vb = qkv
                attn = jnp.einsum('bhid,bhjd->bhij', qb, kb)
                attn = jnp.where(causal, attn, 0.0)
                o = jnp.einsum('bhij,bhjv->bhiv', attn, vb) + jnp.einsum('bhid,bhdv->bhiv', qb, S)
                S = S + jnp.einsum('bhid,bhiv->bhdv', kb, vb)
                return (S, o)
            S0 = jnp.zeros((b, H, DK, DV), x.dtype)
            _, o = jax.lax.scan(step, S0, (qc, kc, vc))
            o = o.transpose(1, 2, 0, 3, 4).reshape(b, H, t, DV)
            o = rmsnorm(o, out_norm_w)
            o = o.transpose(0, 2, 1, 3).reshape(b, t, H * DV)
            return o @ Wo
        key = jax.random.key(seed)
        ks = jax.random.split(key, 9)
        s = 0.02
        return {'hidden_states': jax.random.normal(ks[0], (B, T, D), jnp.float32), 'attn_norm_w': jnp.ones((D,), jnp.float32), 'Wq': jax.random.normal(ks[1], (D, H * DK), jnp.float32) * s, 'Wk': jax.random.normal(ks[2], (D, H * DK), jnp.float32) * s, 'Wv': jax.random.normal(ks[3], (D, H * DV), jnp.float32) * s, 'Wo': jax.random.normal(ks[4], (H * DV, D), jnp.float32) * s, 'attn_out_norm_w': jnp.ones((DV,), jnp.float32), 'mlp_norm_w': jnp.ones((D,), jnp.float32), 'Wgate': jax.random.normal(ks[5], (D, INTER), jnp.float32) * s, 'Wup': jax.random.normal(ks[6], (D, INTER), jnp.float32) * s, 'Wdown': jax.random.normal(ks[7], (INTER, D), jnp.float32) * s}
    _L1_attn_in = _L1_attn_setup()

    def _L1_ffn_setup():
        import jax, jax.numpy as jnp
        import numpy as np
        DIM = 256
        HID = 512
        OUT = 256
        NE = 8
        TOPK = 2

        def _xavier(key, shape):
            fan_in, fan_out = (shape[-2], shape[-1])
            lim = jnp.sqrt(6.0 / (fan_in + fan_out))
            return jax.random.uniform(key, shape, jnp.float32, -lim, lim)
        key = jax.random.key(seed)
        ks = jax.random.split(key, 8)
        X = jax.random.normal(ks[0], (4, 256, DIM), jnp.float32)
        W1 = _xavier(ks[1], (NE, DIM, HID))
        W3 = _xavier(ks[2], (NE, DIM, HID))
        W2 = _xavier(ks[3], (NE, HID, OUT))
        b1 = jnp.zeros((NE, HID), jnp.float32)
        b3 = jnp.zeros((NE, HID), jnp.float32)
        b2 = jnp.zeros((NE, OUT), jnp.float32)
        Wg = _xavier(ks[4], (DIM, NE))
        bg = jnp.zeros((NE,), jnp.float32)
        Wf = _xavier(ks[5], (OUT, OUT))
        bf = jnp.zeros((OUT,), jnp.float32)
        return {'X': X, 'W1': W1, 'b1': b1, 'W3': W3, 'b3': b3, 'W2': W2, 'b2': b2, 'Wg': Wg, 'bg': bg, 'Wf': Wf, 'bf': bf}
    _L1_ffn_in = _L1_ffn_setup()
    _d = {'L0_attn_x': _L0_attn_in['x'], 'L0_attn_rby': _L0_attn_in['rby'], 'L0_attn_Wq': _L0_attn_in['Wq'], 'L0_attn_bq': _L0_attn_in['bq'], 'L0_attn_Wk': _L0_attn_in['Wk'], 'L0_attn_bk': _L0_attn_in['bk'], 'L0_attn_Wv': _L0_attn_in['Wv'], 'L0_attn_bv': _L0_attn_in['bv'], 'L0_attn_Wo': _L0_attn_in['Wo'], 'L0_attn_bo': _L0_attn_in['bo'], 'L0_attn_ln_gamma': _L0_attn_in['ln_gamma'], 'L0_attn_ln_beta': _L0_attn_in['ln_beta'], 'L0_ffn_W_fc': _L0_ffn_in['W_fc'], 'L0_ffn_W_proj': _L0_ffn_in['W_proj'], 'L1_attn_attn_norm_w': _L1_attn_in['attn_norm_w'], 'L1_attn_Wq': _L1_attn_in['Wq'], 'L1_attn_Wk': _L1_attn_in['Wk'], 'L1_attn_Wv': _L1_attn_in['Wv'], 'L1_attn_Wo': _L1_attn_in['Wo'], 'L1_attn_attn_out_norm_w': _L1_attn_in['attn_out_norm_w'], 'L1_attn_mlp_norm_w': _L1_attn_in['mlp_norm_w'], 'L1_attn_Wgate': _L1_attn_in['Wgate'], 'L1_attn_Wup': _L1_attn_in['Wup'], 'L1_attn_Wdown': _L1_attn_in['Wdown'], 'L1_ffn_W1': _L1_ffn_in['W1'], 'L1_ffn_b1': _L1_ffn_in['b1'], 'L1_ffn_W3': _L1_ffn_in['W3'], 'L1_ffn_b3': _L1_ffn_in['b3'], 'L1_ffn_W2': _L1_ffn_in['W2'], 'L1_ffn_b2': _L1_ffn_in['b2'], 'L1_ffn_Wg': _L1_ffn_in['Wg'], 'L1_ffn_bg': _L1_ffn_in['bg'], 'L1_ffn_Wf': _L1_ffn_in['Wf'], 'L1_ffn_bf': _L1_ffn_in['bf']}
    _x0 = _d['L0_attn_x']
    _d['L0_attn_x'] = jax.random.normal(jax.random.fold_in(jax.random.key(seed), 1), (2, 2048, 256), dtype=_x0.dtype)
    del _x0
    return _d

def reference(L0_attn_x, L0_attn_rby, L0_attn_Wq, L0_attn_bq, L0_attn_Wk, L0_attn_bk, L0_attn_Wv, L0_attn_bv, L0_attn_Wo, L0_attn_bo, L0_attn_ln_gamma, L0_attn_ln_beta, L0_ffn_W_fc, L0_ffn_W_proj, L1_attn_attn_norm_w, L1_attn_Wq, L1_attn_Wk, L1_attn_Wv, L1_attn_Wo, L1_attn_attn_out_norm_w, L1_attn_mlp_norm_w, L1_attn_Wgate, L1_attn_Wup, L1_attn_Wdown, L1_ffn_W1, L1_ffn_b1, L1_ffn_W3, L1_ffn_b3, L1_ffn_W2, L1_ffn_b2, L1_ffn_Wg, L1_ffn_bg, L1_ffn_Wf, L1_ffn_bf):

    def _L0_attn_ref(x, rby, Wq, bq, Wk, bk, Wv, bv, Wo, bo, ln_gamma, ln_beta):
        import jax, jax.numpy as jnp
        import numpy as np
        import math
        D_MODEL = 256
        N_HEADS = 16
        D_K = D_MODEL // N_HEADS
        BATCH = 4
        SEQ = 512
        TRAINING_PROGRESS = 0.25
        CONVERGENCE_PHASE = 0.5
        TENSION = abs(1.0 - 1.0)

        def _pos_encoding(seq_len, d, yellow):
            phase_mod = 0.1 * math.sin(2.0 * math.pi * TRAINING_PROGRESS)
            i_even = jnp.arange(0, d, 2, dtype=jnp.float32)
            denom = jnp.power(10000.0, 2.0 * i_even / d) * (1.0 + yellow * phase_mod)
            pos = jnp.arange(seq_len, dtype=jnp.float32)
            ang = pos[:, None] / denom[None, :]
            pe = jnp.zeros((seq_len, d), jnp.float32)
            pe = pe.at[:, 0::2].set(jnp.sin(ang))
            pe = pe.at[:, 1::2].set(jnp.cos(ang))
            return pe
        B, S, d = x.shape
        red, blue, yellow = (rby[0], rby[1], rby[2])
        x = x + _pos_encoding(S, d, yellow)[None, :, :]

        def proj(W, b):
            return (x @ W.T + b).reshape(B, S, N_HEADS, D_K).transpose(0, 2, 1, 3)
        Q, K, V = (proj(Wq, bq), proj(Wk, bk), proj(Wv, bv))
        scale = jnp.sqrt(D_K * (1.0 + TENSION * red))
        logits = jnp.einsum('bhqd,bhkd->bhqk', Q, K) / scale
        scale_matrix = 1.0 + red * 0.1 + blue * 0.05 + yellow * 0.15
        logits = logits * scale_matrix
        attn = jax.nn.softmax(logits, axis=-1)
        eps_adaptive = 0.1 * math.sin(2.0 * math.pi * CONVERGENCE_PHASE)
        out = jnp.einsum('bhqk,bhkd->bhqd', attn, V) * (1.0 + yellow * eps_adaptive)
        out = out.transpose(0, 2, 1, 3).reshape(B, S, d)
        out = out @ Wo.T + bo
        x = x + out
        mean = jnp.mean(x, axis=-1, keepdims=True)
        var = jnp.var(x, axis=-1, keepdims=True)
        eps_rby = 1e-05 * (1.0 + blue * 0.1)
        gamma_rby = ln_gamma * (1.0 + red * 0.1 + yellow * 0.05)
        normalized = (x - mean) / jnp.sqrt(var + eps_rby)
        return normalized * gamma_rby + ln_beta

    def _L0_ffn_ref(x, W_fc, W_proj):
        import jax, jax.numpy as jnp
        import numpy as np
        import math
        BETA = 0.9
        THRESHOLD = 1.0
        NUM_STEPS = 5
        ALPHA = 2.0

        @jax.custom_vjp
        def spike_fn(u):
            return (u > 0).astype(u.dtype)

        def _spike_fwd(u):
            return (spike_fn(u), u)

        def _spike_bwd(u, g):
            s = jnp.pi / 2.0 * ALPHA * u
            return (g * (ALPHA / 2.0) / (1.0 + s * s),)
        spike_fn.defvjp(_spike_fwd, _spike_bwd)
        h = jnp.square(jax.nn.relu(jnp.einsum('bsd,fd->bsf', x, W_fc)))
        y = jnp.einsum('bsf,df->bsd', h, W_proj)

        def step(mem, _):
            reset = jax.lax.stop_gradient(spike_fn(mem - THRESHOLD))
            mem_new = BETA * mem + y - reset * THRESHOLD
            spk = spike_fn(mem_new - THRESHOLD)
            return (mem_new, spk)
        mem0 = jnp.zeros_like(y)
        _, spks = jax.lax.scan(step, mem0, None, length=NUM_STEPS)
        return jnp.sum(spks, axis=0) / NUM_STEPS

    def _L1_attn_ref(hidden_states, attn_norm_w, Wq, Wk, Wv, Wo, attn_out_norm_w, mlp_norm_w, Wgate, Wup, Wdown):
        import jax, jax.numpy as jnp
        import numpy as np
        B, T, D = (2, 1024, 256)
        H, DK, DV = (8, 128, 128)
        INTER = 1024
        CHUNK = 128
        EPS = 1e-05

        def rmsnorm(x, w, eps=EPS):
            return x * jax.lax.rsqrt(jnp.mean(x * x, axis=-1, keepdims=True) + eps) * w

        def linear_attention(x, Wq, Wk, Wv, Wo, out_norm_w):
            b, t, d = x.shape
            n = t // CHUNK
            q = (x @ Wq).reshape(b, t, H, DK).transpose(0, 2, 1, 3)
            k = (x @ Wk).reshape(b, t, H, DK).transpose(0, 2, 1, 3)
            v = (x @ Wv).reshape(b, t, H, DV).transpose(0, 2, 1, 3)
            qc = q.reshape(b, H, n, CHUNK, DK).transpose(2, 0, 1, 3, 4)
            kc = k.reshape(b, H, n, CHUNK, DK).transpose(2, 0, 1, 3, 4)
            vc = v.reshape(b, H, n, CHUNK, DV).transpose(2, 0, 1, 3, 4)
            causal = jnp.tril(jnp.ones((CHUNK, CHUNK), dtype=bool))

            def step(S, qkv):
                qb, kb, vb = qkv
                attn = jnp.einsum('bhid,bhjd->bhij', qb, kb)
                attn = jnp.where(causal, attn, 0.0)
                o = jnp.einsum('bhij,bhjv->bhiv', attn, vb) + jnp.einsum('bhid,bhdv->bhiv', qb, S)
                S = S + jnp.einsum('bhid,bhiv->bhdv', kb, vb)
                return (S, o)
            S0 = jnp.zeros((b, H, DK, DV), x.dtype)
            _, o = jax.lax.scan(step, S0, (qc, kc, vc))
            o = o.transpose(1, 2, 0, 3, 4).reshape(b, H, t, DV)
            o = rmsnorm(o, out_norm_w)
            o = o.transpose(0, 2, 1, 3).reshape(b, t, H * DV)
            return o @ Wo
        x = hidden_states
        h = rmsnorm(x, attn_norm_w)
        x = x + linear_attention(h, Wq, Wk, Wv, Wo, attn_out_norm_w)
        h = rmsnorm(x, mlp_norm_w)
        x = x + jax.nn.silu(h @ Wgate) * (h @ Wup) @ Wdown
        return x

    def _L1_ffn_ref(X, W1, b1, W3, b3, W2, b2, Wg, bg, Wf, bf):
        import jax, jax.numpy as jnp
        import numpy as np
        DIM = 256
        HID = 512
        OUT = 256
        NE = 8
        TOPK = 2

        def _xavier(key, shape):
            fan_in, fan_out = (shape[-2], shape[-1])
            lim = jnp.sqrt(6.0 / (fan_in + fan_out))
            return jax.random.uniform(key, shape, jnp.float32, -lim, lim)
        gating = jax.nn.softmax(X @ Wg + bg, axis=-1)
        top_k_indices = jnp.argsort(gating, axis=-1)[..., -TOPK:]
        h1 = jnp.einsum('bsd,edh->bseh', X, W1) + b1
        h3 = jnp.einsum('bsd,edh->bseh', X, W3) + b3
        h = jax.nn.silu(h1 * h3)
        expert_outputs = jnp.einsum('bseh,eho->bseo', h, W2) + b2
        topk_out = jnp.take_along_axis(expert_outputs, top_k_indices[..., None], axis=2)
        topk_w = jnp.take_along_axis(gating, top_k_indices, axis=-1)
        mixed = jnp.sum(topk_w[..., None] * topk_out, axis=2)
        return mixed @ Wf + bf
    x = L0_attn_x
    x = _layernorm(x + _L0_attn_ref(x, L0_attn_rby, L0_attn_Wq, L0_attn_bq, L0_attn_Wk, L0_attn_bk, L0_attn_Wv, L0_attn_bv, L0_attn_Wo, L0_attn_bo, L0_attn_ln_gamma, L0_attn_ln_beta), axis=-1)
    x = _layernorm(x + _L0_ffn_ref(x, L0_ffn_W_fc, L0_ffn_W_proj), axis=-1)
    x = _layernorm(x + _L1_attn_ref(x, L1_attn_attn_norm_w, L1_attn_Wq, L1_attn_Wk, L1_attn_Wv, L1_attn_Wo, L1_attn_attn_out_norm_w, L1_attn_mlp_norm_w, L1_attn_Wgate, L1_attn_Wup, L1_attn_Wdown), axis=-1)
    x = _layernorm(x + _L1_ffn_ref(x, L1_ffn_W1, L1_ffn_b1, L1_ffn_W3, L1_ffn_b3, L1_ffn_W2, L1_ffn_b2, L1_ffn_Wg, L1_ffn_bg, L1_ffn_Wf, L1_ffn_bf), axis=-1)
    return x

_drawn_inputs = setup_inputs


def setup_inputs(seed=0):
    import zlib

    import numpy as np

    out = dict(_drawn_inputs(seed))
    spreads = {'L0_attn_bq': (0.0, 0.8),
     'L0_attn_bk': (0.0, 0.8),
     'L0_attn_bv': (0.0, 0.1),
     'L0_attn_bo': (0.0, 0.1),
     'L0_attn_ln_gamma': (1.0, 0.2),
     'L0_attn_ln_beta': (0.0, 0.1),
     'L1_attn_attn_norm_w': (1.0, 0.2),
     'L1_attn_attn_out_norm_w': (1.0, 0.2),
     'L1_attn_mlp_norm_w': (1.0, 0.6),
     'L1_ffn_b1': (0.0, 0.268),
     'L1_ffn_b3': (0.0, 0.275),
     'L1_ffn_b2': (0.0, 0.1),
     'L1_ffn_bg': (0.0, 0.1),
     'L1_ffn_bf': (0.0, 0.1)}
    factors = {'L0_attn_Wq': 8.0, 'L0_attn_Wk': 8.0}
    for name, (base, spread) in spreads.items():
        noise = np.random.default_rng([zlib.crc32(name.encode()), seed]).standard_normal(out[name].shape)
        drawn = base * np.exp(spread * noise) if base else spread * noise
        out[name] = jnp.asarray(drawn.astype(out[name].dtype))
    for name, factor in factors.items():
        out[name] = (out[name] * factor).astype(out[name].dtype)
    return out
```

```python
import math
from contextlib import ExitStack

import numpy as np

import concourse.bass as bass
from concourse import mybir

F32 = mybir.dt.float32
BF16 = mybir.dt.bfloat16
ALU = mybir.AluOpType
ACT = mybir.ActivationFunctionType
AX = mybir.AxisListType
ds = bass.ds

P = 128
BATCH, SEQ, D = 2, 2048, 256
TILES = BATCH * SEQ // P
TPB = SEQ // P
KD = D // P
HEADS, DK = 16, 16
PAIRS = BATCH * HEADS
VW = DK + 1
PARTS = 3
STACK = 6 * DK
SHIFT = TPB
QB = SEQ // 512
GT = 4
GROUPS = TILES // GT


class Names:
    pass


class Chain:

    def __init__(self, eng, sem, base=0):
        self.eng, self.sem, self.base, self.n = eng, sem, base, 0

    def mark(self, ins):
        ins.then_inc(self.sem, 1)
        self.n += 1
        return self.base + self.n

    def link(self, ins):
        self.eng.wait_ge(self.sem, self.mark(ins))


def wait(eng, sem, value):
    if not isinstance(value, int) or value > 0:
        eng.wait_ge(sem, value)


def hold(eng, sem, value, held):
    eng.wait_ge(sem, value)
    eng.sem_inc(held, 1)


def run_rounds(eng, body, rounds):
    body(0)
    with eng.Fori(1, rounds) as r:
        body(r)


def part_views(ap):
    return ap.rearrange("(t p) d -> p t d", p=P)


def embed_and_project(nc, io, mem, sem):
    ctx = ExitStack()
    with ctx:
        def sb(name, shape, dt=F32):
            return ctx.enter_context(nc.sbuf_tensor(name, shape, dt))

        def ps(name, shape):
            return ctx.enter_context(nc.psum_tensor(name, shape, F32))

        wq, wk, wv = (sb(n, [P, KD, D]) for n in ("wq", "wk", "wv"))
        bq, bk = sb("bq", [P, KD]), sb("bk", [P, KD])
        bqc = sb("bqc", [P, KD])
        bv = sb("bv", [P, D])
        pos, powers = sb("pos", [P, TPB]), sb("powers", [P, P])
        denom = sb("denom", [P, P])
        spare = mem.attn[:, :, :, :].rearrange("p s t d -> p (s t d)")
        angle, turns, reduced = (spare[:, SEQ * i:SEQ * i + SEQ].rearrange("p (t f) -> p t f", f=P) for i in range(3))
        scal = sb("scal", [P, 8])
        x0 = mem.qst[:, 0:2, :].rearrange("p a t -> p (a t)").bitcast(F32).rearrange("p (j t d) -> p j t d", j=2, d=D)
        x0T = sb("x0T", [P, 2, KD, 512])
        qkf = sb("qkf", [P, 2, KD, 512])
        parts = sb("parts", [P, 2, 2, PARTS, KD, 512], BF16)
        pT, pQ, pK, pV = (ps(n, [P, KD, 512]) for n in ("pT", "pQ", "pK", "pV"))
        x_in, c_in = sem("a_x_in"), sem("a_c_in")
        dve_s, act_s = sem("a_dve"), sem("a_act")
        square_ready, root_ready = sem("a_square"), sem("a_root")
        angles_ready, enc_ready = sem("a_angles"), sem("a_enc")
        x0_ready, x0_used = sem("a_x0"), sem("a_x0_used")
        xT_ready, xT_copied = sem("a_xT"), sem("a_xT_copied")
        q_ready, k_ready, v_ready = sem("a_q"), sem("a_k"), sem("a_v")
        q_out, k_out, v_out = sem("a_q_out"), sem("a_k_out"), sem("a_v_out")
        p1, r1, p2, p3 = (sem(f"a_{n}") for n in ("p1", "r1", "p2", "p3"))
        stored = [sem(f"a_stored{j}") for j in range(2)]
        ready0 = sem("a_ready0")
        enc_v = mem.enc[:, :, :].rearrange("p t (f two) -> p t f two", two=2)
        CONSTS = 13
        N_DVE0 = 24

        block = ctx.enter_context(nc.Block())

        @block.sync
        def _(sp):
            for dst, src in ((pos, io.pos), (powers, io.powers), (mem.rby, io.rby),
                             (mem.ident, io.ident), (wq, io.wq), (wk, io.wk), (wv, io.wv),
                             (bv, io.bv), (bq, io.bq), (bk, io.bk), (mem.delta, io.delta)):
                sp.dma_start(dst[:], src).then_inc(c_in, 16)
            sp.dma_start(mem.xs[:, 0:TPB, :], part_views(io.x)[:, 0:TPB, :]).then_inc(x_in, 16)
            sp.dma_start(mem.xs[:, TPB:, :], part_views(io.x)[:, TPB:, :]).then_inc(x_in, 16)

            def store(pair):
                for g in range(2):
                    b, slot = pair // 2, (2 * pair + g) % GT
                    sp.wait_ge(p3, 4 * pair + 2 * g + 2)
                    for w, scratch in ((0, io.q_parts), (1, io.k_parts)):
                        for s in range(PARTS):
                            dst = scratch[s, ds(b, 1), :, ds(512 * slot, 512)]
                            sp.dma_start(dst.rearrange("o (m p) t -> p (o m) t", p=P),
                                         parts[:, g, w, s, :, :]).then_inc(stored[g], 16)

            run_rounds(sp, store, GROUPS // 2)
            for j in range(2):
                sp.wait_ge(stored[j], 4 * 96)

        @block.gpsimd
        def _(pool):
            nc.gpsimd.memset(mem.minus_half[:], -0.5).then_inc(ready0, 1)
            pool.wait_ge(ready0, 1)
            pool.wait_ge(square_ready, 1)
            nc.gpsimd.tensor_tensor(scal[:, 5:6], scal[:, 7:8], mem.minus_half[:, 0:1], ALU.pow).then_inc(root_ready, 1)
            nc.gpsimd.memset(mem.values[:, :, :, DK:VW], 1.0).then_inc(ready0, 1)
            nc.gpsimd.memset(mem.vstage[:], 0.0).then_inc(ready0, 1)
            pool.wait_ge(ready0, 3)
            nc.gpsimd.memset(mem.kst[STACK:STACK + SHIFT, :, :], 1.0).then_inc(ready0, 1)
            pool.wait_ge(ready0, 4)

        @block.scalar
        def _(act):
            act.wait_ge(angles_ready, 1)
            nc.scalar.activation(enc_v[:, :, :, 0], reduced, ACT.Sin).then_inc(enc_ready, 1)
            act.wait_ge(angles_ready, 2)
            nc.scalar.activation(enc_v[:, :, :, 1], turns, ACT.Sin).then_inc(enc_ready, 1)

            def pair_of_groups(pair):
                for g in range(2):
                    n = 2 * pair + g + 1
                    act.wait_ge(xT_ready, n)
                    nc.scalar.activation(x0T[:, g % 2], pT[:], ACT.Copy).then_inc(xT_copied, 1)
                    wait(act, p3, 2 * n - 2)
                    act.wait_ge(q_ready, n)
                    for m in range(KD):
                        last = nc.scalar.activation(qkf[:, 0, m], pQ[:, m], ACT.Identity,
                                                    bias=bqc[:, m:m + 1], scale=mem.logit_scale[:, 0:1])
                    last.then_inc(q_out, 1)
                    act.wait_ge(k_ready, n)
                    for m in range(KD):
                        last = nc.scalar.activation(qkf[:, 1, m], pK[:, m], ACT.Identity,
                                                    bias=bk[:, m:m + 1])
                    last.then_inc(k_out, 1)
                    wait(act, stored[g], 96 * pair)
                    for w, done in ((0, q_out), (1, k_out)):
                        act.wait_ge(done, n)
                        nc.scalar.activation(parts[:, g % 2, w, 0], qkf[:, w], ACT.Copy).then_inc(p1, 1)
                    for w in range(2):
                        act.wait_ge(r1, 2 * n - 1 + w)
                        nc.scalar.activation(parts[:, g % 2, w, 1], qkf[:, w], ACT.Copy).then_inc(p2, 1)

            run_rounds(act, pair_of_groups, GROUPS // 2)

        @block.vector
        def _(dve):
            ch = Chain(dve, dve_s)
            dve.wait_ge(c_in, 11 * 16)
            red, blue, yellow = (mem.rby[:, i:i + 1] for i in range(3))
            v = nc.vector
            ch.link(v.tensor_scalar(scal[:, 0:1], yellow, 0.1 * math.sin(0.5 * math.pi), 1.0, ALU.mult, ALU.add))
            ch.link(v.tensor_scalar(denom[:], powers[:], scal[:, 0:1], None, ALU.mult))
            ch.link(v.reciprocal(denom[:], denom[:]))
            ch.link(v.tensor_tensor(angle, pos[:, :].unsqueeze(2).to_broadcast([P, TPB, P]),
                                    denom[:, :].unsqueeze(1).to_broadcast([P, TPB, P]), ALU.mult))
            two_pi = 2 * math.pi
            c1 = float(np.float32(6.28125))
            c2 = float(np.float32(two_pi - c1))
            c2 = math.floor(c2 * 2 ** 21) / 2 ** 21
            c3 = two_pi - c1 - c2
            magic = 1.5 * 2 ** 23
            for quarter, dst in ((0, reduced), (1, turns)):
                if quarter:
                    dve.wait_ge(enc_ready, 1)
                whole = turns if not quarter else reduced
                ch.link(v.tensor_scalar(whole, angle, 1 / two_pi, 0.25 * quarter, ALU.mult, ALU.add))
                ch.link(v.tensor_scalar(whole, whole, magic, magic, ALU.add, ALU.subtract))
                ch.link(v.scalar_tensor_tensor(dst, whole, -c1, angle, ALU.mult, ALU.add))
                ch.link(v.scalar_tensor_tensor(dst, whole, -c2, dst, ALU.mult, ALU.add))
                ch.link(v.scalar_tensor_tensor(dst, whole, -c3, dst, ALU.mult, ALU.add))
                if quarter:
                    ch.link(v.tensor_scalar(dst, dst, math.pi / 2, None, ALU.add))
                v.tensor_scalar(dst, dst, 3.1415925, -3.1415925, ALU.min, ALU.max).then_inc(angles_ready, 1)
            ch.link(v.tensor_scalar(scal[:, 1:2], red, 0.1, 1.0, ALU.mult, ALU.add))
            ch.link(v.scalar_tensor_tensor(scal[:, 2:3], blue, 0.05, scal[:, 1:2], ALU.mult, ALU.add))
            ch.link(v.scalar_tensor_tensor(scal[:, 3:4], yellow, 0.15, scal[:, 2:3], ALU.mult, ALU.add))
            ch.link(v.tensor_scalar(scal[:, 4:5], red, 0.0, 1.0, ALU.mult, ALU.add))
            v.tensor_scalar(scal[:, 7:8], scal[:, 4:5], float(DK), None, ALU.mult).then_inc(square_ready, 1)
            dve.wait_ge(root_ready, 1)
            ch.link(v.tensor_tensor(mem.logit_scale[:, 0:1], scal[:, 3:4], scal[:, 5:6], ALU.mult))
            ch.link(v.tensor_scalar(bqc[:], bq[:], mem.logit_scale[:, 0:1], None, ALU.mult))
            ch.link(v.tensor_scalar(mem.out_scale[:, 0:1], yellow, 0.1 * math.sin(math.pi), 1.0, ALU.mult, ALU.add))
            dve.wait_ge(x_in, 32)
            dve.wait_ge(enc_ready, 2)

            def pair_of_groups(pair):
                for g in range(2):
                    n = 2 * pair + g + 1
                    b, slot = pair // 2, (2 * pair + g) % GT
                    wait(dve, xT_ready, n - 2)
                    v.tensor_tensor(x0[:, g % 2], mem.xs[:, ds(GT * (2 * pair + g), GT), :],
                                    mem.enc[:, ds(GT * slot, GT), :], ALU.add).then_inc(x0_ready, 1)
                    dve.wait_ge(v_ready, n)
                    v.tensor_tensor(
                        mem.values[:, ds(HEADS * b, HEADS), ds(GT * slot, GT), 0:DK].rearrange("p h t d -> p t h d"),
                        pV[:].rearrange("p a (c h d) -> p (a c) h d", c=2, d=DK),
                        bv[:, :].rearrange("p (h d) -> p h d", d=DK).unsqueeze(1).to_broadcast([P, GT, HEADS, DK]),
                        ALU.add).then_inc(v_out, 1)
                    for w in range(2):
                        dve.wait_ge(p1, 2 * n - 1 + w)
                        v.tensor_tensor(qkf[:, w], qkf[:, w], parts[:, g % 2, w, 0], ALU.subtract).then_inc(r1, 1)
                    for w in range(2):
                        dve.wait_ge(p2, 2 * n - 1 + w)
                        v.tensor_tensor(parts[:, g % 2, w, 2], qkf[:, w], parts[:, g % 2, w, 1],
                                        ALU.subtract).then_inc(p3, 1)

            run_rounds(dve, pair_of_groups, GROUPS // 2)

        @block.tensor
        def _(pe):

            def pair_of_groups(pair):
                for g in range(2):
                    n = 2 * pair + g + 1
                    pe.wait_ge(x0_ready, n)
                    wait(pe, xT_copied, n - 1)
                    for t in range(GT):
                        for k in range(KD):
                            last = nc.tensor.transpose(pT[:, k, P * t:P * t + P],
                                                       x0[:, g % 2, t, P * k:P * k + P], mem.ident[:])
                    last.then_inc(xT_ready, 1)
                    pe.wait_ge(xT_copied, n)
                    for w, acc, done, free in ((wq, pQ, q_ready, q_out), (wk, pK, k_ready, k_out)):
                        wait(pe, free, n - 1)
                        for m in range(KD):
                            for k in range(KD):
                                last = nc.tensor.matmul(acc[:, m], w[:, k, P * m:P * m + P], x0T[:, g % 2, k],
                                                        start=k == 0, stop=k == KD - 1)
                        last.then_inc(done, 1)
                    wait(pe, v_out, n - 1)
                    for t in range(GT):
                        for k in range(KD):
                            last = nc.tensor.matmul(pV[:, t // 2, D * (t % 2):D * (t % 2) + D],
                                                    x0T[:, g % 2, k, P * t:P * t + P], wv[:, k],
                                                    start=k == 0, stop=k == KD - 1)
                    last.then_inc(v_ready, 1)

            run_rounds(pe, pair_of_groups, GROUPS // 2)


Q_PARTS, K_PARTS = (0, 0, 0, 1, 1, 2), (0, 1, 2, 0, 1, 0)


def attend(nc, io, mem, sem):
    ctx = ExitStack()
    with ctx:
        def sb(name, shape, dt=F32):
            return ctx.enter_context(nc.sbuf_tensor(name, shape, dt))

        def ps(name, shape):
            return ctx.enter_context(nc.psum_tensor(name, shape, F32))

        RING = 4
        AHEAD = 4
        qst, kst = mem.qst, mem.kst
        probs = sb("probs", [P, RING, SEQ])
        top = sb("top", [P, 2, TPB, QB])
        most = sb("most", [P, TPB])
        mostT = sb("mostT", [SHIFT, P], BF16)
        oT = sb("oT", [P, 512])
        recip = sb("recip", [P, QB, QB])
        scoresT, scores, outT = ps("scoresT", [P, 2, 1024]), ps("scores", [P, 2, 512]), ps("outT", [P, 2, 512])
        loaded = [sem(f"b_loaded{j}") for j in range(RING)]
        m_ready, m_used = sem("b_m_ready"), sem("b_m_used")
        e_ready, p_ready, pv_done = sem("b_e_ready"), sem("b_p_ready"), sem("b_pv_done")
        v_staged = sem("b_v_staged")
        most_ready, mostT_ready, mostT_cast, shift_ready = (sem(f"b_{x}") for x in ("most", "mostT", "mostT_cast", "shift"))
        o_copied, oT_ready, o_done = sem("b_o_copied"), sem("b_oT"), sem("b_o_done")
        dve_s = sem("b_dve")
        ROUNDS = PAIRS // RING
        LOADS = 16 * (len(Q_PARTS) + len(K_PARTS))

        def rounds(eng, body):
            body(0)
            with eng.Fori(1, ROUNDS - 1) as r:
                body(r)
            body(ROUNDS - 1)

        def ahead(kt):
            return 1 + (kt + AHEAD) // TPB, (kt + AHEAD) % TPB

        def is_last(r, j, of=PAIRS - 1):
            return isinstance(r, int) and RING * r + j >= of

        block = ctx.enter_context(nc.Block())

        @block.sync
        def _(sp):
            def load(s, j):
                for stack, scratch, order in ((qst, io.q_parts, Q_PARTS), (kst, io.k_parts, K_PARTS)):
                    rows = scratch.rearrange("s b f t -> s (b f) t")
                    for i, part in enumerate(order):
                        sp.dma_start(stack[DK * i:DK * i + DK, j, :], rows[part, ds(DK * s, DK), :]).then_inc(loaded[j], 16)

            for j in range(RING):
                load(j, j)

            def body(r):
                for j in range(RING):
                    if not is_last(r, j, PAIRS - RING):
                        sp.wait_ge(e_ready, 2 * TPB * (RING * r + j + 1))
                        load(RING * r + j + RING, j)

            rounds(sp, body)

        @block.gpsimd
        def _(pool):
            def shift(s, j):
                pool.wait_ge(mostT_cast, s + 1)
                pool.wait_ge(v_staged, s + 1)
                nc.gpsimd.tensor_tensor(
                    qst[STACK:STACK + SHIFT, j, :].rearrange("p (t q) -> p t q", q=P),
                    mostT[:, :].unsqueeze(1).to_broadcast([SHIFT, TPB, P]),
                    mem.delta[:, :].rearrange("p (t q) -> p t q", q=P), ALU.mult).then_inc(shift_ready, 1)

            def stage(s, j):
                wait(pool, shift_ready, s)
                nc.gpsimd.tensor_copy(mem.vstage[:, j % 2, :, 0:VW],
                                      mem.values[:, ds(s, 1), :, :].rearrange("p o t d -> p (o t) d")).then_inc(v_staged, 1)

            stage(0, 0)
            shift(0, 0)

            def body(r):
                for j in range(RING):
                    if not is_last(r, j):
                        s = RING * r + j
                        wait(pool, pv_done, TPB * s)
                        stage(s + 1, j + 1)
                        shift(s + 1, (j + 1) % RING)

            rounds(pool, body)

        @block.scalar
        def _(act):
            def cast_most(s, j):
                act.wait_ge(mostT_ready, s + 1)
                wait(act, shift_ready, s)
                nc.scalar.activation(mostT[:], outT[0:SHIFT, j % 2, 0:P], ACT.Copy, scale=-1.0).then_inc(mostT_cast, 1)

            def take_out(s, j):
                act.wait_ge(pv_done, TPB * (s + 1))
                wait(act, oT_ready, s)
                nc.scalar.activation(oT[:], outT[:, j % 2], ACT.Copy).then_inc(o_copied, 1)

            cast_most(0, 0)

            def body(r):
                for j in range(RING):
                    s = RING * r + j
                    for kt in range(TPB):
                        if kt == 1 and not (isinstance(r, int) and r == 0 and j == 0):
                            take_out(s - 1, j - 1)
                        if kt == 13 and not is_last(r, j):
                            cast_most(s + 1, j + 1)
                        wait(act, pv_done, TPB * s + kt - RING + 1)
                        for half in range(2):
                            act.wait_ge(e_ready, 2 * TPB * s + 2 * kt + half + 1)
                            nc.scalar.activation(probs[:, kt % RING, 1024 * half:1024 * half + 1024],
                                                 scoresT[:, half], ACT.Exp).then_inc(p_ready, 1)

            rounds(act, body)
            take_out(PAIRS - 1, RING - 1)

        @block.vector
        def _(dve):
            v = nc.vector
            ch = [0]

            def block_max(s, par, t, first=False):
                if t == 0:
                    wait(dve, most_ready, s - 1)
                for quarter in range(QB):
                    dve.wait_ge(m_ready, 4 * TPB * s + QB * t + quarter + 1)
                    v.reduce_max(top[:, par, t, quarter:quarter + 1], scores[:, quarter % 2], AX.X).then_inc(m_used, 1)

            def pair_max(s, par):
                dve.wait_ge(m_used, 4 * TPB * (s + 1))
                wait(dve, mostT_ready, s)
                v.reduce_max(most[:], top[:, par], AX.X).then_inc(most_ready, 1)

            def normalise(s, par):
                dve.wait_ge(oT_ready, s + 1)
                out = outT[:, par].rearrange("p (c j d) -> p c j d", j=QB, d=32)
                wait(dve, o_done, s)
                v.reciprocal(recip[:], out[:, :, :, DK]).then_inc(dve_s, 1)
                dve.wait_ge(dve_s, 2 * s + 1)
                v.tensor_scalar(recip[:], recip[:], mem.out_scale[:, 0:1], None, ALU.mult).then_inc(dve_s, 1)
                dve.wait_ge(dve_s, 2 * s + 2)
                v.tensor_tensor(mem.attn[:, ds(s, 1), :, :].rearrange("p o (j c) d -> p c (o j) d", c=QB),
                                out[:, :, :, 0:DK], recip[:, :, :].unsqueeze(3).to_broadcast([P, QB, QB, DK]),
                                ALU.mult).then_inc(o_done, 1)

            for t in range(TPB):
                block_max(0, 0, t)
            pair_max(0, 0)
            for t in range(AHEAD):
                block_max(1, 1, t)

            def body(r):
                for j in range(RING):
                    s = RING * r + j
                    for kt in range(TPB):
                        more, t = ahead(kt)
                        if kt == 3 and not (isinstance(r, int) and r == 0 and j == 0):
                            normalise(s - 1, (j - 1) % 2)
                        if kt == TPB - AHEAD and not is_last(r, j):
                            pair_max(s + 1, (j + 1) % 2)
                        if not is_last(r, j + more - 1):
                            block_max(s + more, (j + more) % 2, t)

            rounds(dve, body)
            normalise(PAIRS - 1, 1)

        @block.tensor
        def _(pe):
            def query_scores(s, r, j, t, quarter):
                if t == 0 and quarter == 0:
                    pe.wait_ge(loaded[j % RING], LOADS * (r + j // RING + 1))
                wait(pe, m_used, 4 * TPB * s + QB * t + quarter - 1)
                nc.tensor.matmul(scores[:, quarter % 2], qst[0:STACK, j % RING, P * t:P * t + P],
                                 kst[0:STACK, j % RING, 512 * quarter:512 * quarter + 512],
                                 start=True, stop=True).then_inc(m_ready, 1)

            def key_scores(s, j, kt, half):
                if kt == 0 and half == 0:
                    pe.wait_ge(shift_ready, s + 1)
                wait(pe, p_ready, 2 * TPB * s + 2 * kt + half - 1)
                for q in range(2):
                    last = nc.tensor.matmul(scoresT[:, half, 512 * q:512 * q + 512],
                                            kst[0:STACK + SHIFT, j % RING, P * kt:P * kt + P],
                                            qst[0:STACK + SHIFT, j % RING, 1024 * half + 512 * q:1024 * half + 512 * q + 512],
                                            start=True, stop=True)
                last.then_inc(e_ready, 1)

            def weigh_values(s, j, kt):
                if kt == 0:
                    pe.wait_ge(v_staged, s + 1)
                    wait(pe, o_done, s - 1)
                    pe.wait_ge(mostT_cast, s + 1)
                pe.wait_ge(p_ready, 2 * TPB * s + 2 * kt + 2)
                for q in range(QB):
                    last = nc.tensor.matmul(outT[32 * q:32 * q + 32, j % 2], mem.vstage[:, j % 2, kt, :],
                                            probs[:, kt % RING, 512 * q:512 * q + 512],
                                            start=kt == 0, stop=kt == TPB - 1)
                last.then_inc(pv_done, 1)

            def turn_out(s, j):
                pe.wait_ge(o_copied, s + 1)
                for c in range(QB):
                    last = nc.tensor.transpose(outT[:, j % 2, P * c:P * c + P], oT[:, P * c:P * c + P], mem.ident[:])
                last.then_inc(oT_ready, 1)

            def turn_most(s, j):
                pe.wait_ge(most_ready, s + 1)
                wait(pe, o_done, s - 1)
                nc.tensor.transpose(outT[0:SHIFT, j % 2, 0:P], most[:], mem.ident[:]).then_inc(mostT_ready, 1)

            for t in range(TPB):
                for quarter in range(QB):
                    query_scores(0, 0, 0, t, quarter)
            turn_most(0, 0)
            for t in range(AHEAD):
                for quarter in range(QB):
                    query_scores(1, 0, 1, t, quarter)

            def body(r):
                for j in range(RING):
                    s = RING * r + j
                    for kt in range(TPB):
                        more, t = ahead(kt)

                        def beside(quarter):
                            if not is_last(r, j + more - 1):
                                query_scores(s + more, r, j + more, t, quarter)

                        beside(0)
                        key_scores(s, j, kt, 0)
                        beside(1)
                        key_scores(s, j, kt, 1)
                        beside(2)
                        if kt:
                            weigh_values(s, j, kt - 1)
                        elif not (isinstance(r, int) and r == 0 and j == 0):
                            weigh_values(s - 1, j - 1, TPB - 1)
                        if kt == 2 and not (isinstance(r, int) and r == 0 and j == 0):
                            turn_out(s - 1, j - 1)
                        if kt == TPB - AHEAD and not is_last(r, j):
                            turn_most(s + 1, j + 1)
                        beside(3)

            rounds(pe, body)
            weigh_values(PAIRS - 1, RING - 1, TPB - 1)
            turn_out(PAIRS - 1, RING - 1)




def normalise_rows(dve, v, ch, work, src, dst, eps, asked, answered, count):
    tiles = src.shape[1]
    for t in range(tiles):
        last = ch.mark(v.bn_stats(work.stats[:, t], src[:, t]))
    hold(dve, ch.sem, last, work.held)
    for t in range(tiles):
        last = ch.mark(v.bn_aggr(work.moments[:, t], work.stats[:, t]))
    dve.wait_ge(ch.sem, last)
    v.tensor_scalar(work.var[:, 0:tiles], work.moments[:, 0:tiles, 1], eps, None, ALU.add).then_inc(asked, 1)
    dve.wait_ge(answered, count)
    for t in range(tiles):
        last = v.tensor_scalar(dst[:, t], src[:, t], work.moments[:, t, 0:1], work.rstd[:, t:t + 1],
                               ALU.subtract, ALU.mult)
    return last


def mix_and_spike(nc, io, mem, sem):
    ctx = ExitStack()
    with ctx:
        def sb(name, shape, dt=F32):
            return ctx.enter_context(nc.sbuf_tensor(name, shape, dt))

        def ps(name, shape):
            return ctx.enter_context(nc.psum_tensor(name, shape, F32))

        HID = 4 * D
        KH = HID // P
        wo, wfc, wproj = sb("wo", [P, KD, D]), sb("wfc", [P, KD, HID]), sb("wproj", [P, KH, D])
        bo, gamma, beta = sb("bo", [P, D]), sb("gamma", [P, D]), sb("beta", [P, D])
        scal = sb("c_scal", [P, 4])
        aT, x1T, hT = sb("aT", [P, KD, 512]), sb("x1T", [P, KD, 512]), sb("hT", [P, KH, 512])
        total, plain = sb("total", [P, GT, D]), sb("plain", [P, GT, D])
        heads_out, x1 = sb("heads_out", [P, GT, D]), sb("x1", [P, GT, D])
        y, count, rise, level = (sb(n, [P, GT, D]) for n in ("y", "count", "rise", "level"))
        work = Names()
        work.held = sem("c_held")
        work.stats, work.moments = sb("c_stats", [P, GT, 6]), sb("c_moments", [P, GT, 2])
        work.var, work.rstd = sb("c_var", [P, GT]), sb("c_rstd", [P, GT])
        turned, mixed, filled, spikes = (ps(n, [P, 2, 512]) for n in ("turned", "mixed", "filled", "spikes"))
        w_in, ready = sem("c_w_in"), sem("c_ready")
        sums_ready, heads_ready = sem("c_sums"), sem("c_heads")
        var_ready, rstd_ready = sem("c_var_ready"), sem("c_rstd_ready")
        aT_ready, aT_copied = sem("c_aT_ready"), sem("c_aT_copied")
        w_ready, w_used, x1_ready, x2_ready = sem("c_w_ready"), sem("c_w_used"), sem("c_x1_ready"), sem("c_x2_ready")
        x1_staged = sem("c_x1_staged")
        x1T_ready, x1T_copied = sem("c_x1T_ready"), sem("c_x1T_copied")
        f_ready, f_used, h_ready = sem("c_f_ready"), sem("c_f_used"), sem("c_h_ready")
        y_ready, y_copied = sem("c_y_ready"), sem("c_y_copied")
        dve_s = sem("c_dve")
        LINKS = 41

        block = ctx.enter_context(nc.Block())

        @block.sync
        def _(sp):
            for dst, src in ((bo, io.bo), (gamma, io.gamma), (beta, io.beta), (wo, io.wo), (wfc, io.wfc), (wproj, io.wproj)):
                sp.dma_start(dst[:], src).then_inc(w_in, 16)

        @block.gpsimd
        def _(pool):
            def power(n):
                pool.wait_ge(var_ready, n)
                nc.gpsimd.tensor_tensor(work.rstd[:], work.var[:], mem.minus_half[:, 0:GT], ALU.pow).then_inc(rstd_ready, 1)

            def sums(g, b, slot):
                wait(pool, aT_ready, g)
                nc.gpsimd.tensor_copy(heads_out[:, :, :].rearrange("p t (h d) -> p h t d", d=DK),
                                      mem.attn[:, ds(HEADS * b, HEADS), ds(GT * slot, GT), :]).then_inc(heads_ready, 1)
                wait(pool, x1_ready, g)
                nc.gpsimd.tensor_tensor(total[:], mem.xs[:, ds(GT * g, GT), :], mem.enc[:, ds(GT * slot, GT), :], ALU.add).then_inc(sums_ready, 1)
                nc.gpsimd.tensor_tensor(plain[:], mem.xs[:, ds(GT * g, GT), :],
                                        beta[:, :].unsqueeze(1).to_broadcast([P, GT, D]), ALU.add).then_inc(sums_ready, 1)

            pool.wait_ge(ready, 1)
            sums(0, 0, 0)
            power(1)
            power(2)

            def round_of(g):
                sums(g + 1, (g + 1) // (TPB // GT), (g + 1) % (TPB // GT))
                power(3 * g + 3)
                power(3 * g + 4)
                power(3 * g + 5)

            run_rounds(pool, round_of, GROUPS - 1)
            power(3 * GROUPS)

        @block.scalar
        def _(act):
            def copy_aT(g):
                act.wait_ge(aT_ready, g + 1)
                nc.scalar.activation(aT[:], turned[:], ACT.Copy).then_inc(aT_copied, 1)

            def net(g):
                act.wait_ge(x1T_ready, g + 1)
                nc.scalar.activation(x1T[:], turned[:], ACT.Copy).then_inc(x1T_copied, 1)
                for m in range(KH + 1):
                    if m < KH:
                        act.wait_ge(f_ready, KH * g + m + 1)
                        if m == 0:
                            wait(act, y_ready, g)
                        nc.scalar.activation(hT[:, m], filled[:, m % 2], ACT.Relu).then_inc(f_used, 1)
                    if m:
                        act.wait_ge(f_used, KH * g + m)
                        nc.scalar.activation(hT[:, m - 1], hT[:, m - 1], ACT.Square).then_inc(h_ready, 1)

            def stage_x1(g):
                act.wait_ge(x1_ready, g + 1)
                wait(act, x1T_ready, g)
                nc.scalar.activation(x1[:], mem.xs[:, ds(GT * g, GT), :], ACT.Copy).then_inc(x1_staged, 1)

            def copy_y(g):
                act.wait_ge(y_ready, g + 1)
                wait(act, x2_ready, g)
                nc.scalar.activation(y[:], spikes[:].rearrange("p a (c d) -> p (a c) d", d=D), ACT.Copy).then_inc(y_copied, 1)

            copy_aT(0)
            stage_x1(0)

            def round_of(g):
                net(g)
                copy_aT(g + 1)
                stage_x1(g + 1)
                copy_y(g)

            run_rounds(act, round_of, GROUPS - 1)
            net(GROUPS - 1)
            copy_y(GROUPS - 1)

        @block.vector
        def _(dve):
            v = nc.vector

            def wide(row):
                return row[:, :].unsqueeze(1).to_broadcast([P, GT, D])

            def norms(g, ch, n):
                dve.wait_ge(w_ready, g + 1)
                dve.wait_ge(sums_ready, 2 * g + 2)
                v.tensor_tensor(total[:], total[:], mixed[:].rearrange("p a (c d) -> p (a c) d", d=D), ALU.add).then_inc(w_used, 1)
                dve.wait_ge(w_used, g + 1)
                ch.link(normalise_rows(dve, v, ch, work, total, total, scal[:, 0:1], var_ready, rstd_ready, n))
                ch.link(v.tensor_tensor(total[:], total[:], wide(gamma), ALU.mult))
                ch.link(v.tensor_tensor(total[:], total[:], plain[:], ALU.add))
                normalise_rows(dve, v, ch, work, total, mem.xs[:, ds(GT * g, GT), :], 1e-5, var_ready, rstd_ready,
                               n + 1).then_inc(x1_ready, 1)

            def spike(g, ch, n):
                dve.wait_ge(y_copied, g + 1)
                ch.link(v.tensor_scalar(count[:], y[:], 1.0, None, ALU.is_gt))
                ch.link(v.scalar_tensor_tensor(rise[:], y[:], 0.9, y[:], ALU.mult, ALU.add))
                ch.link(v.tensor_tensor(level[:], count[:], rise[:], ALU.subtract))
                for step in range(3):
                    ch.mark(v.scalar_tensor_tensor(count[:], level[:], -1.0, count[:], ALU.is_lt, ALU.add))
                    ch.link(v.scalar_tensor_tensor(rise[:], level[:], -0.9, y[:], ALU.mult, ALU.add))
                    ch.link(v.scalar_tensor_tensor(level[:], level[:], -1.0, rise[:], ALU.is_lt, ALU.subtract))
                ch.link(v.scalar_tensor_tensor(count[:], level[:], -1.0, count[:], ALU.is_lt, ALU.add))
                xs = mem.xs[:, ds(GT * g, GT), :]
                dve.wait_ge(x1_staged, g + 1)
                ch.link(v.scalar_tensor_tensor(count[:], count[:], 0.2, xs, ALU.mult, ALU.add))
                normalise_rows(dve, v, ch, work, count, xs, 1e-5, var_ready, rstd_ready, n).then_inc(x2_ready, 1)

            ch = Chain(dve, dve_s)
            dve.wait_ge(w_in, 6 * 16)
            red, blue, yellow = (mem.rby[:, i:i + 1] for i in range(3))
            ch.link(v.tensor_scalar(scal[:, 0:1], blue, 1e-6, 1e-5, ALU.mult, ALU.add))
            ch.link(v.tensor_scalar(scal[:, 1:2], red, 0.1, 1.0, ALU.mult, ALU.add))
            ch.link(v.scalar_tensor_tensor(scal[:, 2:3], yellow, 0.05, scal[:, 1:2], ALU.mult, ALU.add))
            ch.link(v.tensor_scalar(gamma[:], gamma[:], scal[:, 2:3], None, ALU.mult))
            v.tensor_tensor(mem.enc[:], mem.enc[:], bo[:, :].unsqueeze(1).to_broadcast([P, TPB, D]), ALU.add).then_inc(ready, 1)
            norms(0, ch, 1)
            base = ch.n

            def round_of(g):
                ch = Chain(dve, dve_s, base + LINKS * g)
                norms(g + 1, ch, 3 * g + 3)
                spike(g, ch, 3 * g + 5)
                assert ch.n == LINKS, ch.n

            run_rounds(dve, round_of, GROUPS - 1)
            spike(GROUPS - 1, Chain(dve, dve_s, base + LINKS * (GROUPS - 1)), 3 * GROUPS)

        @block.tensor
        def _(pe):
            def mix(g):
                wait(pe, x1T_copied, g)
                pe.wait_ge(heads_ready, g + 1)
                for t in range(GT):
                    for k in range(KD):
                        last = nc.tensor.transpose(turned[:, k, P * t:P * t + P], heads_out[:, t, P * k:P * k + P], mem.ident[:])
                last.then_inc(aT_ready, 1)
                pe.wait_ge(aT_copied, g + 1)
                wait(pe, w_used, g)
                for t in range(GT):
                    for k in range(KD):
                        last = nc.tensor.matmul(mixed[:, t // 2, D * (t % 2):D * (t % 2) + D], aT[:, k, P * t:P * t + P],
                                                wo[:, k], start=k == 0, stop=k == KD - 1)
                last.then_inc(w_ready, 1)

            def first(g):
                pe.wait_ge(x1_staged, g + 1)
                for t in range(GT):
                    for k in range(KD):
                        last = nc.tensor.transpose(turned[:, k, P * t:P * t + P], x1[:, t, P * k:P * k + P], mem.ident[:])
                last.then_inc(x1T_ready, 1)
                pe.wait_ge(x1T_copied, g + 1)
                for m in range(KH):
                    wait(pe, f_used, KH * g + max(m - 1, 0))
                    for k in range(KD):
                        last = nc.tensor.matmul(filled[:, m % 2], wfc[:, k, P * m:P * m + P], x1T[:, k], start=k == 0, stop=k == KD - 1)
                    last.then_inc(f_ready, 1)

            def second(g):
                pe.wait_ge(h_ready, KH * (g + 1))
                wait(pe, y_copied, g)
                for t in range(GT):
                    for k in range(KH):
                        last = nc.tensor.matmul(spikes[:, t // 2, D * (t % 2):D * (t % 2) + D], hT[:, k, P * t:P * t + P],
                                                wproj[:, k], start=k == 0, stop=k == KH - 1)
                last.then_inc(y_ready, 1)

            pe.wait_ge(ready, 1)
            mix(0)

            def round_of(g):
                first(g)
                mix(g + 1)
                second(g)

            run_rounds(pe, round_of, GROUPS - 1)
            first(GROUPS - 1)
            second(GROUPS - 1)


def linear_attention_and_gate(nc, io, mem, sem):
    ctx = ExitStack()
    with ctx:
        def sb(name, shape, dt=F32):
            return ctx.enter_context(nc.sbuf_tensor(name, shape, dt))

        def ps(name, shape):
            return ctx.enter_context(nc.psum_tensor(name, shape, F32))

        NH = 8
        W = NH * P
        wq, wk, wv, wg, wu = (sb(f"d_{n}", [P, KD, W]) for n in ("wq", "wk", "wv", "wg", "wu"))
        wo, wd = sb("d_wo", [P, NH, D]), sb("d_wd", [P, NH, D])
        norm_in, norm_out, norm_mlp = sb("norm_in", [P, KD]), sb("norm_out", [P, 1]), sb("norm_mlp", [P, KD])
        causal, keep = sb("causal", [P, P]), sb("keep", [P, TILES + 1])
        square, wide_square = sb("square", [P, D]), sb("wide_square", [P, NH, P])
        ms, rs = sb("ms", [P, 2]), sb("rs", [P, 2])
        oms, ors = sb("oms", [P, NH]), sb("ors", [P, NH])
        h, h2 = sb("h", [P, D]), sb("h2", [P, D])
        hT, h2T = sb("d_hT", [P, KD, P]), sb("d_h2T", [P, KD, P])
        qT, kT, kt, v_, at, on, onT = (sb(f"d_{n}", [P, NH, P]) for n in ("qT", "kT", "kt", "v", "at", "on", "onT"))
        state = sb("state", [P, NH, P])
        mid, res = sb("mid", [P, D]), sb("res", [P, 1, D])
        gate, guT = sb("gate", [P, NH, P]), sb("guT", [P, NH, P])
        work = Names()
        work.held = sem("d_held")
        work.stats, work.moments = sb("d_stats", [P, 1, 6]), sb("d_moments", [P, 1, 2])
        work.var, work.rstd = sb("d_var", [P, 1]), sb("d_rstd", [P, 1])
        A, B, C, E = (ps(n, [P, 2, 512]) for n in "ABCE")
        heads_of = lambda bank: bank[:].rearrange("p a (h i) -> p (a h) i", i=P)
        names = ("w_in ready ms_eps oms_eps ms2_eps ms_ready rs_ready h_ready hT_ready hT_copied q_ready q_out k_ready k_out "
                 "v_ready v_out kt_ready kt_out at_ready at_out o_ready o_squared oms_ready ors_ready on_ready "
                 "kv_ready kv_used state_ready onT_ready onT_copied wo_ready mid_ready "
                 "ms2_ready rs2_ready h2_ready h2T_ready h2T_copied g_ready g_out u_ready gu_ready d_ready d_used "
                 "var_ready rstd_ready x_ready dve_s pool_held act_held").split()
        S = {n: sem(f"d_{n}") for n in names}

        def rounds(eng, side_by_side):
            run_rounds(eng, lambda c: side_by_side(c, True), TILES - 2)
            side_by_side(TILES - 2, False)

        block = ctx.enter_context(nc.Block())

        @block.sync
        def _(sp):
            for dst, src in ((norm_in, io.norm_in), (norm_out, io.norm_out), (norm_mlp, io.norm_mlp), (causal, io.causal),
                             (keep, io.keep), (wq, io.l1q), (wk, io.l1k), (wv, io.l1v), (wo, io.l1o), (wg, io.l1g),
                             (wu, io.l1u), (wd, io.l1d)):
                sp.dma_start(dst[:], src).then_inc(S["w_in"], 16)

        @block.gpsimd
        def _(pool):
            def input_root(c):
                hold(pool, S["ms_ready"], c + 1, S["pool_held"])
                nc.gpsimd.tensor_scalar(ms[:, 0:1], ms[:, 0:1], 1e-5, None, ALU.add).then_inc(S["ms_eps"], 1)
                pool.wait_ge(S["ms_eps"], c + 1)
                nc.gpsimd.tensor_tensor(rs[:, 0:1], ms[:, 0:1], mem.minus_half[:, 0:1], ALU.pow).then_inc(S["rs_ready"], 1)

            def output_roots(c):
                hold(pool, S["oms_ready"], c + 1, S["pool_held"])
                nc.gpsimd.tensor_scalar(oms[:], oms[:], 1.0 / P, 1e-5, ALU.mult, ALU.add).then_inc(S["oms_eps"], 1)
                pool.wait_ge(S["oms_eps"], c + 1)
                nc.gpsimd.tensor_tensor(ors[:], oms[:], mem.minus_half[:, 0:NH], ALU.pow).then_inc(S["ors_ready"], 1)

            def net_root(c):
                hold(pool, S["ms2_ready"], c + 1, S["pool_held"])
                nc.gpsimd.tensor_scalar(ms[:, 1:2], ms[:, 1:2], 1e-5, None, ALU.add).then_inc(S["ms2_eps"], 1)
                pool.wait_ge(S["ms2_eps"], c + 1)
                nc.gpsimd.tensor_tensor(rs[:, 1:2], ms[:, 1:2], mem.minus_half[:, 0:1], ALU.pow).then_inc(S["rs2_ready"], 1)

            def final_root(c):
                pool.wait_ge(S["var_ready"], c + 1)
                nc.gpsimd.tensor_tensor(work.rstd[:], work.var[:], mem.minus_half[:, 0:1], ALU.pow).then_inc(S["rstd_ready"], 1)

            def side_by_side(c, more):
                output_roots(c + 1)
                if more:
                    input_root(c + 2)
                final_root(c)
                net_root(c + 1)

            input_root(0)
            output_roots(0)
            input_root(1)
            net_root(0)
            rounds(pool, side_by_side)
            final_root(TILES - 1)

        @block.scalar
        def _(act):
            a = nc.scalar.activation

            def norm_input(c):
                xs = mem.xs[:, ds(c, 1), :].rearrange("p o d -> p (o d)")
                a(square[:], xs, ACT.Square, scale=D ** -0.5, accum_out=ms[:, 0:1]).then_inc(S["ms_ready"], 1)
                wait(act, S["hT_ready"], c)
                hold(act, S["rs_ready"], c + 1, S["act_held"])
                a(h[:], xs, ACT.Copy, scale=rs[:, 0:1]).then_inc(S["h_ready"], 1)
                act.wait_ge(S["hT_ready"], c + 1)
                wait(act, S["v_ready"], c)
                a(hT[:], E[:, 0, 0:D].rearrange("p (k t) -> p k t", k=KD), ACT.Copy).then_inc(S["hT_copied"], 1)

            def project(c):
                act.wait_ge(S["q_ready"], c + 1)
                wait(act, S["o_ready"], c)
                a(qT[:], heads_of(A), ACT.Copy).then_inc(S["q_out"], 1)
                act.wait_ge(S["v_ready"], c + 1)
                wait(act, S["kv_ready"], c)
                a(v_[:], heads_of(C), ACT.Copy).then_inc(S["v_out"], 1)
                act.wait_ge(S["kt_ready"], c + 1)
                a(kt[:], heads_of(E), ACT.Copy).then_inc(S["kt_out"], 1)

            def norm_output(c):
                act.wait_ge(S["o_ready"], c + 1)
                wait(act, S["oms_ready"], c)
                a(wide_square[:], heads_of(B), ACT.Square).then_inc(S["o_squared"], 1)

            def turn_output(c):
                act.wait_ge(S["onT_ready"], c + 1)
                wait(act, S["wo_ready"], c)
                a(onT[:], heads_of(C), ACT.Copy).then_inc(S["onT_copied"], 1)

            def net_input(c):
                act.wait_ge(S["mid_ready"], c + 1)
                a(square[:], mid[:], ACT.Square, scale=D ** -0.5, accum_out=ms[:, 1:2]).then_inc(S["ms2_ready"], 1)
                act.wait_ge(S["rs2_ready"], c + 1)
                wait(act, S["h2T_ready"], c)
                a(h2[:], mid[:], ACT.Copy, scale=rs[:, 1:2]).then_inc(S["h2_ready"], 1)

            def turn_net_input(c):
                act.wait_ge(S["h2T_ready"], c + 1)
                wait(act, S["u_ready"], c)
                a(h2T[:], E[:, 1, 0:D].rearrange("p (k t) -> p k t", k=KD), ACT.Copy).then_inc(S["h2T_copied"], 1)

            def silu(c):
                act.wait_ge(S["g_ready"], c + 1)
                wait(act, S["gu_ready"], c)
                a(gate[:], heads_of(C), ACT.Silu).then_inc(S["g_out"], 1)

            norm_input(0)
            project(0)
            norm_output(0)
            turn_output(0)
            norm_input(1)
            net_input(0)

            def side_by_side(c, more):
                project(c + 1)
                turn_net_input(c)
                silu(c)
                norm_output(c + 1)
                turn_output(c + 1)
                if more:
                    norm_input(c + 2)
                net_input(c + 1)

            rounds(act, side_by_side)
            turn_net_input(TILES - 1)
            silu(TILES - 1)

        @block.vector
        def _(dve):
            v = nc.vector

            def attention(c):
                dve.wait_ge(S["k_ready"], c + 1)
                wait(dve, S["at_ready"], c)
                v.tensor_copy(kT[:], heads_of(B)).then_inc(S["k_out"], 1)
                dve.wait_ge(S["at_ready"], c + 1)
                wait(dve, S["o_ready"], c)
                v.tensor_tensor(at[:], heads_of(A), causal[:, :].unsqueeze(1).to_broadcast([P, NH, P]), ALU.mult).then_inc(S["at_out"], 1)

            def output(c):
                dve.wait_ge(S["o_squared"], c + 1)
                wait(dve, S["ors_ready"], c)
                v.reduce_sum(oms[:], wide_square[:], AX.X).then_inc(S["oms_ready"], 1)
                dve.wait_ge(S["kv_ready"], c + 1)
                v.tensor_tensor(state[:], state[:], heads_of(A), ALU.add).then_inc(S["kv_used"], 1)
                dve.wait_ge(S["kv_used"], c + 1)
                v.tensor_scalar(state[:], state[:], keep[:, ds(c + 1, 1)], None, ALU.mult).then_inc(S["state_ready"], 1)
                dve.wait_ge(S["ors_ready"], c + 1)
                wait(dve, S["onT_ready"], c)
                v.tensor_tensor(on[:], heads_of(B), ors[:, :].unsqueeze(2).to_broadcast([P, NH, P]), ALU.mult).then_inc(S["on_ready"], 1)

            def gated(c):
                dve.wait_ge(S["g_out"], c + 1)
                dve.wait_ge(S["u_ready"], c + 1)
                wait(dve, S["d_ready"], c)
                v.tensor_tensor(guT[:], gate[:], heads_of(E), ALU.mult).then_inc(S["gu_ready"], 1)

            def finish(c):
                LINKS = 3
                ch = Chain(dve, S["dve_s"], LINKS * c)
                xs = mem.xs[:, ds(c, 1), :]
                dve.wait_ge(S["d_ready"], c + 1)
                v.tensor_tensor(res[:, 0], mid[:], A[:, 0, 0:D], ALU.add).then_inc(S["d_used"], 1)
                dve.wait_ge(S["h2_ready"], c + 1)
                dve.wait_ge(S["d_used"], c + 1)
                ch.link(v.tensor_tensor(res[:], res[:], xs, ALU.add))
                normalise_rows(dve, v, ch, work, res, xs, 1e-5, S["var_ready"], S["rstd_ready"], c + 1).then_inc(S["x_ready"], 1)
                assert ch.n == LINKS

            def middle(c):
                dve.wait_ge(S["wo_ready"], c + 1)
                xs = mem.xs[:, ds(c, 1), :].rearrange("p o d -> p (o d)")
                v.tensor_tensor(mid[:], xs, B[:, 0, 0:D], ALU.add).then_inc(S["mid_ready"], 1)

            dve.wait_ge(S["w_in"], 12 * 16)
            for w, norm in ((wq, norm_in), (wk, norm_in), (wv, norm_in), (wg, norm_mlp), (wu, norm_mlp)):
                for k in range(KD):
                    v.tensor_scalar(w[:, k], w[:, k], norm[:, k:k + 1], None, ALU.mult).then_inc(S["ready"], 1)
            v.tensor_scalar(wo[:], wo[:], norm_out[:, 0:1], None, ALU.mult).then_inc(S["ready"], 1)
            v.memset(state[:], 0.0).then_inc(S["ready"], 1)
            attention(0)
            output(0)
            middle(0)

            def side_by_side(c, more):
                attention(c + 1)
                output(c + 1)
                gated(c)
                finish(c)
                middle(c + 1)

            rounds(dve, side_by_side)
            gated(TILES - 1)
            finish(TILES - 1)

        @block.tensor
        def _(pe):
            mm, turn = nc.tensor.matmul, nc.tensor.transpose
            bank = lambda X, i: X[:, i // 4, P * (i % 4):P * (i % 4) + P]

            def start(c):
                pe.wait_ge(S["h_ready"], c + 1)
                for k in range(KD):
                    last = turn(E[:, 0, P * k:P * k + P], h[:, P * k:P * k + P], mem.ident[:])
                last.then_inc(S["hT_ready"], 1)

            def project(c):
                pe.wait_ge(S["hT_copied"], c + 1)
                for w, X, done in ((wq, A, S["q_ready"]), (wk, B, S["k_ready"])):
                    if w is wk:
                        wait(pe, S["mid_ready"], c)
                    for i in range(NH):
                        for k in range(KD):
                            last = mm(bank(X, i), w[:, k, P * i:P * i + P], hT[:, k], start=k == 0, stop=k == KD - 1)
                    last.then_inc(done, 1)
                for half in range(2):
                    for k in range(KD):
                        last = mm(C[:, half], hT[:, k], wv[:, k, 512 * half:512 * half + 512], start=k == 0, stop=k == KD - 1)
                last.then_inc(S["v_ready"], 1)

            def turn_keys(c):
                pe.wait_ge(S["k_out"], c + 1)
                for i in range(NH):
                    last = turn(bank(E, i), kT[:, i], mem.ident[:])
                last.then_inc(S["kt_ready"], 1)

            def scores(c):
                pe.wait_ge(S["q_out"], c + 1)
                for i in range(NH):
                    last = mm(bank(A, i), kT[:, i], qT[:, i], start=True, stop=True)
                last.then_inc(S["at_ready"], 1)

            def outputs(c):
                pe.wait_ge(S["at_out"], c + 1)
                pe.wait_ge(S["v_out"], c + 1)
                wait(pe, S["state_ready"], c)
                for i in range(NH):
                    mm(bank(B, i), at[:, i], v_[:, i], start=True, stop=False)
                    last = mm(bank(B, i), qT[:, i], state[:, i], start=False, stop=True)
                last.then_inc(S["o_ready"], 1)

            def keys_values(c):
                pe.wait_ge(S["kt_out"], c + 1)
                for i in range(NH):
                    last = mm(bank(A, i), kt[:, i], v_[:, i], start=True, stop=True)
                last.then_inc(S["kv_ready"], 1)

            def turn_output(c):
                pe.wait_ge(S["on_ready"], c + 1)
                for i in range(NH):
                    last = turn(bank(C, i), on[:, i], mem.ident[:])
                last.then_inc(S["onT_ready"], 1)

            def output_projection(c):
                pe.wait_ge(S["onT_copied"], c + 1)
                for i in range(NH):
                    last = mm(B[:, 0, 0:D], onT[:, i], wo[:, i], start=i == 0, stop=i == NH - 1)
                last.then_inc(S["wo_ready"], 1)

            def turn_net_input(c):
                pe.wait_ge(S["h2_ready"], c + 1)
                for k in range(KD):
                    last = turn(E[:, 1, P * k:P * k + P], h2[:, P * k:P * k + P], mem.ident[:])
                last.then_inc(S["h2T_ready"], 1)

            def net(c, w, X, done):
                for i in range(NH):
                    for k in range(KD):
                        last = mm(bank(X, i), w[:, k, P * i:P * i + P], h2T[:, k], start=k == 0, stop=k == KD - 1)
                last.then_inc(done, 1)

            def down(c):
                pe.wait_ge(S["gu_ready"], c + 1)
                for i in range(NH):
                    last = mm(A[:, 0, 0:D], guT[:, i], wd[:, i], start=i == 0, stop=i == NH - 1)
                last.then_inc(S["d_ready"], 1)

            pe.wait_ge(S["ready"], 12)
            start(0)
            project(0)
            turn_keys(0)
            scores(0)
            outputs(0)
            keys_values(0)
            turn_output(0)
            output_projection(0)
            start(1)

            def side_by_side(c, more):
                wait(pe, S["d_used"], c)
                project(c + 1)
                turn_keys(c + 1)
                scores(c + 1)
                pe.wait_ge(S["kt_out"], c + 2)
                turn_net_input(c)
                pe.wait_ge(S["h2T_copied"], c + 1)
                net(c, wg, C, S["g_ready"])
                outputs(c + 1)
                keys_values(c + 1)
                net(c, wu, E, S["u_ready"])
                pe.wait_ge(S["g_out"], c + 1)
                turn_output(c + 1)
                pe.wait_ge(S["kv_used"], c + 2)
                down(c)
                output_projection(c + 1)
                if more:
                    start(c + 2)

            rounds(pe, side_by_side)
            turn_net_input(TILES - 1)
            pe.wait_ge(S["h2T_copied"], TILES)
            net(TILES - 1, wg, C, S["g_ready"])
            net(TILES - 1, wu, E, S["u_ready"])
            pe.wait_ge(S["d_used"], TILES - 1)
            down(TILES - 1)


def experts(nc, io, mem, sem):
    ctx = ExitStack()
    with ctx:
        def sb(name, shape, dt=F32):
            return ctx.enter_context(nc.sbuf_tensor(name, shape, dt))

        def ps(name, shape):
            return ctx.enter_context(nc.psum_tensor(name, shape, F32))

        NE, HID = 8, 512
        KH = HID // P
        w1, w3, w2 = sb("e_w1", [P, NE, KD, HID]), sb("e_w3", [P, NE, KD, HID]), sb("e_w2", [P, NE, KH, D])
        b1, b3, b2 = sb("e_b1", [P, NE, KH]), sb("e_b3", [P, NE, KH]), sb("e_b2", [NE, D])
        wg, wf, bg, bf = sb("e_wg", [P, KD, NE]), sb("e_wf", [P, KD, D]), sb("e_bg", [P, NE]), sb("e_bf", [P, D])
        later = sb("later", [P, NE, NE])
        x, xT = sb("e_x", [P, GT, D]), sb("e_xT", [P, KD, 512])
        gate, top, total = sb("e_gate", [P, GT, NE]), sb("e_top", [P, GT]), sb("e_total", [P, GT])
        above, same, rank = sb("above", [P, GT, NE, NE]), sb("same", [P, GT, NE, NE]), sb("rank", [P, GT, NE])
        weight, weightT = sb("weight", [P, GT, NE]), sb("weightT", [NE, GT, P])
        h1, h3, hT = sb("e_h1", [P, 2, 512]), sb("e_h3", [P, 2, 512]), sb("e_hT", [P, KH, 512])
        mix, mixT, out = sb("e_mix", [P, GT, D]), sb("e_mixT", [P, KD, 512]), sb("e_out", [P, GT, D])
        work = Names()
        work.held = sem("e_held")
        work.stats, work.moments = sb("e_stats", [P, GT, 6]), sb("e_moments", [P, GT, 2])
        work.var, work.rstd = sb("e_var", [P, GT]), sb("e_rstd", [P, GT])
        turned, first, third, second = (ps(f"e_{n}", [P, 2, 512]) for n in ("turned", "first", "third", "second"))
        names = ("w_in x_ready xT_ready xT_copied logit_ready logit_out shifted exp_ready gates_ready gT_ready gT_copied "
                  "b_ready b_out h1_ready h3_ready h1_out h_out h_ready o_ready o_used mT_ready mT_copied "
                  "f_ready f_used var_ready rstd_ready done stored dve_s").split()
        S = {n: sem(f"e_{n}") for n in names}
        tiles_of = lambda bank: bank[:].rearrange("p a (c d) -> p (a c) d", d=D)
        block = ctx.enter_context(nc.Block())

        @block.sync
        def _(sp):
            loads = ((wg, io.wg), (bg, io.bg), (bf, io.bf), (later, io.later), (b1, io.b1), (b3, io.b3), (b2, io.b2),
                     (w1, io.w1), (w3, io.w3), (w2, io.w2), (wf, io.wf))
            for dst, src in loads:
                sp.dma_start(dst[:], src).then_inc(S["w_in"], 16)
            
            def group(g):
                sp.wait_ge(S["done"], g + 1)
                sp.dma_start(io.out[:, ds(GT * g, GT), :], out[:]).then_inc(S["stored"], 16)

            run_rounds(sp, group, GROUPS)
            sp.wait_ge(S["stored"], 16 * GROUPS)

        @block.gpsimd
        def _(pool):
            def group(g):
                pool.wait_ge(S["var_ready"], g + 1)
                nc.gpsimd.tensor_tensor(work.rstd[:], work.var[:], mem.minus_half[:, 0:GT], ALU.pow).then_inc(S["rstd_ready"], 1)

            run_rounds(pool, group, GROUPS)

        @block.scalar
        def _(act):
            a = nc.scalar.activation
            act.wait_ge(S["w_in"], 16 * 11)
            
            def group(g):
                wait(act, S["done"], g)
                a(x[:], mem.xs[:, ds(GT * g, GT), :], ACT.Copy).then_inc(S["x_ready"], 1)
                act.wait_ge(S["xT_ready"], g + 1)
                a(xT[:], turned[:], ACT.Copy).then_inc(S["xT_copied"], 1)
                act.wait_ge(S["shifted"], g + 1)
                a(gate[:], gate[:], ACT.Exp).then_inc(S["exp_ready"], 1)
                for e in range(NE):
                    for m in range(KH + 1):
                        n = KH * NE * g + KH * e + m
                        if m < KH:
                            act.wait_ge(S["h1_ready"], n + 1)
                            wait_from = n - 1 if e or m > 1 else KH * NE * g
                            wait(act, S["h_out"], wait_from)
                            a(h1[:, m % 2], first[:, m % 2], ACT.Identity, bias=b1[:, e, m:m + 1]).then_inc(S["h1_out"], 1)
                        if m:
                            wait(act, S["h_out"], n)
                            if m == 1:
                                wait(act, S["o_ready"], NE * g + e)
                            a(hT[:, m - 1], h3[:, (m - 1) % 2], ACT.Silu).then_inc(S["h_ready"], 1)
                    if e == 0:
                        act.wait_ge(S["gT_ready"], g + 1)
                        a(weightT[:], turned[0:NE, 0, :].rearrange("p (t q) -> p t q", q=P), ACT.Copy).then_inc(S["gT_copied"], 1)
                act.wait_ge(S["mT_ready"], g + 1)
                a(mixT[:], turned[:], ACT.Copy).then_inc(S["mT_copied"], 1)

            run_rounds(act, group, GROUPS)

        @block.vector
        def _(dve):
            v = nc.vector
            LINKS = 24
            dve.wait_ge(S["w_in"], 16 * 11)
            
            def group(g):
                ch = Chain(dve, S["dve_s"], LINKS * g)
                dve.wait_ge(S["logit_ready"], g + 1)
                v.tensor_tensor(gate[:], turned[:, 1, 0:GT * NE].rearrange("p (t e) -> p t e", e=NE),
                                bg[:, :].unsqueeze(1).to_broadcast([P, GT, NE]), ALU.add).then_inc(S["logit_out"], 1)
                dve.wait_ge(S["logit_out"], g + 1)
                ch.link(v.reduce_max(top[:], gate[:], AX.X))
                v.tensor_tensor(gate[:], gate[:], top[:, :].unsqueeze(2).to_broadcast([P, GT, NE]), ALU.subtract).then_inc(S["shifted"], 1)
                dve.wait_ge(S["exp_ready"], g + 1)
                ch.link(v.reduce_sum(total[:], gate[:], AX.X))
                ch.link(v.reciprocal(total[:], total[:]))
                ch.link(v.tensor_tensor(gate[:], gate[:], total[:, :].unsqueeze(2).to_broadcast([P, GT, NE]), ALU.mult))
                for t in range(GT):
                    other = gate[:, t, :].unsqueeze(1).to_broadcast([P, NE, NE])
                    own = gate[:, t, :].unsqueeze(2).to_broadcast([P, NE, NE])
                    ch.mark(v.tensor_tensor(above[:, t], other, own, ALU.is_gt))
                    last = ch.mark(v.tensor_tensor(same[:, t], other, own, ALU.is_equal))
                dve.wait_ge(ch.sem, last)
                ch.link(v.tensor_tensor(same[:], same[:], later[:, :, :].unsqueeze(1).to_broadcast([P, GT, NE, NE]), ALU.mult))
                ch.link(v.tensor_tensor(above[:], above[:], same[:], ALU.add))
                ch.link(v.reduce_sum(rank[:], above[:], AX.X))
                v.scalar_tensor_tensor(weight[:], rank[:], 1.5, gate[:], ALU.is_lt, ALU.mult).then_inc(S["gates_ready"], 1)
                def product(e, m):
                    n = KH * NE * g + KH * e + m
                    dve.wait_ge(S["h3_ready"], n + 1)
                    dve.wait_ge(S["h1_out"], n + 1)
                    wait(dve, S["h_ready"], n - 1 if e or m > 1 else KH * NE * g)
                    v.scalar_tensor_tensor(h3[:, m % 2], third[:, m % 2], b3[:, e, m:m + 1], h1[:, m % 2],
                                           ALU.add, ALU.mult).then_inc(S["h_out"], 1)

                def add_expert(e):
                    dve.wait_ge(S["o_ready"], NE * g + e + 1)
                    for t in range(GT):
                        last = v.scalar_tensor_tensor(mix[:, t], tiles_of(second)[:, t], weight[:, t, e:e + 1], mix[:, t],
                                                      ALU.mult, ALU.add)
                    last.then_inc(S["o_used"], 1)
                    dve.wait_ge(S["o_used"], NE * g + e + 1)

                for e in range(NE):
                    for m in range(KH):
                        product(e, m)
                    if e == 0:
                        dve.wait_ge(S["b_ready"], g + 1)
                        v.tensor_copy(mix[:], tiles_of(second)).then_inc(S["b_out"], 1)
                        dve.wait_ge(S["b_out"], g + 1)
                    else:
                        add_expert(e - 1)
                add_expert(NE - 1)
                dve.wait_ge(S["f_ready"], g + 1)
                wait(dve, S["stored"], 16 * g)
                v.tensor_tensor(out[:], tiles_of(first), bf[:, :].unsqueeze(1).to_broadcast([P, GT, D]), ALU.add).then_inc(S["f_used"], 1)
                dve.wait_ge(S["f_used"], g + 1)
                ch.link(v.tensor_tensor(out[:], out[:], x[:], ALU.add))
                normalise_rows(dve, v, ch, work, out, out, 1e-5, S["var_ready"], S["rstd_ready"], g + 1).then_inc(S["done"], 1)
                assert ch.n == LINKS, ch.n

            run_rounds(dve, group, GROUPS)

        @block.tensor
        def _(pe):
            mm, turn = nc.tensor.matmul, nc.tensor.transpose
            pe.wait_ge(S["w_in"], 16 * 11)
            
            def group(g):
                pe.wait_ge(S["x_ready"], g + 1)
                wait(pe, S["mT_copied"], g)
                for t in range(GT):
                    for k in range(KD):
                        last = turn(turned[:, k, P * t:P * t + P], x[:, t, P * k:P * k + P], mem.ident[:])
                last.then_inc(S["xT_ready"], 1)
                pe.wait_ge(S["xT_copied"], g + 1)
                for t in range(GT):
                    for k in range(KD):
                        last = mm(turned[:, 1, NE * t:NE * t + NE], xT[:, k, P * t:P * t + P], wg[:, k], start=k == 0, stop=k == KD - 1)
                last.then_inc(S["logit_ready"], 1)
                wait(pe, S["f_used"], g)

                def up(e):
                    for m in range(KH):
                        n = KH * NE * g + KH * e + m
                        for w, bank, free, done in ((w1, first, S["h1_out"], S["h1_ready"]), (w3, third, S["h_out"], S["h3_ready"])):
                            wait(pe, free, n - 1 if e or m > 1 else KH * NE * g)
                            for k in range(KD):
                                last = mm(bank[:, m % 2], w[:, e, k, P * m:P * m + P], xT[:, k], start=k == 0, stop=k == KD - 1)
                            last.then_inc(done, 1)

                def down(e):
                    pe.wait_ge(S["h_ready"], KH * NE * g + KH * e + KH)
                    if e:
                        pe.wait_ge(S["o_used"], NE * g + e)
                    for t in range(GT):
                        for k in range(KH):
                            last = mm(tiles_of(second)[:, t], hT[:, k, P * t:P * t + P], w2[:, e, k], start=k == 0, stop=k == KH - 1)
                    last.then_inc(S["o_ready"], 1)

                up(0)
                pe.wait_ge(S["gates_ready"], g + 1)
                for t in range(GT):
                    last = turn(turned[0:NE, 0, P * t:P * t + P], weight[:, t], mem.ident[:])
                last.then_inc(S["gT_ready"], 1)
                pe.wait_ge(S["gT_copied"], g + 1)
                for t in range(GT):
                    last = mm(tiles_of(second)[:, t], weightT[:, t], b2[:], start=True, stop=True)
                last.then_inc(S["b_ready"], 1)
                pe.wait_ge(S["b_out"], g + 1)
                down(0)
                for e in range(1, NE):
                    up(e)
                    down(e)
                pe.wait_ge(S["o_used"], NE * g + NE)
                for t in range(GT):
                    for k in range(KD):
                        last = turn(turned[:, k, P * t:P * t + P], mix[:, t, P * k:P * k + P], mem.ident[:])
                last.then_inc(S["mT_ready"], 1)
                pe.wait_ge(S["mT_copied"], g + 1)
                for t in range(GT):
                    for k in range(KD):
                        last = mm(tiles_of(first)[:, t], mixT[:, k, P * t:P * t + P], wf[:, k], start=k == 0, stop=k == KD - 1)
                last.then_inc(S["f_ready"], 1)

            run_rounds(pe, group, GROUPS)


def build(nc, a, out, upto=9):
    ctx = ExitStack()
    with ctx:
        sem = lambda name: ctx.enter_context(nc.semaphore(name))
        io, mem = Names(), Names()
        io.x = a["L0_attn_x"].rearrange("b s d -> (b s) d")
        io.wq, io.wk, io.wv, io.wo = (a[f"L0_attn_W{n}"].rearrange("(k p) n -> p k n", p=P) for n in "qkvo")
        io.bq, io.bk = (a[f"L0_attn_b{n}"] for n in "qk")
        io.bv = a["L0_attn_bv"].partition_broadcast(P)
        io.rby = a["L0_attn_rby"].partition_broadcast(P)
        io.pos, io.powers, io.ident, io.delta = (a[n] for n in ("pos", "powers", "ident", "delta"))
        io.powers = io.powers.partition_broadcast(P)
        io.q_parts = nc.dram_tensor("q_parts", (PARTS, BATCH, D, SEQ), BF16, kind="Internal").ap()
        io.k_parts = nc.dram_tensor("k_parts", (PARTS, BATCH, D, SEQ), BF16, kind="Internal").ap()

        io.bo, io.gamma, io.beta = (a[n].partition_broadcast(P) for n in ("L0_attn_bo", "L0_attn_ln_gamma", "L0_attn_ln_beta"))
        io.wfc = a["L0_ffn_W_fc"].rearrange("(k p) n -> p k n", p=P)
        io.wproj = a["L0_ffn_W_proj"].rearrange("(k p) n -> p k n", p=P)

        io.norm_in, io.norm_out, io.norm_mlp = (a[f"L1_attn_{n}"] for n in ("attn_norm_w", "attn_out_norm_w", "mlp_norm_w"))
        io.l1q, io.l1k, io.l1v, io.l1o, io.l1g, io.l1u, io.l1d = (
            a[f"L1_attn_W{n}"].rearrange("(k p) n -> p k n", p=P) for n in ("q", "k", "v", "o", "gate", "up", "down"))
        io.causal, io.keep = a["causal"], a["keep"].partition_broadcast(P)

        io.w1, io.w3, io.w2 = (a[f"L1_ffn_W{n}"].rearrange("e (k p) n -> p e k n", p=P) for n in "132")
        io.b1, io.b3, io.b2 = a["L1_ffn_b1"], a["L1_ffn_b3"], a["L1_ffn_b2"]
        io.wg, io.wf = (a[f"L1_ffn_W{n}"].rearrange("(k p) n -> p k n", p=P) for n in "gf")
        io.bg, io.bf = (a[f"L1_ffn_b{n}"].partition_broadcast(P) for n in "gf")
        io.later = a["later"]
        io.out = out.rearrange("b s d -> (b s) d").rearrange("(t p) d -> p t d", p=P)

        def sb(c, name, shape, dt=F32):
            return c.enter_context(nc.sbuf_tensor(name, shape, dt))

        mem.xs = sb(ctx, "xs", [P, TILES, D])
        mem.ident = sb(ctx, "ident", [P, P])
        mem.minus_half = sb(ctx, "minus_half", [P, 8])
        mem.rby = sb(ctx, "rby", [P, 3])
        mem.logit_scale, mem.out_scale = sb(ctx, "logit_scale", [P, 1]), sb(ctx, "out_scale", [P, 1])
        first = ctx.enter_context(ExitStack())
        mem.enc = sb(first, "enc", [P, TPB, D])
        mem.attn = sb(first, "attn", [P, PAIRS, TPB, DK])
        heads = first.enter_context(ExitStack())
        mem.delta = sb(heads, "delta", [SHIFT, SEQ], BF16)
        mem.values = sb(heads, "values", [P, PAIRS, TPB, VW])
        mem.vstage = sb(heads, "vstage", [P, 2, TPB, 32])
        mem.qst = sb(heads, "qst", [P, 4, SEQ], BF16)
        mem.kst = sb(heads, "kst", [P, 4, SEQ], BF16)
        embed_and_project(nc, io, mem, sem)
        if upto < 2: return
        attend(nc, io, mem, sem)
        heads.close()
        if upto < 3: return
        mix_and_spike(nc, io, mem, sem)
        first.close()
        if upto < 4: return
        linear_attention_and_gate(nc, io, mem, sem)
        if upto < 5: return
        experts(nc, io, mem, sem)


def layout(inputs):
    a = {n: np.ascontiguousarray(v) for n, v in inputs.items()}
    for n in ("L0_attn_Wq", "L0_attn_Wk", "L0_attn_Wv", "L0_attn_Wo", "L0_ffn_W_fc", "L0_ffn_W_proj"):
        a[n] = np.ascontiguousarray(a[n].T)
    for n in ("L0_attn_bq", "L0_attn_bk", "L1_attn_attn_norm_w", "L1_attn_attn_out_norm_w", "L1_attn_mlp_norm_w"):
        a[n] = np.ascontiguousarray(a[n].reshape(-1, P).T)
    a["pos"] = (np.arange(TPB)[None, :] * P + np.arange(P)[:, None]).astype(np.float32)
    a["powers"] = np.power(np.float32(10000.0), np.float32(2.0) * np.arange(0, D, 2, dtype=np.float32) / np.float32(D)).astype(np.float32)
    for n in ("L1_ffn_b1", "L1_ffn_b3"):
        a[n] = np.ascontiguousarray(a[n].reshape(len(a[n]), -1, P).transpose(2, 0, 1))
    a["later"] = np.ascontiguousarray(np.broadcast_to(np.triu(np.ones((8, 8), np.float32), 1), (P, 8, 8)))
    a["causal"] = np.triu(np.ones((P, P), np.float32))
    a["keep"] = (np.arange(TILES + 1) % TPB != 0).astype(np.float32)
    a["ident"] = np.eye(P, dtype=np.float32)
    a["delta"] = np.repeat(np.eye(SHIFT), P, axis=1).astype(mybir.dt.np(BF16))
    return {f"in_{n}": v for n, v in a.items()}


def kernel(**inputs):
    import concourse.bacc as bacc
    from concourse.bass_utils import run_bass_kernel_spmd

    nc = bacc.Bacc("TRN2", target_bir_lowering=False, num_devices=1)
    arrays = layout(inputs)
    a = {n[len("in_"):]: nc.dram_tensor(n, v.shape, mybir.dt.from_np(v.dtype), kind="ExternalInput").ap()
         for n, v in arrays.items()}
    out = nc.dram_tensor("out", (BATCH, SEQ, D), F32, kind="ExternalOutput").ap()
    build(nc, a, out)
    return run_bass_kernel_spmd(nc, [arrays], core_ids=[0]).results[0]["out"]
```

```python
import math
from contextlib import ExitStack

import numpy as np

import concourse.bass as bass
from concourse import mybir

F32 = mybir.dt.float32
BF16 = mybir.dt.bfloat16
ALU = mybir.AluOpType
ACT = mybir.ActivationFunctionType
AX = mybir.AxisListType
ds = bass.ds

P = 128
BATCH, SEQ, D = 2, 2048, 256
TILES = BATCH * SEQ // P
TPB = SEQ // P
KD = D // P
HEADS, DK = 16, 16
PAIRS = BATCH * HEADS
VW = DK + 1
PARTS = 3
STACK = 6 * DK
SHIFT = TPB
QB = SEQ // 512
GT = 4
GROUPS = TILES // GT


class Names:
    pass


class Chain:

    def __init__(self, eng, sem, base=0):
        self.eng, self.sem, self.base, self.n = eng, sem, base, 0

    def mark(self, ins):
        ins.then_inc(self.sem, 1)
        self.n += 1
        return self.base + self.n

    def link(self, ins):
        self.eng.wait_ge(self.sem, self.mark(ins))


def wait(eng, sem, value):
    if not isinstance(value, int) or value > 0:
        eng.wait_ge(sem, value)


def hold(eng, sem, value, held):
    eng.wait_ge(sem, value)
    eng.sem_inc(held, 1)


def run_rounds(eng, body, rounds):
    body(0)
    with eng.Fori(1, rounds) as r:
        body(r)


def part_views(ap):
    return ap.rearrange("(t p) d -> p t d", p=P)


def embed_and_project(nc, io, mem, sem):
    ctx = ExitStack()
    with ctx:
        def sb(name, shape, dt=F32):
            return ctx.enter_context(nc.sbuf_tensor(name, shape, dt))

        def ps(name, shape):
            return ctx.enter_context(nc.psum_tensor(name, shape, F32))

        wq, wk, wv = (sb(n, [P, KD, D]) for n in ("wq", "wk", "wv"))
        bq, bk = sb("bq", [P, KD]), sb("bk", [P, KD])
        bqc = sb("bqc", [P, KD])
        bv = sb("bv", [P, D])
        pos, powers = sb("pos", [P, TPB]), sb("powers", [P, P])
        denom = sb("denom", [P, P])
        spare = mem.attn[:, :, :, :].rearrange("p s t d -> p (s t d)")
        angle, turns, reduced = (spare[:, SEQ * i:SEQ * i + SEQ].rearrange("p (t f) -> p t f", f=P) for i in range(3))
        scal = sb("scal", [P, 8])
        x0 = mem.qst[:, 0:2, :].rearrange("p a t -> p (a t)").bitcast(F32).rearrange("p (j t d) -> p j t d", j=2, d=D)
        x0T = sb("x0T", [P, 2, KD, 512])
        qkf = sb("qkf", [P, 2, KD, 512])
        parts = sb("parts", [P, 2, 2, PARTS, KD, 512], BF16)
        pT, pQ, pK, pV = (ps(n, [P, KD, 512]) for n in ("pT", "pQ", "pK", "pV"))
        x_in, c_in = sem("a_x_in"), sem("a_c_in")
        dve_s, act_s = sem("a_dve"), sem("a_act")
        square_ready, root_ready = sem("a_square"), sem("a_root")
        angles_ready, enc_ready = sem("a_angles"), sem("a_enc")
        x0_ready, x0_used = sem("a_x0"), sem("a_x0_used")
        xT_ready, xT_copied = sem("a_xT"), sem("a_xT_copied")
        q_ready, k_ready, v_ready = sem("a_q"), sem("a_k"), sem("a_v")
        q_out, k_out, v_out = sem("a_q_out"), sem("a_k_out"), sem("a_v_out")
        p1, r1, p2, p3 = (sem(f"a_{n}") for n in ("p1", "r1", "p2", "p3"))
        stored = [sem(f"a_stored{j}") for j in range(2)]
        ready0 = sem("a_ready0")
        enc_v = mem.enc[:, :, :].rearrange("p t (f two) -> p t f two", two=2)
        CONSTS = 13
        N_DVE0 = 24

        block = ctx.enter_context(nc.Block())

        @block.sync
        def _(sp):
            for dst, src in ((pos, io.pos), (powers, io.powers), (mem.rby, io.rby),
                             (mem.ident, io.ident), (wq, io.wq), (wk, io.wk), (wv, io.wv),
                             (bv, io.bv), (bq, io.bq), (bk, io.bk), (mem.delta, io.delta)):
                sp.dma_start(dst[:], src).then_inc(c_in, 16)
            sp.dma_start(mem.xs[:, 0:TPB, :], part_views(io.x)[:, 0:TPB, :]).then_inc(x_in, 16)
            sp.dma_start(mem.xs[:, TPB:, :], part_views(io.x)[:, TPB:, :]).then_inc(x_in, 16)

            def store(pair):
                for g in range(2):
                    b, slot = pair // 2, (2 * pair + g) % GT
                    sp.wait_ge(p3, 4 * pair + 2 * g + 2)
                    for w, scratch in ((0, io.q_parts), (1, io.k_parts)):
                        for s in range(PARTS):
                            dst = scratch[s, ds(b, 1), :, ds(512 * slot, 512)]
                            sp.dma_start(dst.rearrange("o (m p) t -> p (o m) t", p=P),
                                         parts[:, g, w, s, :, :]).then_inc(stored[g], 16)

            run_rounds(sp, store, GROUPS // 2)
            for j in range(2):
                sp.wait_ge(stored[j], 4 * 96)

        @block.gpsimd
        def _(pool):
            nc.gpsimd.memset(mem.minus_half[:], -0.5).then_inc(ready0, 1)
            pool.wait_ge(ready0, 1)
            pool.wait_ge(square_ready, 1)
            nc.gpsimd.tensor_tensor(scal[:, 5:6], scal[:, 7:8], mem.minus_half[:, 0:1], ALU.pow).then_inc(root_ready, 1)
            nc.gpsimd.memset(mem.values[:, :, :, DK:VW], 1.0).then_inc(ready0, 1)
            nc.gpsimd.memset(mem.vstage[:], 0.0).then_inc(ready0, 1)
            pool.wait_ge(ready0, 3)
            nc.gpsimd.memset(mem.kst[STACK:STACK + SHIFT, :, :], 1.0).then_inc(ready0, 1)
            pool.wait_ge(ready0, 4)

        @block.scalar
        def _(act):
            act.wait_ge(angles_ready, 1)
            nc.scalar.activation(enc_v[:, :, :, 0], reduced, ACT.Sin).then_inc(enc_ready, 1)
            act.wait_ge(angles_ready, 2)
            nc.scalar.activation(enc_v[:, :, :, 1], turns, ACT.Sin).then_inc(enc_ready, 1)

            def pair_of_groups(pair):
                for g in range(2):
                    n = 2 * pair + g + 1
                    act.wait_ge(xT_ready, n)
                    nc.scalar.activation(x0T[:, g % 2], pT[:], ACT.Copy).then_inc(xT_copied, 1)
                    wait(act, p3, 2 * n - 2)
                    act.wait_ge(q_ready, n)
                    for m in range(KD):
                        last = nc.scalar.activation(qkf[:, 0, m], pQ[:, m], ACT.Identity,
                                                    bias=bqc[:, m:m + 1], scale=mem.logit_scale[:, 0:1])
                    last.then_inc(q_out, 1)
                    act.wait_ge(k_ready, n)
                    for m in range(KD):
                        last = nc.scalar.activation(qkf[:, 1, m], pK[:, m], ACT.Identity,
                                                    bias=bk[:, m:m + 1])
                    last.then_inc(k_out, 1)
                    wait(act, stored[g], 96 * pair)
                    for w, done in ((0, q_out), (1, k_out)):
                        act.wait_ge(done, n)
                        nc.scalar.activation(parts[:, g % 2, w, 0], qkf[:, w], ACT.Copy).then_inc(p1, 1)
                    for w in range(2):
                        act.wait_ge(r1, 2 * n - 1 + w)
                        nc.scalar.activation(parts[:, g % 2, w, 1], qkf[:, w], ACT.Copy).then_inc(p2, 1)

            run_rounds(act, pair_of_groups, GROUPS // 2)

        @block.vector
        def _(dve):
            ch = Chain(dve, dve_s)
            dve.wait_ge(c_in, 11 * 16)
            red, blue, yellow = (mem.rby[:, i:i + 1] for i in range(3))
            v = nc.vector
            ch.link(v.tensor_scalar(scal[:, 0:1], yellow, 0.1 * math.sin(0.5 * math.pi), 1.0, ALU.mult, ALU.add))
            ch.link(v.tensor_scalar(denom[:], powers[:], scal[:, 0:1], None, ALU.mult))
            ch.link(v.reciprocal(denom[:], denom[:]))
            ch.link(v.tensor_tensor(angle, pos[:, :].unsqueeze(2).to_broadcast([P, TPB, P]),
                                    denom[:, :].unsqueeze(1).to_broadcast([P, TPB, P]), ALU.mult))
            two_pi = 2 * math.pi
            c1 = float(np.float32(6.28125))
            c2 = float(np.float32(two_pi - c1))
            c2 = math.floor(c2 * 2 ** 21) / 2 ** 21
            c3 = two_pi - c1 - c2
            magic = 1.5 * 2 ** 23
            for quarter, dst in ((0, reduced), (1, turns)):
                if quarter:
                    dve.wait_ge(enc_ready, 1)
                whole = turns if not quarter else reduced
                ch.link(v.tensor_scalar(whole, angle, 1 / two_pi, 0.25 * quarter, ALU.mult, ALU.add))
                ch.link(v.tensor_scalar(whole, whole, magic, magic, ALU.add, ALU.subtract))
                ch.link(v.scalar_tensor_tensor(dst, whole, -c1, angle, ALU.mult, ALU.add))
                ch.link(v.scalar_tensor_tensor(dst, whole, -c2, dst, ALU.mult, ALU.add))
                ch.link(v.scalar_tensor_tensor(dst, whole, -c3, dst, ALU.mult, ALU.add))
                if quarter:
                    ch.link(v.tensor_scalar(dst, dst, math.pi / 2, None, ALU.add))
                v.tensor_scalar(dst, dst, 3.1415925, -3.1415925, ALU.min, ALU.max).then_inc(angles_ready, 1)
            ch.link(v.tensor_scalar(scal[:, 1:2], red, 0.1, 1.0, ALU.mult, ALU.add))
            ch.link(v.scalar_tensor_tensor(scal[:, 2:3], blue, 0.05, scal[:, 1:2], ALU.mult, ALU.add))
            ch.link(v.scalar_tensor_tensor(scal[:, 3:4], yellow, 0.15, scal[:, 2:3], ALU.mult, ALU.add))
            ch.link(v.tensor_scalar(scal[:, 4:5], red, 0.0, 1.0, ALU.mult, ALU.add))
            v.tensor_scalar(scal[:, 7:8], scal[:, 4:5], float(DK), None, ALU.mult).then_inc(square_ready, 1)
            dve.wait_ge(root_ready, 1)
            ch.link(v.tensor_tensor(mem.logit_scale[:, 0:1], scal[:, 3:4], scal[:, 5:6], ALU.mult))
            ch.link(v.tensor_scalar(bqc[:], bq[:], mem.logit_scale[:, 0:1], None, ALU.mult))
            ch.link(v.tensor_scalar(mem.out_scale[:, 0:1], yellow, 0.1 * math.sin(math.pi), 1.0, ALU.mult, ALU.add))
            dve.wait_ge(x_in, 32)
            dve.wait_ge(enc_ready, 2)

            def pair_of_groups(pair):
                for g in range(2):
                    n = 2 * pair + g + 1
                    b, slot = pair // 2, (2 * pair + g) % GT
                    wait(dve, xT_ready, n - 2)
                    v.tensor_tensor(x0[:, g % 2], mem.xs[:, ds(GT * (2 * pair + g), GT), :],
                                    mem.enc[:, ds(GT * slot, GT), :], ALU.add).then_inc(x0_ready, 1)
                    dve.wait_ge(v_ready, n)
                    v.tensor_tensor(
                        mem.values[:, ds(HEADS * b, HEADS), ds(GT * slot, GT), 0:DK].rearrange("p h t d -> p t h d"),
                        pV[:].rearrange("p a (c h d) -> p (a c) h d", c=2, d=DK),
                        bv[:, :].rearrange("p (h d) -> p h d", d=DK).unsqueeze(1).to_broadcast([P, GT, HEADS, DK]),
                        ALU.add).then_inc(v_out, 1)
                    for w in range(2):
                        dve.wait_ge(p1, 2 * n - 1 + w)
                        v.tensor_tensor(qkf[:, w], qkf[:, w], parts[:, g % 2, w, 0], ALU.subtract).then_inc(r1, 1)
                    for w in range(2):
                        dve.wait_ge(p2, 2 * n - 1 + w)
                        v.tensor_tensor(parts[:, g % 2, w, 2], qkf[:, w], parts[:, g % 2, w, 1],
                                        ALU.subtract).then_inc(p3, 1)

            run_rounds(dve, pair_of_groups, GROUPS // 2)

        @block.tensor
        def _(pe):

            def pair_of_groups(pair):
                for g in range(2):
                    n = 2 * pair + g + 1
                    pe.wait_ge(x0_ready, n)
                    wait(pe, xT_copied, n - 1)
                    for t in range(GT):
                        for k in range(KD):
                            last = nc.tensor.transpose(pT[:, k, P * t:P * t + P],
                                                       x0[:, g % 2, t, P * k:P * k + P], mem.ident[:])
                    last.then_inc(xT_ready, 1)
                    pe.wait_ge(xT_copied, n)
                    for w, acc, done, free in ((wq, pQ, q_ready, q_out), (wk, pK, k_ready, k_out)):
                        wait(pe, free, n - 1)
                        for m in range(KD):
                            for k in range(KD):
                                last = nc.tensor.matmul(acc[:, m], w[:, k, P * m:P * m + P], x0T[:, g % 2, k],
                                                        start=k == 0, stop=k == KD - 1)
                        last.then_inc(done, 1)
                    wait(pe, v_out, n - 1)
                    for t in range(GT):
                        for k in range(KD):
                            last = nc.tensor.matmul(pV[:, t // 2, D * (t % 2):D * (t % 2) + D],
                                                    x0T[:, g % 2, k, P * t:P * t + P], wv[:, k],
                                                    start=k == 0, stop=k == KD - 1)
                    last.then_inc(v_ready, 1)

            run_rounds(pe, pair_of_groups, GROUPS // 2)


Q_PARTS, K_PARTS = (0, 0, 0, 1, 1, 2), (0, 1, 2, 0, 1, 0)


def attend(nc, io, mem, sem):
    ctx = ExitStack()
    with ctx:
        def sb(name, shape, dt=F32):
            return ctx.enter_context(nc.sbuf_tensor(name, shape, dt))

        def ps(name, shape):
            return ctx.enter_context(nc.psum_tensor(name, shape, F32))

        RING = 4
        AHEAD = 4
        qst, kst = mem.qst, mem.kst
        probs = sb("probs", [P, RING, SEQ])
        top = sb("top", [P, 2, TPB, QB])
        most = sb("most", [P, TPB])
        mostT = sb("mostT", [SHIFT, P], BF16)
        oT = sb("oT", [P, 512])
        recip = sb("recip", [P, QB, QB])
        scoresT, outT = ps("scoresT", [P, 2, 1024]), ps("outT", [P, 512])
        scores = ps("scores", [P, 3, 512])
        loaded = [sem(f"b_loaded{j}") for j in range(RING)]
        m_ready, m_used = sem("b_m_ready"), sem("b_m_used")
        e_ready, p_ready, pv_done = sem("b_e_ready"), sem("b_p_ready"), sem("b_pv_done")
        v_staged = sem("b_v_staged")
        most_ready, mostT_ready, mostT_cast, shift_ready = (sem(f"b_{x}") for x in ("most", "mostT", "mostT_cast", "shift"))
        o_copied, oT_ready, o_done = sem("b_o_copied"), sem("b_oT"), sem("b_o_done")
        dve_s = sem("b_dve")
        bo, zeros = sb("bo", [P, D]), sb("zeros", [P, D])
        bo_in, zeros_ready, cleared, enc_ready = sem("b_bo_in"), sem("b_zeros"), sem("b_cleared"), sem("b_enc")
        ROUNDS = PAIRS // RING
        LOADS = 16 * (len(Q_PARTS) + len(K_PARTS))

        def rounds(eng, body):
            body(0)
            with eng.Fori(1, ROUNDS - 1) as r:
                body(r)
            body(ROUNDS - 1)

        def ahead(kt):
            return 1 + (kt + AHEAD) // TPB, (kt + AHEAD) % TPB

        TURN_OUT, TURN_MOST = 2, TPB - AHEAD
        OUT_USE, MOST_USE = QB * (TURN_OUT + 1), QB * (TURN_MOST + 1) + 1
        block_use = lambda kt, quarter: QB * kt + quarter + (kt > TURN_OUT) + (kt > TURN_MOST)
        FIRST_MOST_USE = QB * TPB
        first_use = lambda t, quarter: QB * t + quarter
        second_use = lambda t, quarter: FIRST_MOST_USE + 1 + QB * t + quarter
        bank = lambda use: scores[:, use % 3]

        def is_last(r, j, of=PAIRS - 1):
            return isinstance(r, int) and RING * r + j >= of

        block = ctx.enter_context(nc.Block())

        @block.sync
        def _(sp):
            def load(s, j):
                for stack, scratch, order in ((qst, io.q_parts, Q_PARTS), (kst, io.k_parts, K_PARTS)):
                    rows = scratch.rearrange("s b f t -> s (b f) t")
                    for i, part in enumerate(order):
                        sp.dma_start(stack[DK * i:DK * i + DK, j, :], rows[part, ds(DK * s, DK), :]).then_inc(loaded[j], 16)

            for j in range(RING):
                load(j, j)
            sp.dma_start(bo[:], io.bo).then_inc(bo_in, 16)
            sp.wait_ge(zeros_ready, 1)
            sp.dma_start(io.sorted_x.rearrange("(t p) d -> p t d", p=P),
                         zeros[:, :].unsqueeze(1).to_broadcast([P, MAX_TILES, D])).then_inc(cleared, 16)

            def body(r):
                for j in range(RING):
                    if not is_last(r, j, PAIRS - RING):
                        sp.wait_ge(e_ready, 2 * TPB * (RING * r + j + 1))
                        load(RING * r + j + RING, j)

            rounds(sp, body)
            sp.wait_ge(cleared, 16)

        @block.gpsimd
        def _(pool):
            def shift(s, j):
                pool.wait_ge(mostT_cast, s + 1)
                pool.wait_ge(v_staged, s + 1)
                nc.gpsimd.tensor_tensor(
                    qst[STACK:STACK + SHIFT, j, :].rearrange("p (t q) -> p t q", q=P),
                    mostT[:, :].unsqueeze(1).to_broadcast([SHIFT, TPB, P]),
                    mem.delta[:, :].rearrange("p (t q) -> p t q", q=P), ALU.mult).then_inc(shift_ready, 1)

            def stage(s, j):
                wait(pool, shift_ready, s)
                nc.gpsimd.tensor_copy(mem.vstage[:, j % 2, :, 0:VW],
                                      mem.values[:, ds(s, 1), :, :].rearrange("p o t d -> p (o t) d")).then_inc(v_staged, 1)

            stage(0, 0)
            shift(0, 0)
            pool.wait_ge(shift_ready, 1)
            nc.gpsimd.memset(zeros[:], 0.0).then_inc(zeros_ready, 1)
            pool.wait_ge(bo_in, 16)
            pool.wait_ge(zeros_ready, 1)
            nc.gpsimd.tensor_tensor(mem.enc[:], mem.enc[:], bo[:, :].unsqueeze(1).to_broadcast([P, TPB, D]), ALU.add).then_inc(enc_ready, 1)
            pool.wait_ge(enc_ready, 1)

            def body(r):
                for j in range(RING):
                    if not is_last(r, j):
                        s = RING * r + j
                        wait(pool, pv_done, TPB * s)
                        stage(s + 1, j + 1)
                        shift(s + 1, (j + 1) % RING)

            rounds(pool, body)

        @block.scalar
        def _(act):
            def cast_most(s, use=MOST_USE):
                act.wait_ge(mostT_ready, s + 1)
                wait(act, shift_ready, s)
                nc.scalar.activation(mostT[:], bank(use)[0:SHIFT, 0:P], ACT.Copy, scale=-1.0).then_inc(mostT_cast, 1)

            def take_out(s):
                act.wait_ge(pv_done, TPB * (s + 1))
                wait(act, oT_ready, s)
                nc.scalar.activation(oT[:], outT[:], ACT.Copy).then_inc(o_copied, 1)

            cast_most(0, FIRST_MOST_USE)

            def body(r):
                for j in range(RING):
                    s = RING * r + j
                    for kt in range(TPB):
                        if kt == 1 and not (isinstance(r, int) and r == 0 and j == 0):
                            take_out(s - 1)
                        if kt == 13 and not is_last(r, j):
                            cast_most(s + 1)
                        wait(act, pv_done, TPB * s + kt - RING + 1)
                        for half in range(2):
                            act.wait_ge(e_ready, 2 * TPB * s + 2 * kt + half + 1)
                            nc.scalar.activation(probs[:, kt % RING, 1024 * half:1024 * half + 1024],
                                                 scoresT[:, half], ACT.Exp).then_inc(p_ready, 1)

            rounds(act, body)
            take_out(PAIRS - 1)

        @block.vector
        def _(dve):
            v = nc.vector
            ch = [0]

            def block_max(s, par, t, use):
                if t == 0:
                    wait(dve, most_ready, s - 1)
                for quarter in range(QB):
                    dve.wait_ge(m_ready, 4 * TPB * s + QB * t + quarter + 1)
                    v.reduce_max(top[:, par, t, quarter:quarter + 1], bank(use + quarter), AX.X).then_inc(m_used, 1)

            def pair_max(s, par):
                dve.wait_ge(m_used, 4 * TPB * (s + 1))
                wait(dve, mostT_ready, s)
                v.reduce_max(most[:], top[:, par], AX.X).then_inc(most_ready, 1)

            def normalise(s):
                dve.wait_ge(oT_ready, s + 1)
                out = bank(OUT_USE).rearrange("p (c j d) -> p c j d", j=QB, d=32)
                wait(dve, o_done, s)
                v.reciprocal(recip[:], out[:, :, :, DK]).then_inc(dve_s, 1)
                dve.wait_ge(dve_s, 2 * s + 1)
                v.tensor_scalar(recip[:], recip[:], mem.out_scale[:, 0:1], None, ALU.mult).then_inc(dve_s, 1)
                dve.wait_ge(dve_s, 2 * s + 2)
                v.tensor_tensor(mem.attn[:, ds(s, 1), :, :].rearrange("p o (j c) d -> p c (o j) d", c=QB),
                                out[:, :, :, 0:DK], recip[:, :, :].unsqueeze(3).to_broadcast([P, QB, QB, DK]),
                                ALU.mult).then_inc(o_done, 1)

            for t in range(TPB):
                block_max(0, 0, t, first_use(t, 0))
            pair_max(0, 0)
            for t in range(AHEAD):
                block_max(1, 1, t, second_use(t, 0))

            def body(r):
                for j in range(RING):
                    s = RING * r + j
                    for kt in range(TPB):
                        more, t = ahead(kt)
                        if kt == 3 and not (isinstance(r, int) and r == 0 and j == 0):
                            normalise(s - 1)
                        if kt == TPB - AHEAD and not is_last(r, j):
                            pair_max(s + 1, (j + 1) % 2)
                        if not is_last(r, j + more - 1):
                            block_max(s + more, (j + more) % 2, t, block_use(kt, 0))

            rounds(dve, body)
            normalise(PAIRS - 1)

        @block.tensor
        def _(pe):
            def free_bank(use, blocks, turned):
                if use - 3 in turned:
                    wait(pe, *turned[use - 3])
                elif use - 1 in turned or use - 2 in turned:
                    wait(pe, m_used, blocks - 1)
                else:
                    wait(pe, m_used, blocks - 2)

            def query_scores(s, r, j, t, quarter, use, turned):
                if t == 0 and quarter == 0:
                    pe.wait_ge(loaded[j % RING], LOADS * (r + j // RING + 1))
                free_bank(use, QB * (TPB * s + t) + quarter, turned)
                nc.tensor.matmul(bank(use), qst[0:STACK, j % RING, P * t:P * t + P],
                                 kst[0:STACK, j % RING, 512 * quarter:512 * quarter + 512],
                                 start=True, stop=True).then_inc(m_ready, 1)

            def key_scores(s, j, kt, half):
                if kt == 0 and half == 0:
                    pe.wait_ge(shift_ready, s + 1)
                wait(pe, p_ready, 2 * TPB * s + 2 * kt + half - 1)
                for q in range(2):
                    last = nc.tensor.matmul(scoresT[:, half, 512 * q:512 * q + 512],
                                            kst[0:STACK + SHIFT, j % RING, P * kt:P * kt + P],
                                            qst[0:STACK + SHIFT, j % RING, 1024 * half + 512 * q:1024 * half + 512 * q + 512],
                                            start=True, stop=True)
                last.then_inc(e_ready, 1)

            def weigh_values(s, j, kt):
                if kt == 0:
                    pe.wait_ge(v_staged, s + 1)
                    wait(pe, o_copied, s)
                pe.wait_ge(p_ready, 2 * TPB * s + 2 * kt + 2)
                for q in range(QB):
                    last = nc.tensor.matmul(outT[32 * q:32 * q + 32], mem.vstage[:, j % 2, kt, :],
                                            probs[:, kt % RING, 512 * q:512 * q + 512],
                                            start=kt == 0, stop=kt == TPB - 1)
                last.then_inc(pv_done, 1)

            def turn_out(s):
                pe.wait_ge(o_copied, s + 1)
                for c in range(QB):
                    last = nc.tensor.transpose(bank(OUT_USE)[:, P * c:P * c + P], oT[:, P * c:P * c + P], mem.ident[:])
                last.then_inc(oT_ready, 1)

            def turn_most(s, use=MOST_USE):
                pe.wait_ge(most_ready, s + 1)
                nc.tensor.transpose(bank(use)[0:SHIFT, 0:P], most[:], mem.ident[:]).then_inc(mostT_ready, 1)

            for t in range(TPB):
                for quarter in range(QB):
                    query_scores(0, 0, 0, t, quarter, first_use(t, quarter), {})
            turn_most(0, FIRST_MOST_USE)
            for t in range(AHEAD):
                for quarter in range(QB):
                    query_scores(1, 0, 1, t, quarter, second_use(t, quarter), {FIRST_MOST_USE: (mostT_cast, 1)})

            def body(r):
                for j in range(RING):
                    s = RING * r + j
                    for kt in range(TPB):
                        more, t = ahead(kt)

                        turned = {OUT_USE: (o_done, s), MOST_USE: (mostT_cast, s + 2)}
                        blocks = QB * (TPB * (s + 1) + kt + AHEAD + 1)

                        def beside(quarter):
                            if not is_last(r, j + more - 1):
                                query_scores(s + more, r, j + more, t, quarter, block_use(kt, quarter), turned)

                        beside(0)
                        key_scores(s, j, kt, 0)
                        beside(1)
                        key_scores(s, j, kt, 1)
                        beside(2)
                        beside(3)
                        if kt:
                            weigh_values(s, j, kt - 1)
                        elif not (isinstance(r, int) and r == 0 and j == 0):
                            weigh_values(s - 1, j - 1, TPB - 1)
                        if kt == TURN_OUT and not (isinstance(r, int) and r == 0 and j == 0):
                            if not is_last(r, j + more - 1):
                                free_bank(OUT_USE, blocks, turned)
                            turn_out(s - 1)
                        if kt == TURN_MOST and not is_last(r, j):
                            if not is_last(r, j + more - 1):
                                free_bank(MOST_USE, blocks, turned)
                            turn_most(s + 1)

            rounds(pe, body)
            weigh_values(PAIRS - 1, RING - 1, TPB - 1)
            pe.wait_ge(o_done, PAIRS - 1)
            turn_out(PAIRS - 1)




def normalise_rows(dve, v, ch, work, src, dst, eps, asked, answered, count):
    tiles = src.shape[1]
    for t in range(tiles):
        last = ch.mark(v.bn_stats(work.stats[:, t], src[:, t]))
    hold(dve, ch.sem, last, work.held)
    for t in range(tiles):
        last = ch.mark(v.bn_aggr(work.moments[:, t], work.stats[:, t]))
    dve.wait_ge(ch.sem, last)
    v.tensor_scalar(work.var[:, 0:tiles], work.moments[:, 0:tiles, 1], eps, None, ALU.add).then_inc(asked, 1)
    dve.wait_ge(answered, count)
    for t in range(tiles):
        last = v.tensor_scalar(dst[:, t], src[:, t], work.moments[:, t, 0:1], work.rstd[:, t:t + 1],
                               ALU.subtract, ALU.mult)
    return last


def mix_and_spike(nc, io, mem, sem):
    ctx = ExitStack()
    with ctx:
        def sb(name, shape, dt=F32):
            return ctx.enter_context(nc.sbuf_tensor(name, shape, dt))

        def ps(name, shape):
            return ctx.enter_context(nc.psum_tensor(name, shape, F32))

        HID = 4 * D
        KH = HID // P
        wo, wfc, wproj = sb("wo", [P, KD, D]), sb("wfc", [P, KD, HID]), sb("wproj", [P, KH, D])
        gamma, beta = sb("gamma", [P, D]), sb("beta", [P, D])
        scal = sb("c_scal", [P, 4])
        aT, x1T, hT = sb("aT", [P, KD, 512]), sb("x1T", [P, KD, 512]), sb("hT", [P, KH, 512])
        total, plain = sb("total", [P, GT, D]), sb("plain", [P, GT, D])
        heads_out, x1 = sb("heads_out", [P, GT, D]), sb("x1", [P, GT, D])
        y, count, rise, level = (sb(n, [P, GT, D]) for n in ("y", "count", "rise", "level"))
        work = Names()
        work.held = sem("c_held")
        work.stats, work.moments = sb("c_stats", [P, GT, 6]), sb("c_moments", [P, GT, 2])
        work.var, work.rstd = sb("c_var", [P, GT]), sb("c_rstd", [P, GT])
        turned, mixed, filled, spikes = (ps(n, [P, 2, 512]) for n in ("turned", "mixed", "filled", "spikes"))
        w_in, net_in, next_in = sem("c_w_in"), sem("c_net_in"), sem("c_next_in")
        sums_ready, heads_ready = sem("c_sums"), sem("c_heads")
        var_ready, rstd_ready = sem("c_var_ready"), sem("c_rstd_ready")
        aT_ready, aT_copied = sem("c_aT_ready"), sem("c_aT_copied")
        w_ready, w_used, x1_ready, x2_ready = sem("c_w_ready"), sem("c_w_used"), sem("c_x1_ready"), sem("c_x2_ready")
        x1_staged = sem("c_x1_staged")
        x1T_ready, x1T_copied = sem("c_x1T_ready"), sem("c_x1T_copied")
        f_ready, f_used, h_ready = sem("c_f_ready"), sem("c_f_used"), sem("c_h_ready")
        y_ready, y_copied = sem("c_y_ready"), sem("c_y_copied")
        dve_s = sem("c_dve")
        LINKS = 41

        block = ctx.enter_context(nc.Block())

        @block.sync
        def _(sp):
            for dst, src in ((gamma, io.gamma), (beta, io.beta), (wo, io.wo)):
                sp.dma_start(dst[:], src).then_inc(w_in, 16)
            for dst, src in ((wfc, io.wfc), (wproj, io.wproj)):
                sp.dma_start(dst[:], src).then_inc(net_in, 16)
            for dst, src in ((mem.l1q, io.l1q), (mem.l1k, io.l1k), (mem.l1v, io.l1v), (mem.l1g, io.l1g), (mem.l1u, io.l1u)):
                sp.dma_start(dst[:], src).then_inc(next_in, 16)
            sp.wait_ge(next_in, 5 * 16)

        @block.gpsimd
        def _(pool):
            def power(n):
                pool.wait_ge(var_ready, n)
                nc.gpsimd.tensor_tensor(work.rstd[:], work.var[:], mem.minus_half[:, 0:GT], ALU.pow).then_inc(rstd_ready, 1)

            def sums(g, b, slot):
                wait(pool, aT_ready, g)
                nc.gpsimd.tensor_copy(heads_out[:, :, :].rearrange("p t (h d) -> p h t d", d=DK),
                                      mem.attn[:, ds(HEADS * b, HEADS), ds(GT * slot, GT), :]).then_inc(heads_ready, 1)
                wait(pool, x1_ready, g)
                nc.gpsimd.tensor_tensor(total[:], mem.xs[:, ds(GT * g, GT), :], mem.enc[:, ds(GT * slot, GT), :], ALU.add).then_inc(sums_ready, 1)
                nc.gpsimd.tensor_tensor(plain[:], mem.xs[:, ds(GT * g, GT), :],
                                        beta[:, :].unsqueeze(1).to_broadcast([P, GT, D]), ALU.add).then_inc(sums_ready, 1)

            pool.wait_ge(w_in, 3 * 16)
            sums(0, 0, 0)
            power(1)
            power(2)
            sums(1, 0, 1)

            def round_of(g, more=True):
                power(3 * g + 3)
                power(3 * g + 4)
                if more:
                    sums(g + 2, (g + 2) // (TPB // GT), (g + 2) % (TPB // GT))
                power(3 * g + 5)

            run_rounds(pool, round_of, GROUPS - 2)
            round_of(GROUPS - 2, False)
            power(3 * GROUPS)

        @block.scalar
        def _(act):
            def copy_aT(g):
                act.wait_ge(aT_ready, g + 1)
                nc.scalar.activation(aT[:], turned[:], ACT.Copy).then_inc(aT_copied, 1)

            def net(g):
                act.wait_ge(x1T_ready, g + 1)
                nc.scalar.activation(x1T[:], turned[:], ACT.Copy).then_inc(x1T_copied, 1)
                for m in range(KH + 1):
                    if m < KH:
                        act.wait_ge(f_ready, KH * g + m + 1)
                        if m == 0:
                            wait(act, y_ready, g)
                        nc.scalar.activation(hT[:, m], filled[:, m % 2], ACT.Relu).then_inc(f_used, 1)
                    if m:
                        act.wait_ge(f_used, KH * g + m)
                        nc.scalar.activation(hT[:, m - 1], hT[:, m - 1], ACT.Square).then_inc(h_ready, 1)

            def stage_x1(g):
                act.wait_ge(x1_ready, g + 1)
                wait(act, x1T_ready, g)
                nc.scalar.activation(x1[:], mem.xs[:, ds(GT * g, GT), :], ACT.Copy).then_inc(x1_staged, 1)

            def copy_y(g):
                act.wait_ge(y_ready, g + 1)
                wait(act, x2_ready, g)
                nc.scalar.activation(y[:], spikes[:].rearrange("p a (c d) -> p (a c) d", d=D), ACT.Copy).then_inc(y_copied, 1)

            copy_aT(0)
            stage_x1(0)

            def round_of(g):
                net(g)
                copy_aT(g + 1)
                stage_x1(g + 1)
                copy_y(g)

            run_rounds(act, round_of, GROUPS - 1)
            net(GROUPS - 1)
            copy_y(GROUPS - 1)

        @block.vector
        def _(dve):
            v = nc.vector

            def wide(row):
                return row[:, :].unsqueeze(1).to_broadcast([P, GT, D])

            def norms(g, ch, n):
                dve.wait_ge(w_ready, g + 1)
                dve.wait_ge(sums_ready, 2 * g + 2)
                v.tensor_tensor(total[:], total[:], mixed[:].rearrange("p a (c d) -> p (a c) d", d=D), ALU.add).then_inc(w_used, 1)
                dve.wait_ge(w_used, g + 1)
                ch.link(normalise_rows(dve, v, ch, work, total, total, scal[:, 0:1], var_ready, rstd_ready, n))
                ch.link(v.tensor_tensor(total[:], total[:], wide(gamma), ALU.mult))
                ch.link(v.tensor_tensor(total[:], total[:], plain[:], ALU.add))
                normalise_rows(dve, v, ch, work, total, mem.xs[:, ds(GT * g, GT), :], 1e-5, var_ready, rstd_ready,
                               n + 1).then_inc(x1_ready, 1)

            def spike(g, ch, n):
                dve.wait_ge(y_copied, g + 1)
                ch.link(v.tensor_scalar(count[:], y[:], 1.0, None, ALU.is_gt))
                ch.link(v.scalar_tensor_tensor(rise[:], y[:], 0.9, y[:], ALU.mult, ALU.add))
                ch.link(v.tensor_tensor(level[:], count[:], rise[:], ALU.subtract))
                for step in range(3):
                    ch.mark(v.scalar_tensor_tensor(count[:], level[:], -1.0, count[:], ALU.is_lt, ALU.add))
                    ch.link(v.scalar_tensor_tensor(rise[:], level[:], -0.9, y[:], ALU.mult, ALU.add))
                    ch.link(v.scalar_tensor_tensor(level[:], level[:], -1.0, rise[:], ALU.is_lt, ALU.subtract))
                ch.link(v.scalar_tensor_tensor(count[:], level[:], -1.0, count[:], ALU.is_lt, ALU.add))
                xs = mem.xs[:, ds(GT * g, GT), :]
                dve.wait_ge(x1_staged, g + 1)
                ch.link(v.scalar_tensor_tensor(count[:], count[:], 0.2, xs, ALU.mult, ALU.add))
                normalise_rows(dve, v, ch, work, count, xs, 1e-5, var_ready, rstd_ready, n).then_inc(x2_ready, 1)

            ch = Chain(dve, dve_s)
            dve.wait_ge(w_in, 3 * 16)
            red, blue, yellow = (mem.rby[:, i:i + 1] for i in range(3))
            ch.link(v.tensor_scalar(scal[:, 0:1], blue, 1e-6, 1e-5, ALU.mult, ALU.add))
            ch.link(v.tensor_scalar(scal[:, 1:2], red, 0.1, 1.0, ALU.mult, ALU.add))
            ch.link(v.scalar_tensor_tensor(scal[:, 2:3], yellow, 0.05, scal[:, 1:2], ALU.mult, ALU.add))
            ch.link(v.tensor_scalar(gamma[:], gamma[:], scal[:, 2:3], None, ALU.mult))
            norms(0, ch, 1)
            base = ch.n

            def round_of(g):
                ch = Chain(dve, dve_s, base + LINKS * g)
                norms(g + 1, ch, 3 * g + 3)
                spike(g, ch, 3 * g + 5)
                assert ch.n == LINKS, ch.n

            run_rounds(dve, round_of, GROUPS - 1)
            spike(GROUPS - 1, Chain(dve, dve_s, base + LINKS * (GROUPS - 1)), 3 * GROUPS)

        @block.tensor
        def _(pe):
            def mix(g):
                wait(pe, x1T_copied, g)
                pe.wait_ge(heads_ready, g + 1)
                for t in range(GT):
                    for k in range(KD):
                        last = nc.tensor.transpose(turned[:, k, P * t:P * t + P], heads_out[:, t, P * k:P * k + P], mem.ident[:])
                last.then_inc(aT_ready, 1)
                pe.wait_ge(aT_copied, g + 1)
                wait(pe, w_used, g)
                for t in range(GT):
                    for k in range(KD):
                        last = nc.tensor.matmul(mixed[:, t // 2, D * (t % 2):D * (t % 2) + D], aT[:, k, P * t:P * t + P],
                                                wo[:, k], start=k == 0, stop=k == KD - 1)
                last.then_inc(w_ready, 1)

            def first(g):
                pe.wait_ge(x1_staged, g + 1)
                for t in range(GT):
                    for k in range(KD):
                        last = nc.tensor.transpose(turned[:, k, P * t:P * t + P], x1[:, t, P * k:P * k + P], mem.ident[:])
                last.then_inc(x1T_ready, 1)
                pe.wait_ge(x1T_copied, g + 1)
                for m in range(KH):
                    wait(pe, f_used, KH * g + max(m - 1, 0))
                    for k in range(KD):
                        last = nc.tensor.matmul(filled[:, m % 2], wfc[:, k, P * m:P * m + P], x1T[:, k], start=k == 0, stop=k == KD - 1)
                    last.then_inc(f_ready, 1)

            def second(g):
                pe.wait_ge(h_ready, KH * (g + 1))
                wait(pe, y_copied, g)
                for t in range(GT):
                    for k in range(KH):
                        last = nc.tensor.matmul(spikes[:, t // 2, D * (t % 2):D * (t % 2) + D], hT[:, k, P * t:P * t + P],
                                                wproj[:, k], start=k == 0, stop=k == KH - 1)
                last.then_inc(y_ready, 1)

            pe.wait_ge(w_in, 3 * 16)
            mix(0)
            pe.wait_ge(net_in, 2 * 16)

            def round_of(g):
                first(g)
                mix(g + 1)
                second(g)

            run_rounds(pe, round_of, GROUPS - 1)
            first(GROUPS - 1)
            second(GROUPS - 1)


def linear_attention_and_gate(nc, io, mem, sem):
    ctx = ExitStack()
    with ctx:
        def sb(name, shape, dt=F32):
            return ctx.enter_context(nc.sbuf_tensor(name, shape, dt))

        def ps(name, shape):
            return ctx.enter_context(nc.psum_tensor(name, shape, F32))

        NH = 8
        W = NH * P
        wq, wk, wv, wg, wu = mem.l1q, mem.l1k, mem.l1v, mem.l1g, mem.l1u
        wo, wd = sb("d_wo", [P, NH, D]), sb("d_wd", [P, NH, D])
        wide = [room[:, W * i:W * i + W].rearrange("p (h i) -> p h i", i=P)
                for room, n in ((mem.attn[:].rearrange("p a t d -> p (a t d)"), 8), (mem.enc[:].rearrange("p t d -> p (t d)"), 4))
                for i in range(n)]
        norm_in, norm_out, norm_mlp = sb("norm_in", [P, KD]), sb("norm_out", [P, 1]), sb("norm_mlp", [P, KD])
        causal, keep = sb("causal", [P, P]), sb("keep", [P, TILES + 1])
        square, wide_square = sb("square", [P, D]), sb("wide_square", [P, NH, P])
        ms, rs = sb("ms", [P, 2]), sb("rs", [P, 2])
        oms, ors = sb("oms", [P, NH]), sb("ors", [P, NH])
        h, h2 = sb("h", [P, D]), sb("h2", [P, D])
        hT, h2T = sb("d_hT", [P, KD, P]), sb("d_h2T", [P, KD, P])
        qT, kT, kt, v_, at, on, onT, state, gate, guT = wide[:10]
        mid, res = sb("mid", [P, D]), sb("res", [P, 1, D])
        work = Names()
        work.held = sem("d_held")
        work.stats, work.moments = sb("d_stats", [P, 1, 6]), sb("d_moments", [P, 1, 2])
        work.var, work.rstd = sb("d_var", [P, 1]), sb("d_rstd", [P, 1])
        A, B, C, E = (ps(n, [P, 2, 512]) for n in "ABCE")
        heads_of = lambda bank: bank[:].rearrange("p a (h i) -> p (a h) i", i=P)
        names = ("w_in out_in out_scaled ready ms_eps oms_eps ms2_eps ms_ready rs_ready h_ready hT_ready hT_copied q_ready q_out k_ready k_out "
                 "v_ready v_out kt_ready kt_out at_ready at_out o_ready o_squared oms_ready ors_ready on_ready "
                 "kv_ready kv_used state_ready onT_ready onT_copied wo_ready mid_ready "
                 "ms2_ready rs2_ready h2_ready h2T_ready h2T_copied g_ready g_out u_ready gu_ready d_ready d_used "
                 "var_ready rstd_ready x_ready dve_s pool_held act_held").split()
        S = {n: sem(f"d_{n}") for n in names}

        def rounds(eng, side_by_side):
            run_rounds(eng, lambda c: side_by_side(c, True), TILES - 2)
            side_by_side(TILES - 2, False)

        block = ctx.enter_context(nc.Block())

        @block.sync
        def _(sp):
            for dst, src in ((norm_in, io.norm_in), (norm_out, io.norm_out), (norm_mlp, io.norm_mlp), (causal, io.causal),
                             (keep, io.keep)):
                sp.dma_start(dst[:], src).then_inc(S["w_in"], 16)
            sp.dma_start(wo[:], io.l1o).then_inc(S["out_in"], 16)
            sp.dma_start(wd[:], io.l1d).then_inc(S["out_in"], 16)

        @block.gpsimd
        def _(pool):
            def input_root(c):
                hold(pool, S["ms_ready"], c + 1, S["pool_held"])
                nc.gpsimd.tensor_scalar(ms[:, 0:1], ms[:, 0:1], 1e-5, None, ALU.add).then_inc(S["ms_eps"], 1)
                pool.wait_ge(S["ms_eps"], c + 1)
                nc.gpsimd.tensor_tensor(rs[:, 0:1], ms[:, 0:1], mem.minus_half[:, 0:1], ALU.pow).then_inc(S["rs_ready"], 1)

            def output_roots(c):
                hold(pool, S["oms_ready"], c + 1, S["pool_held"])
                nc.gpsimd.tensor_scalar(oms[:], oms[:], 1.0 / P, 1e-5, ALU.mult, ALU.add).then_inc(S["oms_eps"], 1)
                pool.wait_ge(S["oms_eps"], c + 1)
                nc.gpsimd.tensor_tensor(ors[:], oms[:], mem.minus_half[:, 0:NH], ALU.pow).then_inc(S["ors_ready"], 1)

            def net_root(c):
                hold(pool, S["ms2_ready"], c + 1, S["pool_held"])
                nc.gpsimd.tensor_scalar(ms[:, 1:2], ms[:, 1:2], 1e-5, None, ALU.add).then_inc(S["ms2_eps"], 1)
                pool.wait_ge(S["ms2_eps"], c + 1)
                nc.gpsimd.tensor_tensor(rs[:, 1:2], ms[:, 1:2], mem.minus_half[:, 0:1], ALU.pow).then_inc(S["rs2_ready"], 1)

            def final_root(c):
                pool.wait_ge(S["var_ready"], c + 1)
                nc.gpsimd.tensor_tensor(work.rstd[:], work.var[:], mem.minus_half[:, 0:1], ALU.pow).then_inc(S["rstd_ready"], 1)

            def side_by_side(c, more):
                output_roots(c + 1)
                if more:
                    input_root(c + 2)
                final_root(c)
                net_root(c + 1)

            input_root(0)
            output_roots(0)
            input_root(1)
            net_root(0)
            rounds(pool, side_by_side)
            final_root(TILES - 1)

        @block.scalar
        def _(act):
            a = nc.scalar.activation

            def norm_input(c):
                xs = mem.xs[:, ds(c, 1), :].rearrange("p o d -> p (o d)")
                a(square[:], xs, ACT.Square, scale=D ** -0.5, accum_out=ms[:, 0:1]).then_inc(S["ms_ready"], 1)
                wait(act, S["hT_ready"], c)
                hold(act, S["rs_ready"], c + 1, S["act_held"])
                a(h[:], xs, ACT.Copy, scale=rs[:, 0:1]).then_inc(S["h_ready"], 1)
                act.wait_ge(S["hT_ready"], c + 1)
                wait(act, S["v_ready"], c)
                a(hT[:], E[:, 0, 0:D].rearrange("p (k t) -> p k t", k=KD), ACT.Copy).then_inc(S["hT_copied"], 1)

            def project(c):
                act.wait_ge(S["q_ready"], c + 1)
                wait(act, S["o_ready"], c)
                a(qT[:], heads_of(A), ACT.Copy).then_inc(S["q_out"], 1)
                act.wait_ge(S["v_ready"], c + 1)
                wait(act, S["kv_ready"], c)
                a(v_[:], heads_of(C), ACT.Copy).then_inc(S["v_out"], 1)
                act.wait_ge(S["kt_ready"], c + 1)
                a(kt[:], heads_of(E), ACT.Copy).then_inc(S["kt_out"], 1)

            def norm_output(c):
                act.wait_ge(S["o_ready"], c + 1)
                wait(act, S["oms_ready"], c)
                a(wide_square[:], heads_of(B), ACT.Square).then_inc(S["o_squared"], 1)

            def turn_output(c):
                act.wait_ge(S["onT_ready"], c + 1)
                wait(act, S["wo_ready"], c)
                a(onT[:], heads_of(C), ACT.Copy).then_inc(S["onT_copied"], 1)

            def net_input(c):
                act.wait_ge(S["mid_ready"], c + 1)
                a(square[:], mid[:], ACT.Square, scale=D ** -0.5, accum_out=ms[:, 1:2]).then_inc(S["ms2_ready"], 1)
                act.wait_ge(S["rs2_ready"], c + 1)
                wait(act, S["h2T_ready"], c)
                a(h2[:], mid[:], ACT.Copy, scale=rs[:, 1:2]).then_inc(S["h2_ready"], 1)

            def turn_net_input(c):
                act.wait_ge(S["h2T_ready"], c + 1)
                wait(act, S["u_ready"], c)
                a(h2T[:], E[:, 1, 0:D].rearrange("p (k t) -> p k t", k=KD), ACT.Copy).then_inc(S["h2T_copied"], 1)

            def silu(c):
                act.wait_ge(S["g_ready"], c + 1)
                wait(act, S["gu_ready"], c)
                a(gate[:], heads_of(C), ACT.Silu).then_inc(S["g_out"], 1)

            norm_input(0)
            project(0)
            norm_output(0)
            turn_output(0)
            norm_input(1)
            net_input(0)

            def side_by_side(c, more):
                project(c + 1)
                turn_net_input(c)
                silu(c)
                norm_output(c + 1)
                turn_output(c + 1)
                if more:
                    norm_input(c + 2)
                net_input(c + 1)

            rounds(act, side_by_side)
            turn_net_input(TILES - 1)
            silu(TILES - 1)

        @block.vector
        def _(dve):
            v = nc.vector

            def attention(c):
                dve.wait_ge(S["k_ready"], c + 1)
                wait(dve, S["at_ready"], c)
                v.tensor_copy(kT[:], heads_of(B)).then_inc(S["k_out"], 1)
                dve.wait_ge(S["at_ready"], c + 1)
                wait(dve, S["o_ready"], c)
                v.tensor_tensor(at[:], heads_of(A), causal[:, :].unsqueeze(1).to_broadcast([P, NH, P]), ALU.mult).then_inc(S["at_out"], 1)

            def output(c):
                dve.wait_ge(S["o_squared"], c + 1)
                wait(dve, S["ors_ready"], c)
                v.reduce_sum(oms[:], wide_square[:], AX.X).then_inc(S["oms_ready"], 1)
                dve.wait_ge(S["kv_ready"], c + 1)
                v.tensor_tensor(state[:], state[:], heads_of(A), ALU.add).then_inc(S["kv_used"], 1)
                dve.wait_ge(S["kv_used"], c + 1)
                v.tensor_scalar(state[:], state[:], keep[:, ds(c + 1, 1)], None, ALU.mult).then_inc(S["state_ready"], 1)
                dve.wait_ge(S["ors_ready"], c + 1)
                wait(dve, S["onT_ready"], c)
                v.tensor_tensor(on[:], heads_of(B), ors[:, :].unsqueeze(2).to_broadcast([P, NH, P]), ALU.mult).then_inc(S["on_ready"], 1)

            def gated(c):
                dve.wait_ge(S["g_out"], c + 1)
                dve.wait_ge(S["u_ready"], c + 1)
                wait(dve, S["d_ready"], c)
                v.tensor_tensor(guT[:], gate[:], heads_of(E), ALU.mult).then_inc(S["gu_ready"], 1)

            def finish(c):
                LINKS = 3
                ch = Chain(dve, S["dve_s"], LINKS * c)
                xs = mem.xs[:, ds(c, 1), :]
                dve.wait_ge(S["d_ready"], c + 1)
                v.tensor_tensor(res[:, 0], mid[:], A[:, 0, 0:D], ALU.add).then_inc(S["d_used"], 1)
                dve.wait_ge(S["h2_ready"], c + 1)
                dve.wait_ge(S["d_used"], c + 1)
                ch.link(v.tensor_tensor(res[:], res[:], xs, ALU.add))
                normalise_rows(dve, v, ch, work, res, xs, 1e-5, S["var_ready"], S["rstd_ready"], c + 1).then_inc(S["x_ready"], 1)
                assert ch.n == LINKS

            def middle(c):
                dve.wait_ge(S["wo_ready"], c + 1)
                xs = mem.xs[:, ds(c, 1), :].rearrange("p o d -> p (o d)")
                v.tensor_tensor(mid[:], xs, B[:, 0, 0:D], ALU.add).then_inc(S["mid_ready"], 1)

            dve.wait_ge(S["w_in"], 5 * 16)
            v.memset(state[:], 0.0).then_inc(S["ready"], 1)
            for w, norm in ((wq, norm_in), (wk, norm_in), (wv, norm_in), (wg, norm_mlp), (wu, norm_mlp)):
                for k in range(KD):
                    v.tensor_scalar(w[:, k], w[:, k], norm[:, k:k + 1], None, ALU.mult).then_inc(S["ready"], 1)
            attention(0)
            dve.wait_ge(S["out_in"], 2 * 16)
            v.tensor_scalar(wo[:], wo[:], norm_out[:, 0:1], None, ALU.mult).then_inc(S["out_scaled"], 1)
            output(0)
            middle(0)

            def side_by_side(c, more):
                attention(c + 1)
                output(c + 1)
                gated(c)
                finish(c)
                middle(c + 1)

            rounds(dve, side_by_side)
            gated(TILES - 1)
            finish(TILES - 1)

        @block.tensor
        def _(pe):
            mm, turn = nc.tensor.matmul, nc.tensor.transpose
            bank = lambda X, i: X[:, i // 4, P * (i % 4):P * (i % 4) + P]

            def start(c):
                pe.wait_ge(S["h_ready"], c + 1)
                for k in range(KD):
                    last = turn(E[:, 0, P * k:P * k + P], h[:, P * k:P * k + P], mem.ident[:])
                last.then_inc(S["hT_ready"], 1)

            def project(c):
                pe.wait_ge(S["hT_copied"], c + 1)
                for w, X, done in ((wq, A, S["q_ready"]), (wk, B, S["k_ready"])):
                    if w is wk:
                        wait(pe, S["mid_ready"], c)
                    for i in range(NH):
                        for k in range(KD):
                            last = mm(bank(X, i), w[:, k, P * i:P * i + P], hT[:, k], start=k == 0, stop=k == KD - 1)
                    last.then_inc(done, 1)
                for half in range(2):
                    for k in range(KD):
                        last = mm(C[:, half], hT[:, k], wv[:, k, 512 * half:512 * half + 512], start=k == 0, stop=k == KD - 1)
                last.then_inc(S["v_ready"], 1)

            def turn_keys(c):
                pe.wait_ge(S["k_out"], c + 1)
                for i in range(NH):
                    last = turn(bank(E, i), kT[:, i], mem.ident[:])
                last.then_inc(S["kt_ready"], 1)

            def scores(c):
                pe.wait_ge(S["q_out"], c + 1)
                for i in range(NH):
                    last = mm(bank(A, i), kT[:, i], qT[:, i], start=True, stop=True)
                last.then_inc(S["at_ready"], 1)

            def outputs(c):
                pe.wait_ge(S["at_out"], c + 1)
                pe.wait_ge(S["v_out"], c + 1)
                wait(pe, S["state_ready"], c)
                for i in range(NH):
                    mm(bank(B, i), at[:, i], v_[:, i], start=True, stop=False)
                    last = mm(bank(B, i), qT[:, i], state[:, i], start=False, stop=True)
                last.then_inc(S["o_ready"], 1)

            def keys_values(c):
                pe.wait_ge(S["kt_out"], c + 1)
                for i in range(NH):
                    last = mm(bank(A, i), kt[:, i], v_[:, i], start=True, stop=True)
                last.then_inc(S["kv_ready"], 1)

            def turn_output(c):
                pe.wait_ge(S["on_ready"], c + 1)
                for i in range(NH):
                    last = turn(bank(C, i), on[:, i], mem.ident[:])
                last.then_inc(S["onT_ready"], 1)

            def output_projection(c):
                pe.wait_ge(S["onT_copied"], c + 1)
                for i in range(NH):
                    last = mm(B[:, 0, 0:D], onT[:, i], wo[:, i], start=i == 0, stop=i == NH - 1)
                last.then_inc(S["wo_ready"], 1)

            def turn_net_input(c):
                pe.wait_ge(S["h2_ready"], c + 1)
                for k in range(KD):
                    last = turn(E[:, 1, P * k:P * k + P], h2[:, P * k:P * k + P], mem.ident[:])
                last.then_inc(S["h2T_ready"], 1)

            def net(c, w, X, done):
                for i in range(NH):
                    for k in range(KD):
                        last = mm(bank(X, i), w[:, k, P * i:P * i + P], h2T[:, k], start=k == 0, stop=k == KD - 1)
                last.then_inc(done, 1)

            def down(c):
                pe.wait_ge(S["gu_ready"], c + 1)
                for i in range(NH):
                    last = mm(A[:, 0, 0:D], guT[:, i], wd[:, i], start=i == 0, stop=i == NH - 1)
                last.then_inc(S["d_ready"], 1)

            start(0)
            pe.wait_ge(S["ready"], 11)
            project(0)
            turn_keys(0)
            scores(0)
            outputs(0)
            keys_values(0)
            turn_output(0)
            pe.wait_ge(S["out_in"], 2 * 16)
            pe.wait_ge(S["out_scaled"], 1)
            output_projection(0)
            start(1)

            def side_by_side(c, more):
                wait(pe, S["d_used"], c)
                project(c + 1)
                turn_keys(c + 1)
                scores(c + 1)
                pe.wait_ge(S["kt_out"], c + 2)
                turn_net_input(c)
                pe.wait_ge(S["h2T_copied"], c + 1)
                net(c, wg, C, S["g_ready"])
                outputs(c + 1)
                keys_values(c + 1)
                net(c, wu, E, S["u_ready"])
                pe.wait_ge(S["g_out"], c + 1)
                turn_output(c + 1)
                pe.wait_ge(S["kv_used"], c + 2)
                down(c)
                output_projection(c + 1)
                if more:
                    start(c + 2)

            rounds(pe, side_by_side)
            turn_net_input(TILES - 1)
            pe.wait_ge(S["h2T_copied"], TILES)
            net(TILES - 1, wg, C, S["g_ready"])
            net(TILES - 1, wu, E, S["u_ready"])
            pe.wait_ge(S["d_used"], TILES - 1)
            down(TILES - 1)

NE, TOP = 8, 2
MAX_TILES = TOP * TILES + NE


def route(nc, io, mem, moe, sem):
    ctx = ExitStack()
    with ctx:
        def sb(name, shape, dt=F32):
            return ctx.enter_context(nc.sbuf_tensor(name, shape, dt))

        def ps(name, shape):
            return ctx.enter_context(nc.psum_tensor(name, shape, F32))

        I32 = mybir.dt.int32
        wg, bg = sb("r_wg", [P, KD, NE]), sb("r_bg", [P, NE])
        later, earlier = sb("later", [P, NE, NE]), sb("earlier", [P, NE, NE])
        below, ones = sb("below", [P, P]), sb("ones", [P, P])
        tile_numbers = sb("tile_numbers", [P, MAX_TILES])
        x, xT = sb("r_x", [P, GT, D]), sb("r_xT", [P, KD, 512])
        gate, top, total = sb("r_gate", [P, GT, NE]), sb("r_top", [P, GT]), sb("r_total", [P, GT])
        above, same, rank = sb("above", [P, GT, NE, NE]), sb("same", [P, GT, NE, NE]), sb("rank", [P, GT, NE])
        weights, chosen = sb("weights", [P, TILES, NE]), sb("chosen", [P, TILES, NE])
        counts = [sb(f"counts{i}", [P, TILES, NE]) for i in range(2)]
        used, first_tile, after_tile, start = (sb(n, [P, NE]) for n in ("used", "first_tile", "after_tile", "start"))
        pairs = sb("pairs", [P, NE, NE])
        slots, match = sb("slots", [P, TILES, NE]), sb("match", [P, TILES, NE])
        high, low = sb("high", [P, TILES]), sb("low", [P, TILES])
        passed, expert = sb("passed", [P, MAX_TILES, NE]), sb("expert", [P, MAX_TILES])
        turned, sums = ps("r_turned", [P, 2, 512]), ps("r_sums", [P, 2, 512])
        names = ("w_in x_ready xT_ready xT_copied logit_ready logit_out shifted exp_ready gates_ready "
                 "counts_ready sums_ready slots_ready scattered dve_s").split()
        S = {n: sem(f"r_{n}") for n in names}
        LOADS = 7
        block = ctx.enter_context(nc.Block())

        @block.sync
        def _(sp):
            for dst, src in ((wg, io.wg), (bg, io.bg), (later, io.later), (earlier, io.earlier), (below, io.below),
                             (ones, io.ones), (tile_numbers, io.tile_numbers)):
                sp.dma_start(dst[:], src).then_inc(S["w_in"], 16)
            for dst, src in ((moe.w1, io.w1), (moe.w3, io.w3), (moe.w2, io.w2), (moe.b1, io.b1), (moe.b3, io.b3), (moe.b2, io.b2)):
                sp.dma_start(dst[:], src).then_inc(moe.w_in, 16)

        @block.gpsimd
        def _(pool):
            pool.wait_ge(S["slots_ready"], 2)
            for t in range(TILES):
                for i in range(TOP):
                    at = bass.IndirectOffsetOnAxis(ap=moe.slot[:, i, t:t + 1], axis=0)
                    nc.gpsimd.indirect_dma_start(io.sorted_x, at, mem.xs[:, t, :], None).then_inc(S["scattered"], 16)
            pool.wait_ge(S["scattered"], 16 * TOP * TILES)

        @block.scalar
        def _(act):
            a = nc.scalar.activation

            def group(g):
                wait(act, S["xT_ready"], g)
                a(x[:], mem.xs[:, ds(GT * g, GT), :], ACT.Copy).then_inc(S["x_ready"], 1)
                act.wait_ge(S["xT_ready"], g + 1)
                a(xT[:], turned[:], ACT.Copy).then_inc(S["xT_copied"], 1)
                act.wait_ge(S["shifted"], g + 1)
                a(gate[:], gate[:], ACT.Exp).then_inc(S["exp_ready"], 1)

            run_rounds(act, group, GROUPS)

        @block.vector
        def _(dve):
            v = nc.vector
            LINKS = 15
            dve.wait_ge(S["w_in"], 16 * LOADS)

            def group(g):
                ch = Chain(dve, S["dve_s"], LINKS * g)
                wait(dve, S["gates_ready"], g)
                dve.wait_ge(S["logit_ready"], g + 1)
                v.tensor_tensor(gate[:], sums[:, 0, 0:GT * NE].rearrange("p (t e) -> p t e", e=NE),
                                bg[:, :].unsqueeze(1).to_broadcast([P, GT, NE]), ALU.add).then_inc(S["logit_out"], 1)
                dve.wait_ge(S["logit_out"], g + 1)
                ch.link(v.reduce_max(top[:], gate[:], AX.X))
                v.tensor_tensor(gate[:], gate[:], top[:, :].unsqueeze(2).to_broadcast([P, GT, NE]), ALU.subtract).then_inc(S["shifted"], 1)
                dve.wait_ge(S["exp_ready"], g + 1)
                ch.link(v.reduce_sum(total[:], gate[:], AX.X))
                ch.link(v.reciprocal(total[:], total[:]))
                ch.link(v.tensor_tensor(gate[:], gate[:], total[:, :].unsqueeze(2).to_broadcast([P, GT, NE]), ALU.mult))
                for t in range(GT):
                    other = gate[:, t, :].unsqueeze(1).to_broadcast([P, NE, NE])
                    own = gate[:, t, :].unsqueeze(2).to_broadcast([P, NE, NE])
                    ch.mark(v.tensor_tensor(above[:, t], other, own, ALU.is_gt))
                    last = ch.mark(v.tensor_tensor(same[:, t], other, own, ALU.is_equal))
                dve.wait_ge(ch.sem, last)
                ch.link(v.tensor_tensor(same[:], same[:], later[:, :, :].unsqueeze(1).to_broadcast([P, GT, NE, NE]), ALU.mult))
                ch.link(v.tensor_tensor(above[:], above[:], same[:], ALU.add))
                ch.link(v.reduce_sum(rank[:], above[:], AX.X))
                v.tensor_scalar(chosen[:, ds(GT * g, GT), :], rank[:], TOP - 0.5, None, ALU.is_lt)
                v.scalar_tensor_tensor(weights[:, ds(GT * g, GT), :], rank[:], TOP - 0.5, gate[:],
                                       ALU.is_lt, ALU.mult).then_inc(S["gates_ready"], 1)
                assert ch.n == LINKS, ch.n

            run_rounds(dve, group, GROUPS)
            ch = Chain(dve, S["dve_s"], LINKS * GROUPS)
            dve.wait_ge(S["gates_ready"], GROUPS)
            src, step = chosen, 1
            while step < TILES:
                dst = counts[0] if src is not counts[0] else counts[1]
                ch.mark(v.tensor_copy(dst[:, 0:step], src[:, 0:step]))
                ch.link(v.tensor_tensor(dst[:, step:], src[:, step:], src[:, 0:TILES - step], ALU.add))
                src, step = dst, 2 * step
            count = src
            v.tensor_copy(used[:], count[:, TILES - 1, :]).then_inc(S["counts_ready"], 1)
            dve.wait_ge(S["sums_ready"], 1)
            magic = 1.5 * 2 ** 23
            ch.link(v.tensor_scalar(used[:], sums[:, 0, 64:64 + NE], 1.0 / P, (P - 1.0) / P - 0.5 + 1.0 / 512, ALU.mult, ALU.add))
            ch.link(v.tensor_scalar(used[:], used[:], magic, magic, ALU.add, ALU.subtract))
            ch.link(v.tensor_tensor(pairs[:], earlier[:], used[:, :].unsqueeze(1).to_broadcast([P, NE, NE]), ALU.mult))
            ch.link(v.reduce_sum(first_tile[:], pairs[:], AX.X))
            ch.mark(v.tensor_tensor(after_tile[:], first_tile[:], used[:], ALU.add))
            ch.link(v.tensor_scalar(start[:], first_tile[:], float(P), -1.0, ALU.mult, ALU.add))
            ch.link(v.tensor_tensor(start[:], start[:], sums[:, 0, 0:NE], ALU.add))
            ch.link(v.tensor_tensor(slots[:], count[:], start[:, :].unsqueeze(1).to_broadcast([P, TILES, NE]), ALU.add))
            ch.link(v.tensor_tensor(slots[:], slots[:], chosen[:], ALU.mult))
            ch.mark(v.reduce_max(high[:], slots[:], AX.X))
            ch.link(v.reduce_sum(low[:], slots[:], AX.X))
            ch.mark(v.tensor_copy(moe.slot[:, 0, :], high[:]))
            ch.link(v.tensor_tensor(low[:], low[:], high[:], ALU.subtract))
            v.tensor_copy(moe.slot[:, 1, :], low[:]).then_inc(S["slots_ready"], 1)
            ch.link(v.tensor_tensor(passed[:], tile_numbers[:, :].unsqueeze(2).to_broadcast([P, MAX_TILES, NE]),
                                    after_tile[:, :].unsqueeze(1).to_broadcast([P, MAX_TILES, NE]), ALU.is_ge))
            ch.link(v.reduce_sum(expert[:], passed[:], AX.X))
            ch.link(v.tensor_scalar(expert[:], expert[:], NE - 1.0, None, ALU.min))
            v.tensor_copy(moe.expert[:], expert[:]).then_inc(S["slots_ready"], 1)
            ch.link(v.tensor_tensor(match[:], slots[:], high[:, :].unsqueeze(2).to_broadcast([P, TILES, NE]), ALU.is_equal))
            ch.link(v.tensor_tensor(match[:], match[:], weights[:], ALU.mult))
            ch.link(v.reduce_sum(moe.weight[:, 0, :], match[:], AX.X))
            ch.link(v.tensor_tensor(match[:], weights[:], match[:], ALU.subtract))
            ch.link(v.reduce_sum(moe.weight[:, 1, :], match[:], AX.X))

        @block.tensor
        def _(pe):
            mm, turn = nc.tensor.matmul, nc.tensor.transpose
            pe.wait_ge(S["w_in"], 16 * LOADS)

            def group(g):
                pe.wait_ge(S["x_ready"], g + 1)
                for t in range(GT):
                    for k in range(KD):
                        last = turn(turned[:, k, P * t:P * t + P], x[:, t, P * k:P * k + P], mem.ident[:])
                last.then_inc(S["xT_ready"], 1)
                pe.wait_ge(S["xT_copied"], g + 1)
                wait(pe, S["logit_out"], g)
                for t in range(GT):
                    for k in range(KD):
                        last = mm(sums[:, 0, NE * t:NE * t + NE], xT[:, k, P * t:P * t + P], wg[:, k], start=k == 0, stop=k == KD - 1)
                last.then_inc(S["logit_ready"], 1)

            run_rounds(pe, group, GROUPS)
            pe.wait_ge(S["counts_ready"], 1)
            mm(sums[:, 0, 0:NE], below[:], used[:], start=True, stop=True)
            mm(sums[:, 0, 64:64 + NE], ones[:], used[:], start=True, stop=True).then_inc(S["sums_ready"], 1)


def run_experts(nc, io, mem, moe, sem):
    ctx = ExitStack()
    with ctx:
        def sb(name, shape, dt=F32):
            return ctx.enter_context(nc.sbuf_tensor(name, shape, dt))

        def ps(name, shape):
            return ctx.enter_context(nc.psum_tensor(name, shape, F32))

        HID = 512
        KH = HID // P
        x, xT = sb("m_x", [P, 2, D]), sb("m_xT", [P, 2, KD, P])
        h1, h3, h, hT = (sb(n, [P, 2, HID]) for n in ("m_h1", "m_h3", "m_h", "m_hT"))
        y = sb("m_y", [P, 2, D])
        first, third, turned, small = (ps(f"m_{n}", [P, 2, 512]) for n in ("first", "third", "turned", "small"))
        names = ("xT_ready xT_copied h1_ready h1_out h3_ready h3_out product h_ready hT_ready hT_copied y_ready y_out").split()
        S = {n: sem(f"m_{n}") for n in names}
        x_in, stored = [sem(f"m_x_in{j}") for j in range(2)], [sem(f"m_stored{j}") for j in range(2)]
        ROUNDS = MAX_TILES // 2
        block = ctx.enter_context(nc.Block())

        @block.sync
        def _(sp):
            def tiles(r):
                for j in range(2):
                    n = 2 * r + j
                    wait(sp, S["xT_ready"], n - 1)
                    sp.dma_start(x[:, j, :], io.sorted_x[ds(P * n, P), :]).then_inc(x_in[j], 16)

            run_rounds(sp, tiles, ROUNDS)

        @block.gpsimd
        def _(pool):
            def tiles(r):
                for j in range(2):
                    n = 2 * r + j
                    pool.wait_ge(S["y_out"], n + 1)
                    pool.dma_start(io.sorted_y[ds(P * n, P), :], y[:, j, :]).then_inc(stored[j], 16)

            run_rounds(pool, tiles, ROUNDS)
            for j in range(2):
                pool.wait_ge(stored[j], 16 * ROUNDS)

        @block.scalar
        def _(act):
            a = nc.scalar.activation

            def copy_x(n, j):
                act.wait_ge(S["xT_ready"], n + 1)
                wait(act, S["h3_ready"], n - 1)
                a(xT[:, j], small[:, 1 - j, 0:D].rearrange("p (k t) -> p k t", k=KD), ACT.Copy).then_inc(S["xT_copied"], 1)

            def net(n, j):
                act.wait_ge(S["product"], n + 1)
                wait(act, S["hT_ready"], n - 1)
                a(h[:, j], h1[:, j], ACT.Silu).then_inc(S["h_ready"], 1)
                act.wait_ge(S["hT_ready"], n + 1)
                wait(act, S["y_ready"], n - 1)
                a(hT[:, j], turned[:, j], ACT.Copy).then_inc(S["hT_copied"], 1)

            def tiles(r, final=False):
                for j in range(2):
                    n = 2 * r + j
                    net(n, j)
                    if not final:
                        copy_x(n + 2, j)

            copy_x(0, 0)
            copy_x(1, 1)
            run_rounds(act, tiles, ROUNDS - 1)
            tiles(ROUNDS - 1, True)

        @block.vector
        def _(dve):
            v = nc.vector
            dve.wait_ge(moe.w_in, 16 * 6)

            def biases(e, n, j):
                dve.wait_ge(S["h1_ready"], n + 1)
                wait(dve, S["h_ready"], n - 1)
                v.tensor_tensor(h1[:, j], first[:, j], moe.b1[:, ds(e, 1), :].rearrange("p o n -> p (o n)"), ALU.add).then_inc(S["h1_out"], 1)
                dve.wait_ge(S["h3_ready"], n + 1)
                v.tensor_tensor(h3[:, j], third[:, j], moe.b3[:, ds(e, 1), :].rearrange("p o n -> p (o n)"), ALU.add).then_inc(S["h3_out"], 1)
                dve.wait_ge(S["h3_out"], n + 1)
                v.tensor_tensor(h1[:, j], h1[:, j], h3[:, j], ALU.mult).then_inc(S["product"], 1)

            def output(e, n, r, j):
                dve.wait_ge(S["y_ready"], n + 1)
                wait(dve, stored[j], 16 * r)
                v.tensor_tensor(y[:, j], small[:, j, D:2 * D], moe.b2[:, ds(e, 1), :].rearrange("p o n -> p (o n)"), ALU.add).then_inc(S["y_out"], 1)

            def expert_of(n):
                return dve.value_load(moe.expert[0:1, ds(n, 1)], min_val=0, max_val=NE - 1)

            def tiles(r, final=False):
                for j in range(2):
                    n = 2 * r + j
                    if not (final and j == 1):
                        biases(expert_of(n + 1), n + 1, 1 - j)
                    output(expert_of(n), n, r, j)

            biases(expert_of(0), 0, 0)
            run_rounds(dve, tiles, ROUNDS - 1)
            tiles(ROUNDS - 1, True)

        @block.tensor
        def _(pe):
            mm, turn = nc.tensor.matmul, nc.tensor.transpose
            pe.wait_ge(moe.w_in, 16 * 6)

            def expert_of(n):
                return pe.value_load(moe.expert[0:1, ds(n, 1)], min_val=0, max_val=NE - 1)

            def turn_x(n, r, j):
                pe.wait_ge(x_in[j], 16 * (r + 1))
                wait(pe, S["y_out"], n - 2)
                for k in range(KD):
                    last = turn(small[:, 1 - j, P * k:P * k + P], x[:, j, P * k:P * k + P], mem.ident[:])
                last.then_inc(S["xT_ready"], 1)

            def up(e, n, j, w, bank, free, done):
                if w is moe.w1:
                    pe.wait_ge(S["xT_copied"], n + 1)
                wait(pe, S[free], n - 1)
                for k in range(KD):
                    last = mm(bank[:, j], xT[:, j, k], w[:, ds(e, 1), k, :].rearrange("p o n -> p (o n)"), start=k == 0, stop=k == KD - 1)
                last.then_inc(S[done], 1)

            def turn_h(n, j):
                pe.wait_ge(S["h_ready"], n + 1)
                wait(pe, S["hT_copied"], n - 1)
                for k in range(KH):
                    last = turn(turned[:, j, P * k:P * k + P], h[:, j, P * k:P * k + P], mem.ident[:])
                last.then_inc(S["hT_ready"], 1)

            def down(e, n, j):
                pe.wait_ge(S["hT_copied"], n + 1)
                for k in range(KH):
                    last = mm(small[:, j, D:2 * D], hT[:, j, P * k:P * k + P], moe.w2[:, ds(e, 1), k, :].rearrange("p o n -> p (o n)"),
                              start=k == 0, stop=k == KH - 1)
                last.then_inc(S["y_ready"], 1)

            def tiles(r, final=False):
                for j in range(2):
                    n = 2 * r + j
                    more = not (final and j == 1)
                    if more:
                        e = expert_of(n + 1)
                        up(e, n + 1, 1 - j, moe.w1, first, "h1_out", "h1_ready")
                    turn_h(n, j)
                    if not final:
                        turn_x(n + 2, r + 1, j)
                    if more:
                        up(e, n + 1, 1 - j, moe.w3, third, "h3_out", "h3_ready")
                    down(expert_of(n), n, j)

            turn_x(0, 0, 0)
            turn_x(1, 0, 1)
            up(expert_of(0), 0, 0, moe.w1, first, "h1_out", "h1_ready")
            up(expert_of(0), 0, 0, moe.w3, third, "h3_out", "h3_ready")
            run_rounds(pe, tiles, ROUNDS - 1)
            tiles(ROUNDS - 1, True)


def combine(nc, io, mem, moe, sem):
    ctx = ExitStack()
    with ctx:
        def sb(name, shape, dt=F32):
            return ctx.enter_context(nc.sbuf_tensor(name, shape, dt))

        def ps(name, shape):
            return ctx.enter_context(nc.psum_tensor(name, shape, F32))

        wf, bf = sb("o_wf", [P, KD, D]), sb("o_bf", [P, D])
        RING = 4
        back = sb("back", [P, RING, GT, TOP, D])
        mix, mixT, out = sb("o_mix", [P, 2, GT, D]), sb("o_mixT", [P, 2, KD, 512]), sb("o_out", [P, 2, GT, D])
        work = Names()
        work.held = sem("o_held")
        work.stats, work.moments = sb("o_stats", [P, GT, 6]), sb("o_moments", [P, GT, 2])
        work.var, work.rstd = sb("o_var", [P, GT]), sb("o_rstd", [P, GT])
        turned, projected = ps("o_turned", [P, 2, 2, 512]), ps("o_projected", [P, 2, 2, 512])
        names = "w_in mix_ready mT_ready mT_copied f_ready f_used var_ready rstd_ready done dve_s dve_mix".split()
        S = {n: sem(f"o_{n}") for n in names}
        fetched, stored = [sem(f"o_fetched{j}") for j in range(RING)], [sem(f"o_stored{j}") for j in range(2)]
        tiles_of = lambda bank: bank.rearrange("p a (c d) -> p (a c) d", d=D)
        block = ctx.enter_context(nc.Block())

        @block.sync
        def _(sp):
            sp.dma_start(wf[:], io.wf).then_inc(S["w_in"], 16)
            sp.dma_start(bf[:], io.bf).then_inc(S["w_in"], 16)

            def groups(r):
                for j in range(2):
                    g = 2 * r + j
                    sp.wait_ge(S["done"], g + 1)
                    sp.dma_start(io.out[:, ds(GT * g, GT), :], out[:, j]).then_inc(stored[j], 16)

            run_rounds(sp, groups, GROUPS // 2)
            for j in range(2):
                sp.wait_ge(stored[j], 16 * GROUPS // 2)

        @block.gpsimd
        def _(pool):
            def root(g):
                pool.wait_ge(S["var_ready"], g + 1)
                nc.gpsimd.tensor_tensor(work.rstd[:], work.var[:], mem.minus_half[:, 0:GT], ALU.pow).then_inc(S["rstd_ready"], 1)

            for g in range(GROUPS):
                wait(pool, S["mix_ready"], g - RING + 1)
                for t in range(GT):
                    for i in range(TOP):
                        at = bass.IndirectOffsetOnAxis(ap=moe.slot[:, i, GT * g + t:GT * g + t + 1], axis=0)
                        nc.gpsimd.indirect_dma_start(back[:, g % RING, t, i, :], None, io.sorted_y, at).then_inc(fetched[g % RING], 16)
                if g >= 2:
                    root(g - 2)
            root(GROUPS - 2)
            root(GROUPS - 1)

        @block.scalar
        def _(act):
            def groups(r):
                for j in range(2):
                    g = 2 * r + j
                    act.wait_ge(S["mT_ready"], g + 1)
                    wait(act, S["f_ready"], g - 1)
                    nc.scalar.activation(mixT[:, j], turned[:, j], ACT.Copy).then_inc(S["mT_copied"], 1)

            run_rounds(act, groups, GROUPS // 2)

        @block.vector
        def _(dve):
            v = nc.vector
            LINKS = 4 + 1 + 8
            dve.wait_ge(S["w_in"], 32)

            def mixing(g, r, j, ch):
                dve.wait_ge(fetched[j], 16 * TOP * GT * (r + 1))
                wait(dve, S["mT_ready"], g - 1)
                for t in range(GT):
                    last = ch.mark(v.tensor_scalar(mix[:, j % 2, t], back[:, j, t, 0], moe.weight[:, 0, ds(GT * g + t, 1)], None, ALU.mult))
                dve.wait_ge(ch.sem, last)
                for t in range(GT):
                    last = v.scalar_tensor_tensor(mix[:, j % 2, t], back[:, j, t, 1], moe.weight[:, 1, ds(GT * g + t, 1)], mix[:, j % 2, t],
                                                  ALU.mult, ALU.add)
                last.then_inc(S["mix_ready"], 1)

            def finish(g, stores, j, ch):
                dve.wait_ge(S["f_ready"], g + 1)
                wait(dve, stored[j % 2], 16 * stores)
                v.tensor_tensor(out[:, j % 2], tiles_of(projected[:, j % 2]), bf[:, :].unsqueeze(1).to_broadcast([P, GT, D]), ALU.add).then_inc(S["f_used"], 1)
                dve.wait_ge(S["f_used"], g + 1)
                ch.link(v.tensor_tensor(out[:, j % 2], out[:, j % 2], mem.xs[:, ds(GT * g, GT), :], ALU.add))
                normalise_rows(dve, v, ch, work, out[:, j % 2], out[:, j % 2], 1e-5, S["var_ready"], S["rstd_ready"], g + 1).then_inc(S["done"], 1)

            def groups(r):
                for j in range(RING):
                    g = RING * r + j
                    ch = Chain(dve, S["dve_s"], LINKS * g)
                    more = g < GROUPS - 1
                    if more:
                        mixing(g + 1, r + (j + 1) // RING, (j + 1) % RING, ch)
                    finish(g, 2 * r + j // 2, j, ch)
                    assert ch.n == LINKS or not more, ch.n

            ch = Chain(dve, S["dve_mix"], 0)
            mixing(0, 0, 0, ch)
            for r in range(GROUPS // RING):
                groups(r)

        @block.tensor
        def _(pe):
            mm, turn = nc.tensor.matmul, nc.tensor.transpose
            pe.wait_ge(S["w_in"], 32)

            def groups(r):
                for j in range(2):
                    g = 2 * r + j
                    pe.wait_ge(S["mix_ready"], g + 1)
                    wait(pe, S["mT_copied"], g - 1)
                    for t in range(GT):
                        for k in range(KD):
                            last = turn(turned[:, j, k, P * t:P * t + P], mix[:, j, t, P * k:P * k + P], mem.ident[:])
                    last.then_inc(S["mT_ready"], 1)
                    pe.wait_ge(S["mT_copied"], g + 1)
                    wait(pe, S["f_used"], g - 1)
                    for t in range(GT):
                        for k in range(KD):
                            last = mm(tiles_of(projected[:, j])[:, t], mixT[:, j, k, P * t:P * t + P], wf[:, k], start=k == 0, stop=k == KD - 1)
                    last.then_inc(S["f_ready"], 1)

            run_rounds(pe, groups, GROUPS // 2)


def build(nc, a, out, upto=9):
    ctx = ExitStack()
    with ctx:
        sems = []

        def sem(name):
            sems.append(nc.alloc_semaphore(name=name))
            return sems[-1]

        io, mem = Names(), Names()
        io.x = a["L0_attn_x"].rearrange("b s d -> (b s) d")
        io.wq, io.wk, io.wv, io.wo = (a[f"L0_attn_W{n}"].rearrange("(k p) n -> p k n", p=P) for n in "qkvo")
        io.bq, io.bk = (a[f"L0_attn_b{n}"] for n in "qk")
        io.bv = a["L0_attn_bv"].partition_broadcast(P)
        io.rby = a["L0_attn_rby"].partition_broadcast(P)
        io.pos, io.powers, io.ident, io.delta = (a[n] for n in ("pos", "powers", "ident", "delta"))
        io.powers = io.powers.partition_broadcast(P)
        io.q_parts = nc.dram_tensor("q_parts", (PARTS, BATCH, D, SEQ), BF16, kind="Internal").ap()
        io.k_parts = nc.dram_tensor("k_parts", (PARTS, BATCH, D, SEQ), BF16, kind="Internal").ap()

        io.bo, io.gamma, io.beta = (a[n].partition_broadcast(P) for n in ("L0_attn_bo", "L0_attn_ln_gamma", "L0_attn_ln_beta"))
        io.wfc = a["L0_ffn_W_fc"].rearrange("(k p) n -> p k n", p=P)
        io.wproj = a["L0_ffn_W_proj"].rearrange("(k p) n -> p k n", p=P)

        io.norm_in, io.norm_out, io.norm_mlp = (a[f"L1_attn_{n}"] for n in ("attn_norm_w", "attn_out_norm_w", "mlp_norm_w"))
        io.l1q, io.l1k, io.l1v, io.l1o, io.l1g, io.l1u, io.l1d = (
            a[f"L1_attn_W{n}"].rearrange("(k p) n -> p k n", p=P) for n in ("q", "k", "v", "o", "gate", "up", "down"))
        io.causal, io.keep = a["causal"], a["keep"].partition_broadcast(P)

        io.w1, io.w3, io.w2 = (a[f"L1_ffn_W{n}"].rearrange("e (k p) n -> p e k n", p=P) for n in "132")
        io.b1, io.b3, io.b2 = (a[f"L1_ffn_b{n}"].rearrange("e n -> (e n)").partition_broadcast(P).rearrange("p (e n) -> p e n", e=NE) for n in "132")
        io.sorted_x = nc.dram_tensor("sorted_x", (MAX_TILES * P, D), F32, kind="Internal").ap()
        io.sorted_y = nc.dram_tensor("sorted_y", (MAX_TILES * P, D), F32, kind="Internal").ap()
        io.earlier, io.below, io.ones = a["earlier"], a["below"], a["ones"]
        io.tile_numbers = a["tile_numbers"].partition_broadcast(P)
        io.wg, io.wf = (a[f"L1_ffn_W{n}"].rearrange("(k p) n -> p k n", p=P) for n in "gf")
        io.bg, io.bf = (a[f"L1_ffn_b{n}"].partition_broadcast(P) for n in "gf")
        io.later = a["later"]
        io.out = out.rearrange("b s d -> (b s) d").rearrange("(t p) d -> p t d", p=P)

        def sb(c, name, shape, dt=F32):
            return c.enter_context(nc.sbuf_tensor(name, shape, dt))

        mem.xs = sb(ctx, "xs", [P, TILES, D])
        mem.ident = sb(ctx, "ident", [P, P])
        mem.minus_half = sb(ctx, "minus_half", [P, 8])
        mem.rby = sb(ctx, "rby", [P, 3])
        mem.logit_scale, mem.out_scale = sb(ctx, "logit_scale", [P, 1]), sb(ctx, "out_scale", [P, 1])
        first = ctx.enter_context(ExitStack())
        mem.enc = sb(first, "enc", [P, TPB, D])
        mem.attn = sb(first, "attn", [P, PAIRS, TPB, DK])
        heads = first.enter_context(ExitStack())
        mem.delta = sb(heads, "delta", [SHIFT, SEQ], BF16)
        mem.values = sb(heads, "values", [P, PAIRS, TPB, VW])
        mem.vstage = sb(heads, "vstage", [P, 2, TPB, 32])
        mem.qst = sb(heads, "qst", [P, 4, SEQ], BF16)
        mem.kst = sb(heads, "kst", [P, 4, SEQ], BF16)
        embed_and_project(nc, io, mem, sem)
        if upto < 2: return
        attend(nc, io, mem, sem)
        heads.close()
        if upto < 3: return
        mem.l1q, mem.l1k, mem.l1v, mem.l1g, mem.l1u = (sb(first, f"l1_w{n}", [P, KD, 4 * D]) for n in "qkvgu")
        mix_and_spike(nc, io, mem, sem)
        if upto < 4: return
        nc.clear_and_free_semaphores(sems)
        nc.all_engine_barrier()
        linear_attention_and_gate(nc, io, mem, sem)
        first.close()
        if upto < 5: return
        moe = Names()
        moe.slot = sb(ctx, "e_slot", [P, TOP, TILES], mybir.dt.uint32)
        moe.expert = sb(ctx, "e_expert", [P, MAX_TILES], mybir.dt.int32)
        moe.weight = sb(ctx, "e_weight", [P, TOP, TILES])
        nets = ctx.enter_context(ExitStack())
        moe.w1, moe.w3 = sb(nets, "e_w1", [P, NE, KD, 512]), sb(nets, "e_w3", [P, NE, KD, 512])
        moe.w2 = sb(nets, "e_w2", [P, NE, 4, D])
        moe.b1, moe.b3, moe.b2 = sb(nets, "e_b1", [P, NE, 512]), sb(nets, "e_b3", [P, NE, 512]), sb(nets, "e_b2", [P, NE, D])
        moe.w_in = sem("e_w_in")
        route(nc, io, mem, moe, sem)
        if upto < 6: return
        run_experts(nc, io, mem, moe, sem)
        nets.close()
        if upto < 7: return
        combine(nc, io, mem, moe, sem)


def layout(inputs):
    a = {n: np.ascontiguousarray(v) for n, v in inputs.items()}
    for n in ("L0_attn_Wq", "L0_attn_Wk", "L0_attn_Wv", "L0_attn_Wo", "L0_ffn_W_fc", "L0_ffn_W_proj"):
        a[n] = np.ascontiguousarray(a[n].T)
    for n in ("L0_attn_bq", "L0_attn_bk", "L1_attn_attn_norm_w", "L1_attn_attn_out_norm_w", "L1_attn_mlp_norm_w"):
        a[n] = np.ascontiguousarray(a[n].reshape(-1, P).T)
    a["pos"] = (np.arange(TPB)[None, :] * P + np.arange(P)[:, None]).astype(np.float32)
    a["powers"] = np.power(np.float32(10000.0), np.float32(2.0) * np.arange(0, D, 2, dtype=np.float32) / np.float32(D)).astype(np.float32)
    a["below"] = np.triu(np.ones((P, P), np.float32), 1)
    a["ones"] = np.ones((P, P), np.float32)
    a["tile_numbers"] = np.arange(MAX_TILES).astype(np.float32)
    a["earlier"] = np.ascontiguousarray(np.broadcast_to(np.tril(np.ones((NE, NE), np.float32), -1), (P, NE, NE)))
    a["later"] = np.ascontiguousarray(np.broadcast_to(np.triu(np.ones((8, 8), np.float32), 1), (P, 8, 8)))
    a["causal"] = np.triu(np.ones((P, P), np.float32))
    a["keep"] = (np.arange(TILES + 1) % TPB != 0).astype(np.float32)
    a["ident"] = np.eye(P, dtype=np.float32)
    a["delta"] = np.repeat(np.eye(SHIFT), P, axis=1).astype(mybir.dt.np(BF16))
    return {f"in_{n}": v for n, v in a.items()}


def kernel(**inputs):
    import concourse.bacc as bacc
    from concourse.bass_utils import run_bass_kernel_spmd

    nc = bacc.Bacc("TRN2", target_bir_lowering=False, num_devices=1)
    arrays = layout(inputs)
    a = {n[len("in_"):]: nc.dram_tensor(n, v.shape, mybir.dt.from_np(v.dtype), kind="ExternalInput").ap()
         for n, v in arrays.items()}
    out = nc.dram_tensor("out", (BATCH, SEQ, D), F32, kind="ExternalOutput").ap()
    build(nc, a, out)
    return run_bass_kernel_spmd(nc, [arrays], core_ids=[0]).results[0]["out"]
```

```python
import math
from contextlib import ExitStack

import numpy as np

import concourse.bass as bass
from concourse import mybir

F32 = mybir.dt.float32
BF16 = mybir.dt.bfloat16
F32R = mybir.dt.float32r
ALU = mybir.AluOpType
ACT = mybir.ActivationFunctionType
AX = mybir.AxisListType
ds = bass.ds

P = 128
BATCH, SEQ, D = 2, 2048, 256
TILES = BATCH * SEQ // P
TPB = SEQ // P
KD = D // P
HEADS, DK = 16, 16
PAIRS = BATCH * HEADS
VW = DK + 1
PARTS = 3
STACK = 6 * DK
SHIFT = TPB
QB = SEQ // 512
GT = 4
GROUPS = TILES // GT


class Names:
    pass


class Chain:

    def __init__(self, eng, sem, base=0):
        self.eng, self.sem, self.base, self.n = eng, sem, base, 0

    def mark(self, ins):
        ins.then_inc(self.sem, 1)
        self.n += 1
        return self.base + self.n

    def link(self, ins):
        self.eng.wait_ge(self.sem, self.mark(ins))


def wait(eng, sem, value):
    if not isinstance(value, int) or value > 0:
        eng.wait_ge(sem, value)


def hold(eng, sem, value, held):
    eng.wait_ge(sem, value)
    eng.sem_inc(held, 1)


def run_rounds(eng, body, rounds):
    body(0)
    with eng.Fori(1, rounds) as r:
        body(r)


def part_views(ap):
    return ap.rearrange("(t p) d -> p t d", p=P)


def embed_and_project(nc, io, mem, sem):
    ctx = ExitStack()
    with ctx:
        def sb(name, shape, dt=F32):
            return ctx.enter_context(nc.sbuf_tensor(name, shape, dt))

        def ps(name, shape):
            return ctx.enter_context(nc.psum_tensor(name, shape, F32))

        wq, wk, wv = (sb(n, [P, KD, D]) for n in ("wq", "wk", "wv"))
        bq, bk = sb("bq", [P, KD]), sb("bk", [P, KD])
        bqc = sb("bqc", [P, KD])
        bv = sb("bv", [P, D])
        pos, powers = sb("pos", [P, TPB]), sb("powers", [P, P])
        denom = sb("denom", [P, P])
        spare = mem.attn[:, :, :, :].rearrange("p s t d -> p (s t d)")
        angle, turns, reduced = (spare[:, SEQ * i:SEQ * i + SEQ].rearrange("p (t f) -> p t f", f=P) for i in range(3))
        scal = sb("scal", [P, 8])
        x0 = mem.qst[:, 0:2, :].rearrange("p a t -> p (a t)").bitcast(F32).rearrange("p (j t d) -> p j t d", j=2, d=D)
        x0T = sb("x0T", [P, 2, KD, 512])
        qkf = sb("qkf", [P, 2, KD, 512])
        parts = sb("parts", [P, 2, 2, PARTS, KD, 512], BF16)
        pT, pQ, pK, pV = (ps(n, [P, KD, 512]) for n in ("pT", "pQ", "pK", "pV"))
        x_in, c_in = sem("a_x_in"), sem("a_c_in")
        dve_s = sem("a_dve")
        square_ready, root_ready = sem("a_square"), sem("a_root")
        angles_ready, enc_ready = sem("a_angles"), sem("a_enc")
        x0_ready = sem("a_x0")
        xT_ready, xT_copied = sem("a_xT"), sem("a_xT_copied")
        q_ready, k_ready, v_ready = sem("a_q"), sem("a_k"), sem("a_v")
        q_out, k_out, v_out = sem("a_q_out"), sem("a_k_out"), sem("a_v_out")
        p1, r1, p2, p3 = (sem(f"a_{n}") for n in ("p1", "r1", "p2", "p3"))
        stored = [sem(f"a_stored{j}") for j in range(2)]
        ready0 = sem("a_ready0")
        enc_v = mem.enc[:, :, :].rearrange("p t (f two) -> p t f two", two=2)

        def rounds(eng, pair_of_groups):
            run_rounds(eng, pair_of_groups, GROUPS // 2 - 1)
            pair_of_groups(GROUPS // 2 - 1)

        def is_final(pair, g):
            return isinstance(pair, int) and 2 * pair + g == GROUPS - 1

        block = ctx.enter_context(nc.Block())

        @block.sync
        def _(sp):
            for dst, src in ((pos, io.pos), (powers, io.powers), (mem.rby, io.rby),
                             (mem.ident, io.ident), (wq, io.wq), (wk, io.wk), (wv, io.wv),
                             (bv, io.bv), (bq, io.bq), (bk, io.bk), (mem.delta, io.delta)):
                sp.dma_start(dst[:], src).then_inc(c_in, 16)
            sp.dma_start(mem.xs[:, 0:TPB, :], part_views(io.x)[:, 0:TPB, :]).then_inc(x_in, 16)
            sp.dma_start(mem.xs[:, TPB:, :], part_views(io.x)[:, TPB:, :]).then_inc(x_in, 16)

            def store(pair):
                for g in range(2):
                    b, slot = pair // 2, (2 * pair + g) % GT
                    sp.wait_ge(p3, 4 * pair + 2 * g + 2)
                    for w, scratch in ((0, io.q_parts), (1, io.k_parts)):
                        for s in range(PARTS):
                            dst = scratch[s, ds(b, 1), :, ds(512 * slot, 512)]
                            sp.dma_start(dst.rearrange("o (m p) t -> p (o m) t", p=P),
                                         parts[:, g, w, s, :, :]).then_inc(stored[g], 16)

            run_rounds(sp, store, GROUPS // 2)
            for j in range(2):
                sp.wait_ge(stored[j], 4 * 96)

        @block.gpsimd
        def _(pool):
            nc.gpsimd.memset(mem.minus_half[:], -0.5).then_inc(ready0, 1)
            pool.wait_ge(ready0, 1)
            pool.wait_ge(square_ready, 1)
            nc.gpsimd.tensor_tensor(scal[:, 5:6], scal[:, 7:8], mem.minus_half[:, 0:1], ALU.pow).then_inc(root_ready, 1)
            nc.gpsimd.memset(mem.values[:, :, :, DK:VW], 1.0).then_inc(ready0, 1)
            nc.gpsimd.memset(mem.vstage[:], 0.0).then_inc(ready0, 1)
            pool.wait_ge(ready0, 3)
            nc.gpsimd.memset(mem.kst[STACK:STACK + SHIFT, :, :], 1.0).then_inc(ready0, 1)
            pool.wait_ge(ready0, 4)

        @block.scalar
        def _(act):
            act.wait_ge(angles_ready, 1)
            nc.scalar.activation(enc_v[:, :, :, 0], reduced, ACT.Sin).then_inc(enc_ready, 1)
            act.wait_ge(angles_ready, 2)
            nc.scalar.activation(enc_v[:, :, :, 1], turns, ACT.Sin).then_inc(enc_ready, 1)

            def copy_x(n, g):
                act.wait_ge(xT_ready, n)
                nc.scalar.activation(x0T[:, g], pT[:], ACT.Copy).then_inc(xT_copied, 1)

            copy_x(1, 0)

            def pair_of_groups(pair):
                for g in range(2):
                    n = 2 * pair + g + 1
                    wait(act, p3, 2 * n - 2)
                    act.wait_ge(q_ready, n)
                    for m in range(KD):
                        last = nc.scalar.activation(qkf[:, 0, m], pQ[:, m], ACT.Identity,
                                                    bias=bqc[:, m:m + 1], scale=mem.logit_scale[:, 0:1])
                    last.then_inc(q_out, 1)
                    act.wait_ge(k_ready, n)
                    for m in range(KD):
                        last = nc.scalar.activation(qkf[:, 1, m], pK[:, m], ACT.Identity,
                                                    bias=bk[:, m:m + 1])
                    last.then_inc(k_out, 1)
                    if not is_final(pair, g):
                        copy_x(n + 1, 1 - g)
                    wait(act, stored[g], 96 * pair)
                    for w, done in ((0, q_out), (1, k_out)):
                        act.wait_ge(done, n)
                        nc.scalar.activation(parts[:, g % 2, w, 0], qkf[:, w], ACT.Copy).then_inc(p1, 1)
                    for w in range(2):
                        act.wait_ge(r1, 2 * n - 1 + w)
                        nc.scalar.activation(parts[:, g % 2, w, 1], qkf[:, w], ACT.Copy).then_inc(p2, 1)

            rounds(act, pair_of_groups)

        @block.vector
        def _(dve):
            ch = Chain(dve, dve_s)
            dve.wait_ge(c_in, 11 * 16)
            red, blue, yellow = (mem.rby[:, i:i + 1] for i in range(3))
            v = nc.vector
            ch.link(v.tensor_scalar(scal[:, 0:1], yellow, 0.1 * math.sin(0.5 * math.pi), 1.0, ALU.mult, ALU.add))
            ch.link(v.tensor_scalar(denom[:], powers[:], scal[:, 0:1], None, ALU.mult))
            ch.link(v.reciprocal(denom[:], denom[:]))
            ch.link(v.tensor_tensor(angle, pos[:, :].unsqueeze(2).to_broadcast([P, TPB, P]),
                                    denom[:, :].unsqueeze(1).to_broadcast([P, TPB, P]), ALU.mult))
            two_pi = 2 * math.pi
            c1 = float(np.float32(6.28125))
            c2 = float(np.float32(two_pi - c1))
            c2 = math.floor(c2 * 2 ** 21) / 2 ** 21
            c3 = two_pi - c1 - c2
            magic = 1.5 * 2 ** 23
            ch.link(v.tensor_scalar(turns, angle, 1 / two_pi, None, ALU.mult))
            ch.link(v.tensor_scalar(turns, turns, magic, magic, ALU.add, ALU.subtract))
            ch.link(v.scalar_tensor_tensor(reduced, turns, -c1, angle, ALU.mult, ALU.add))
            ch.link(v.scalar_tensor_tensor(reduced, turns, -c2, reduced, ALU.mult, ALU.add))
            ch.link(v.scalar_tensor_tensor(reduced, turns, -c3, reduced, ALU.mult, ALU.add))
            in_range = 3.1415925
            v.tensor_scalar(reduced, reduced, in_range, -in_range, ALU.min, ALU.max).then_inc(angles_ready, 1)
            dve.wait_ge(angles_ready, 1)
            ch.link(v.tensor_scalar(turns, reduced, math.pi / 2, None, ALU.add))
            ch.link(v.tensor_scalar(angle, turns, math.pi, None, ALU.is_gt))
            ch.link(v.scalar_tensor_tensor(turns, angle, -two_pi, turns, ALU.mult, ALU.add))
            v.tensor_scalar(turns, turns, in_range, -in_range, ALU.min, ALU.max).then_inc(angles_ready, 1)
            ch.link(v.tensor_scalar(scal[:, 1:2], red, 0.1, 1.0, ALU.mult, ALU.add))
            ch.link(v.scalar_tensor_tensor(scal[:, 2:3], blue, 0.05, scal[:, 1:2], ALU.mult, ALU.add))
            ch.link(v.scalar_tensor_tensor(scal[:, 3:4], yellow, 0.15, scal[:, 2:3], ALU.mult, ALU.add))
            ch.link(v.tensor_scalar(scal[:, 4:5], red, 0.0, 1.0, ALU.mult, ALU.add))
            v.tensor_scalar(scal[:, 7:8], scal[:, 4:5], float(DK), None, ALU.mult).then_inc(square_ready, 1)
            dve.wait_ge(root_ready, 1)
            ch.link(v.tensor_tensor(mem.logit_scale[:, 0:1], scal[:, 3:4], scal[:, 5:6], ALU.mult))
            ch.link(v.tensor_scalar(bqc[:], bq[:], mem.logit_scale[:, 0:1], None, ALU.mult))
            ch.link(v.tensor_scalar(mem.out_scale[:, 0:1], yellow, 0.1 * math.sin(math.pi), 1.0, ALU.mult, ALU.add))
            dve.wait_ge(x_in, 32)
            dve.wait_ge(enc_ready, 2)

            def encode(n, g):
                wait(dve, xT_ready, n - 2)
                v.tensor_tensor(x0[:, g], mem.xs[:, ds(GT * (n - 1), GT), :],
                                mem.enc[:, ds(GT * ((n - 1) % GT), GT), :], ALU.add).then_inc(x0_ready, 1)

            encode(1, 0)

            def pair_of_groups(pair):
                for g in range(2):
                    n = 2 * pair + g + 1
                    b, slot = pair // 2, (2 * pair + g) % GT
                    if not is_final(pair, g):
                        encode(n + 1, 1 - g)
                    for w in range(2):
                        dve.wait_ge(p1, 2 * n - 1 + w)
                        v.tensor_tensor(qkf[:, w], qkf[:, w], parts[:, g % 2, w, 0], ALU.subtract).then_inc(r1, 1)
                    for w in range(2):
                        dve.wait_ge(p2, 2 * n - 1 + w)
                        v.tensor_tensor(parts[:, g % 2, w, 2], qkf[:, w], parts[:, g % 2, w, 1],
                                        ALU.subtract).then_inc(p3, 1)
                    dve.wait_ge(v_ready, n)
                    v.tensor_tensor(
                        mem.values[:, ds(HEADS * b, HEADS), ds(GT * slot, GT), 0:DK].rearrange("p h t d -> p t h d"),
                        pV[:].rearrange("p a (c h d) -> p (a c) h d", c=2, d=DK),
                        bv[:, :].rearrange("p (h d) -> p h d", d=DK).unsqueeze(1).to_broadcast([P, GT, HEADS, DK]),
                        ALU.add).then_inc(v_out, 1)

            rounds(dve, pair_of_groups)

        @block.tensor
        def _(pe):
            def turn_x(n, g):
                pe.wait_ge(x0_ready, n)
                wait(pe, xT_copied, n - 1)
                for t in range(GT):
                    for k in range(KD):
                        last = nc.tensor.transpose(pT[:, k, P * t:P * t + P], x0[:, g, t, P * k:P * k + P], mem.ident[:])
                last.then_inc(xT_ready, 1)

            turn_x(1, 0)

            def pair_of_groups(pair):
                for g in range(2):
                    n = 2 * pair + g + 1
                    pe.wait_ge(xT_copied, n)
                    for w, acc, done, free in ((wq, pQ, q_ready, q_out), (wk, pK, k_ready, k_out)):
                        wait(pe, free, n - 1)
                        for m in range(KD):
                            for k in range(KD):
                                last = nc.tensor.matmul(acc[:, m], w[:, k, P * m:P * m + P], x0T[:, g % 2, k],
                                                        start=k == 0, stop=k == KD - 1)
                        last.then_inc(done, 1)
                    if not is_final(pair, g):
                        turn_x(n + 1, 1 - g)
                    wait(pe, v_out, n - 1)
                    for t in range(GT):
                        for k in range(KD):
                            last = nc.tensor.matmul(pV[:, t // 2, D * (t % 2):D * (t % 2) + D],
                                                    x0T[:, g % 2, k, P * t:P * t + P], wv[:, k],
                                                    start=k == 0, stop=k == KD - 1)
                    last.then_inc(v_ready, 1)

            rounds(pe, pair_of_groups)


Q_PARTS, K_PARTS = (0, 0, 0, 1, 1, 2), (0, 1, 2, 0, 1, 0)


def attend(nc, io, mem, sem):
    ctx = ExitStack()
    with ctx:
        def sb(name, shape, dt=F32):
            return ctx.enter_context(nc.sbuf_tensor(name, shape, dt))

        def ps(name, shape):
            return ctx.enter_context(nc.psum_tensor(name, shape, F32))

        RING = 4
        AHEAD = 4
        qst, kst = mem.qst, mem.kst
        probs = sb("probs", [P, RING, SEQ])
        top = sb("top", [P, 2, TPB, QB])
        most = sb("most", [P, TPB])
        mostT = sb("mostT", [SHIFT, P], BF16)
        oT = sb("oT", [P, 512])
        recip = sb("recip", [P, QB, QB])
        scoresT, outT = ps("scoresT", [P, 2, 1024]), ps("outT", [P, 512])
        scores = ps("scores", [P, 3, 512])
        loaded = [sem(f"b_loaded{j}") for j in range(RING)]
        m_ready, m_used = sem("b_m_ready"), sem("b_m_used")
        e_ready, p_ready, pv_done = sem("b_e_ready"), sem("b_p_ready"), sem("b_pv_done")
        v_staged = sem("b_v_staged")
        most_ready, mostT_ready, mostT_cast, shift_ready = (sem(f"b_{x}") for x in ("most", "mostT", "mostT_cast", "shift"))
        o_copied, oT_ready, o_done = sem("b_o_copied"), sem("b_oT"), sem("b_o_done")
        dve_s = sem("b_dve")
        bo, zeros = sb("bo", [P, D]), sb("zeros", [P, D])
        bo_in, zeros_ready, cleared, enc_ready = sem("b_bo_in"), sem("b_zeros"), sem("b_cleared"), sem("b_enc")
        ROUNDS = PAIRS // RING
        LOADS = 16 * (len(Q_PARTS) + len(K_PARTS))

        def rounds(eng, body):
            body(0)
            with eng.Fori(1, ROUNDS - 1) as r:
                body(r)
            body(ROUNDS - 1)

        def ahead(kt):
            return 1 + (kt + AHEAD) // TPB, (kt + AHEAD) % TPB

        TURN_OUT, TURN_MOST = 2, TPB - AHEAD
        OUT_USE, MOST_USE = QB * (TURN_OUT + 1), QB * (TURN_MOST + 1) + 1
        block_use = lambda kt, quarter: QB * kt + quarter + (kt > TURN_OUT) + (kt > TURN_MOST)
        FIRST_MOST_USE = QB * TPB
        first_use = lambda t, quarter: QB * t + quarter
        second_use = lambda t, quarter: FIRST_MOST_USE + 1 + QB * t + quarter
        bank = lambda use: scores[:, use % 3]

        def is_last(r, j, of=PAIRS - 1):
            return isinstance(r, int) and RING * r + j >= of

        block = ctx.enter_context(nc.Block())

        @block.sync
        def _(sp):
            def load(s, j):
                for stack, scratch, order in ((qst, io.q_parts, Q_PARTS), (kst, io.k_parts, K_PARTS)):
                    rows = scratch.rearrange("s b f t -> s (b f) t")
                    for i, part in enumerate(order):
                        sp.dma_start(stack[DK * i:DK * i + DK, j, :], rows[part, ds(DK * s, DK), :]).then_inc(loaded[j], 16)

            for j in range(RING):
                load(j, j)
            sp.dma_start(bo[:], io.bo).then_inc(bo_in, 16)
            sp.wait_ge(zeros_ready, 1)
            sp.dma_start(io.sorted_x.rearrange("(t p) d -> p t d", p=P),
                         zeros[:, :].unsqueeze(1).to_broadcast([P, MAX_TILES, D])).then_inc(cleared, 16)

            def body(r):
                for j in range(RING):
                    if not is_last(r, j, PAIRS - RING):
                        sp.wait_ge(e_ready, 2 * TPB * (RING * r + j + 1))
                        load(RING * r + j + RING, j)

            rounds(sp, body)
            sp.wait_ge(cleared, 16)

        @block.gpsimd
        def _(pool):
            def shift(s, j):
                pool.wait_ge(mostT_cast, s + 1)
                pool.wait_ge(v_staged, s + 1)
                nc.gpsimd.tensor_tensor(
                    qst[STACK:STACK + SHIFT, j, :].rearrange("p (t q) -> p t q", q=P),
                    mostT[:, :].unsqueeze(1).to_broadcast([SHIFT, TPB, P]),
                    mem.delta[:, :].rearrange("p (t q) -> p t q", q=P), ALU.mult).then_inc(shift_ready, 1)

            def stage(s, j):
                wait(pool, shift_ready, s)
                nc.gpsimd.tensor_copy(mem.vstage[:, j % 2, :, 0:VW],
                                      mem.values[:, ds(s, 1), :, :].rearrange("p o t d -> p (o t) d")).then_inc(v_staged, 1)

            stage(0, 0)
            shift(0, 0)
            pool.wait_ge(shift_ready, 1)
            nc.gpsimd.memset(zeros[:], 0.0).then_inc(zeros_ready, 1)
            pool.wait_ge(bo_in, 16)
            pool.wait_ge(zeros_ready, 1)
            nc.gpsimd.tensor_tensor(mem.enc[:], mem.enc[:], bo[:, :].unsqueeze(1).to_broadcast([P, TPB, D]), ALU.add).then_inc(enc_ready, 1)
            pool.wait_ge(enc_ready, 1)

            def body(r):
                for j in range(RING):
                    if not is_last(r, j):
                        s = RING * r + j
                        wait(pool, pv_done, TPB * s)
                        stage(s + 1, j + 1)
                        shift(s + 1, (j + 1) % RING)

            rounds(pool, body)

        @block.scalar
        def _(act):
            def cast_most(s, use=MOST_USE):
                act.wait_ge(mostT_ready, s + 1)
                wait(act, shift_ready, s)
                nc.scalar.activation(mostT[:], bank(use)[0:SHIFT, 0:P], ACT.Copy, scale=-1.0).then_inc(mostT_cast, 1)

            def take_out(s):
                act.wait_ge(pv_done, TPB * (s + 1))
                wait(act, oT_ready, s)
                nc.scalar.activation(oT[:], outT[:], ACT.Copy).then_inc(o_copied, 1)

            cast_most(0, FIRST_MOST_USE)

            def body(r):
                for j in range(RING):
                    s = RING * r + j
                    for kt in range(TPB):
                        if kt == 1 and not (isinstance(r, int) and r == 0 and j == 0):
                            take_out(s - 1)
                        if kt == 13 and not is_last(r, j):
                            cast_most(s + 1)
                        wait(act, pv_done, TPB * s + kt - RING + 1)
                        for half in range(2):
                            act.wait_ge(e_ready, 2 * TPB * s + 2 * kt + half + 1)
                            nc.scalar.activation(probs[:, kt % RING, 1024 * half:1024 * half + 1024],
                                                 scoresT[:, half], ACT.Exp).then_inc(p_ready, 1)

            rounds(act, body)
            take_out(PAIRS - 1)

        @block.vector
        def _(dve):
            v = nc.vector
            ch = [0]

            def block_max(s, par, t, use):
                if t == 0:
                    wait(dve, most_ready, s - 1)
                for quarter in range(QB):
                    dve.wait_ge(m_ready, 4 * TPB * s + QB * t + quarter + 1)
                    v.reduce_max(top[:, par, t, quarter:quarter + 1], bank(use + quarter), AX.X).then_inc(m_used, 1)

            def pair_max(s, par):
                dve.wait_ge(m_used, 4 * TPB * (s + 1))
                wait(dve, mostT_ready, s)
                v.reduce_max(most[:], top[:, par], AX.X).then_inc(most_ready, 1)

            def normalise(s):
                dve.wait_ge(oT_ready, s + 1)
                out = bank(OUT_USE).rearrange("p (c j d) -> p c j d", j=QB, d=32)
                wait(dve, o_done, s)
                v.reciprocal(recip[:], out[:, :, :, DK]).then_inc(dve_s, 1)
                dve.wait_ge(dve_s, 2 * s + 1)
                v.tensor_scalar(recip[:], recip[:], mem.out_scale[:, 0:1], None, ALU.mult).then_inc(dve_s, 1)
                dve.wait_ge(dve_s, 2 * s + 2)
                v.tensor_tensor(mem.attn[:, ds(s, 1), :, :].rearrange("p o (j c) d -> p c (o j) d", c=QB),
                                out[:, :, :, 0:DK], recip[:, :, :].unsqueeze(3).to_broadcast([P, QB, QB, DK]),
                                ALU.mult).then_inc(o_done, 1)

            for t in range(TPB):
                block_max(0, 0, t, first_use(t, 0))
            pair_max(0, 0)
            for t in range(AHEAD):
                block_max(1, 1, t, second_use(t, 0))

            def body(r):
                for j in range(RING):
                    s = RING * r + j
                    for kt in range(TPB):
                        more, t = ahead(kt)
                        if kt == 3 and not (isinstance(r, int) and r == 0 and j == 0):
                            normalise(s - 1)
                        if kt == TPB - AHEAD and not is_last(r, j):
                            pair_max(s + 1, (j + 1) % 2)
                        if not is_last(r, j + more - 1):
                            block_max(s + more, (j + more) % 2, t, block_use(kt, 0))

            rounds(dve, body)
            normalise(PAIRS - 1)

        @block.tensor
        def _(pe):
            def free_bank(use, blocks, turned):
                if use - 3 in turned:
                    wait(pe, *turned[use - 3])
                elif use - 1 in turned or use - 2 in turned:
                    wait(pe, m_used, blocks - 1)
                else:
                    wait(pe, m_used, blocks - 2)

            def query_scores(s, r, j, t, quarter, use, turned):
                if t == 0 and quarter == 0:
                    pe.wait_ge(loaded[j % RING], LOADS * (r + j // RING + 1))
                free_bank(use, QB * (TPB * s + t) + quarter, turned)
                nc.tensor.matmul(bank(use), qst[0:STACK, j % RING, P * t:P * t + P],
                                 kst[0:STACK, j % RING, 512 * quarter:512 * quarter + 512],
                                 start=True, stop=True).then_inc(m_ready, 1)

            def key_scores(s, j, kt, half):
                if kt == 0 and half == 0:
                    pe.wait_ge(shift_ready, s + 1)
                wait(pe, p_ready, 2 * TPB * s + 2 * kt + half - 1)
                for q in range(2):
                    last = nc.tensor.matmul(scoresT[:, half, 512 * q:512 * q + 512],
                                            kst[0:STACK + SHIFT, j % RING, P * kt:P * kt + P],
                                            qst[0:STACK + SHIFT, j % RING, 1024 * half + 512 * q:1024 * half + 512 * q + 512],
                                            start=True, stop=True)
                last.then_inc(e_ready, 1)

            def weigh_values(s, j, kt):
                if kt == 0:
                    pe.wait_ge(v_staged, s + 1)
                    wait(pe, o_copied, s)
                pe.wait_ge(p_ready, 2 * TPB * s + 2 * kt + 2)
                for q in range(QB):
                    last = nc.tensor.matmul(outT[32 * q:32 * q + 32], mem.vstage[:, j % 2, kt, :],
                                            probs[:, kt % RING, 512 * q:512 * q + 512],
                                            start=kt == 0, stop=kt == TPB - 1)
                last.then_inc(pv_done, 1)

            def turn_out(s):
                pe.wait_ge(o_copied, s + 1)
                for c in range(QB):
                    last = nc.tensor.transpose(bank(OUT_USE)[:, P * c:P * c + P], oT[:, P * c:P * c + P], mem.ident[:])
                last.then_inc(oT_ready, 1)

            def turn_most(s, use=MOST_USE):
                pe.wait_ge(most_ready, s + 1)
                nc.tensor.transpose(bank(use)[0:SHIFT, 0:P], most[:], mem.ident[:]).then_inc(mostT_ready, 1)

            for t in range(TPB):
                for quarter in range(QB):
                    query_scores(0, 0, 0, t, quarter, first_use(t, quarter), {})
            turn_most(0, FIRST_MOST_USE)
            for t in range(AHEAD):
                for quarter in range(QB):
                    query_scores(1, 0, 1, t, quarter, second_use(t, quarter), {FIRST_MOST_USE: (mostT_cast, 1)})

            def body(r):
                for j in range(RING):
                    s = RING * r + j
                    for kt in range(TPB):
                        more, t = ahead(kt)

                        turned = {OUT_USE: (o_done, s), MOST_USE: (mostT_cast, s + 2)}
                        blocks = QB * (TPB * (s + 1) + kt + AHEAD + 1)

                        def beside(quarter):
                            if not is_last(r, j + more - 1):
                                query_scores(s + more, r, j + more, t, quarter, block_use(kt, quarter), turned)

                        beside(0)
                        key_scores(s, j, kt, 0)
                        beside(1)
                        key_scores(s, j, kt, 1)
                        beside(2)
                        beside(3)
                        if kt:
                            weigh_values(s, j, kt - 1)
                        elif not (isinstance(r, int) and r == 0 and j == 0):
                            weigh_values(s - 1, j - 1, TPB - 1)
                        if kt == TURN_OUT and not (isinstance(r, int) and r == 0 and j == 0):
                            if not is_last(r, j + more - 1):
                                free_bank(OUT_USE, blocks, turned)
                            turn_out(s - 1)
                        if kt == TURN_MOST and not is_last(r, j):
                            if not is_last(r, j + more - 1):
                                free_bank(MOST_USE, blocks, turned)
                            turn_most(s + 1)

            rounds(pe, body)
            weigh_values(PAIRS - 1, RING - 1, TPB - 1)
            pe.wait_ge(o_done, PAIRS - 1)
            turn_out(PAIRS - 1)




def normalise_rows(dve, v, ch, work, src, dst, eps, asked, answered, count):
    tiles = src.shape[1]
    for t in range(tiles):
        last = ch.mark(v.bn_stats(work.stats[:, t], src[:, t]))
    hold(dve, ch.sem, last, work.held)
    for t in range(tiles):
        last = ch.mark(v.bn_aggr(work.moments[:, t], work.stats[:, t]))
    dve.wait_ge(ch.sem, last)
    v.tensor_scalar(work.var[:, 0:tiles], work.moments[:, 0:tiles, 1], eps, None, ALU.add).then_inc(asked, 1)
    dve.wait_ge(answered, count)
    for t in range(tiles):
        last = v.tensor_scalar(dst[:, t], src[:, t], work.moments[:, t, 0:1], work.rstd[:, t:t + 1],
                               ALU.subtract, ALU.mult)
    return last


def mix_and_spike(nc, io, mem, sem):
    ctx = ExitStack()
    with ctx:
        def sb(name, shape, dt=F32):
            return ctx.enter_context(nc.sbuf_tensor(name, shape, dt))

        def ps(name, shape):
            return ctx.enter_context(nc.psum_tensor(name, shape, F32))

        HID = 4 * D
        KH = HID // P
        wo, wfc, wproj = sb("wo", [P, KD, D]), sb("wfc", [P, KD, HID]), sb("wproj", [P, KH, D])
        gamma, beta = sb("gamma", [P, D]), sb("beta", [P, D])
        scal = sb("c_scal", [P, 4])
        aT, x1T, hT = sb("aT", [P, KD, 512]), sb("x1T", [P, KD, 512]), sb("hT", [P, KH, 512])
        total, plain = sb("total", [P, GT, D]), sb("plain", [P, GT, D])
        heads_out, x1 = sb("heads_out", [P, GT, D]), sb("x1", [P, GT, D])
        y, count, rise, level = (sb(n, [P, GT, D]) for n in ("y", "count", "rise", "level"))
        work = Names()
        work.held = sem("c_held")
        work.stats, work.moments = sb("c_stats", [P, GT, 6]), sb("c_moments", [P, GT, 2])
        work.var, work.rstd = sb("c_var", [P, GT]), sb("c_rstd", [P, GT])
        turned, mixed, filled, spikes = (ps(n, [P, 2, 512]) for n in ("turned", "mixed", "filled", "spikes"))
        w_in, net_in, next_in = sem("c_w_in"), sem("c_net_in"), sem("c_next_in")
        sums_ready, heads_ready = sem("c_sums"), sem("c_heads")
        var_ready, rstd_ready = sem("c_var_ready"), sem("c_rstd_ready")
        aT_ready, aT_copied = sem("c_aT_ready"), sem("c_aT_copied")
        w_ready, w_used, x1_ready, x2_ready = sem("c_w_ready"), sem("c_w_used"), sem("c_x1_ready"), sem("c_x2_ready")
        x1_staged = sem("c_x1_staged")
        x1T_ready, x1T_copied = sem("c_x1T_ready"), sem("c_x1T_copied")
        f_ready, f_used, h_ready = sem("c_f_ready"), sem("c_f_used"), sem("c_h_ready")
        y_ready, y_copied = sem("c_y_ready"), sem("c_y_copied")
        dve_s = sem("c_dve")
        LINKS = 41

        block = ctx.enter_context(nc.Block())

        @block.sync
        def _(sp):
            for dst, src in ((gamma, io.gamma), (beta, io.beta), (wo, io.wo)):
                sp.dma_start(dst[:], src).then_inc(w_in, 16)
            for dst, src in ((wfc, io.wfc), (wproj, io.wproj)):
                sp.dma_start(dst[:], src).then_inc(net_in, 16)
            for dst, src in ((mem.l1q, io.l1q), (mem.l1k, io.l1k), (mem.l1v, io.l1v), (mem.l1g, io.l1g), (mem.l1u, io.l1u)):
                sp.dma_start(dst[:], src).then_inc(next_in, 16)
            sp.wait_ge(next_in, 5 * 16)

        @block.gpsimd
        def _(pool):
            def power(n):
                pool.wait_ge(var_ready, n)
                nc.gpsimd.tensor_tensor(work.rstd[:], work.var[:], mem.minus_half[:, 0:GT], ALU.pow).then_inc(rstd_ready, 1)

            def sums(g, b, slot):
                wait(pool, aT_ready, g)
                nc.gpsimd.tensor_copy(heads_out[:, :, :].rearrange("p t (h d) -> p h t d", d=DK),
                                      mem.attn[:, ds(HEADS * b, HEADS), ds(GT * slot, GT), :]).then_inc(heads_ready, 1)
                wait(pool, x1_ready, g)
                nc.gpsimd.tensor_tensor(total[:], mem.xs[:, ds(GT * g, GT), :], mem.enc[:, ds(GT * slot, GT), :], ALU.add).then_inc(sums_ready, 1)
                nc.gpsimd.tensor_tensor(plain[:], mem.xs[:, ds(GT * g, GT), :],
                                        beta[:, :].unsqueeze(1).to_broadcast([P, GT, D]), ALU.add).then_inc(sums_ready, 1)

            pool.wait_ge(w_in, 3 * 16)
            sums(0, 0, 0)
            power(1)
            power(2)
            sums(1, 0, 1)

            def round_of(g, more=True):
                power(3 * g + 3)
                power(3 * g + 4)
                if more:
                    sums(g + 2, (g + 2) // (TPB // GT), (g + 2) % (TPB // GT))
                power(3 * g + 5)

            run_rounds(pool, round_of, GROUPS - 2)
            round_of(GROUPS - 2, False)
            power(3 * GROUPS)

        @block.scalar
        def _(act):
            def copy_aT(g):
                act.wait_ge(aT_ready, g + 1)
                nc.scalar.activation(aT[:], turned[:], ACT.Copy).then_inc(aT_copied, 1)

            def net(g):
                act.wait_ge(x1T_ready, g + 1)
                nc.scalar.activation(x1T[:], turned[:], ACT.Copy).then_inc(x1T_copied, 1)
                for m in range(KH + 1):
                    if m < KH:
                        act.wait_ge(f_ready, KH * g + m + 1)
                        if m == 0:
                            wait(act, y_ready, g)
                        nc.scalar.activation(hT[:, m], filled[:, m % 2], ACT.Relu).then_inc(f_used, 1)
                    if m:
                        act.wait_ge(f_used, KH * g + m)
                        nc.scalar.activation(hT[:, m - 1], hT[:, m - 1], ACT.Square).then_inc(h_ready, 1)

            def stage_x1(g):
                act.wait_ge(x1_ready, g + 1)
                wait(act, x1T_ready, g)
                nc.scalar.activation(x1[:], mem.xs[:, ds(GT * g, GT), :], ACT.Copy).then_inc(x1_staged, 1)

            def copy_y(g):
                act.wait_ge(y_ready, g + 1)
                wait(act, x2_ready, g)
                nc.scalar.activation(y[:], spikes[:].rearrange("p a (c d) -> p (a c) d", d=D), ACT.Copy).then_inc(y_copied, 1)

            copy_aT(0)
            stage_x1(0)

            def round_of(g):
                net(g)
                copy_aT(g + 1)
                stage_x1(g + 1)
                copy_y(g)

            run_rounds(act, round_of, GROUPS - 1)
            net(GROUPS - 1)
            copy_y(GROUPS - 1)

        @block.vector
        def _(dve):
            v = nc.vector

            def wide(row):
                return row[:, :].unsqueeze(1).to_broadcast([P, GT, D])

            def norms(g, ch, n):
                dve.wait_ge(w_ready, g + 1)
                dve.wait_ge(sums_ready, 2 * g + 2)
                v.tensor_tensor(total[:], total[:], mixed[:].rearrange("p a (c d) -> p (a c) d", d=D), ALU.add).then_inc(w_used, 1)
                dve.wait_ge(w_used, g + 1)
                ch.link(normalise_rows(dve, v, ch, work, total, total, scal[:, 0:1], var_ready, rstd_ready, n))
                ch.link(v.tensor_tensor(total[:], total[:], wide(gamma), ALU.mult))
                ch.link(v.tensor_tensor(total[:], total[:], plain[:], ALU.add))
                normalise_rows(dve, v, ch, work, total, mem.xs[:, ds(GT * g, GT), :], 1e-5, var_ready, rstd_ready,
                               n + 1).then_inc(x1_ready, 1)

            def spike(g, ch, n):
                dve.wait_ge(y_copied, g + 1)
                ch.link(v.tensor_scalar(count[:], y[:], 1.0, None, ALU.is_gt))
                ch.link(v.scalar_tensor_tensor(rise[:], y[:], 0.9, y[:], ALU.mult, ALU.add))
                ch.link(v.tensor_tensor(level[:], count[:], rise[:], ALU.subtract))
                for step in range(3):
                    ch.mark(v.scalar_tensor_tensor(count[:], level[:], -1.0, count[:], ALU.is_lt, ALU.add))
                    ch.link(v.scalar_tensor_tensor(rise[:], level[:], -0.9, y[:], ALU.mult, ALU.add))
                    ch.link(v.scalar_tensor_tensor(level[:], level[:], -1.0, rise[:], ALU.is_lt, ALU.subtract))
                ch.link(v.scalar_tensor_tensor(count[:], level[:], -1.0, count[:], ALU.is_lt, ALU.add))
                xs = mem.xs[:, ds(GT * g, GT), :]
                dve.wait_ge(x1_staged, g + 1)
                ch.link(v.scalar_tensor_tensor(count[:], count[:], 0.2, xs, ALU.mult, ALU.add))
                normalise_rows(dve, v, ch, work, count, xs, 1e-5, var_ready, rstd_ready, n).then_inc(x2_ready, 1)

            ch = Chain(dve, dve_s)
            dve.wait_ge(w_in, 3 * 16)
            red, blue, yellow = (mem.rby[:, i:i + 1] for i in range(3))
            ch.link(v.tensor_scalar(scal[:, 0:1], blue, 1e-6, 1e-5, ALU.mult, ALU.add))
            ch.link(v.tensor_scalar(scal[:, 1:2], red, 0.1, 1.0, ALU.mult, ALU.add))
            ch.link(v.scalar_tensor_tensor(scal[:, 2:3], yellow, 0.05, scal[:, 1:2], ALU.mult, ALU.add))
            ch.link(v.tensor_scalar(gamma[:], gamma[:], scal[:, 2:3], None, ALU.mult))
            norms(0, ch, 1)
            base = ch.n

            def round_of(g):
                ch = Chain(dve, dve_s, base + LINKS * g)
                norms(g + 1, ch, 3 * g + 3)
                spike(g, ch, 3 * g + 5)
                assert ch.n == LINKS, ch.n

            run_rounds(dve, round_of, GROUPS - 1)
            spike(GROUPS - 1, Chain(dve, dve_s, base + LINKS * (GROUPS - 1)), 3 * GROUPS)

        @block.tensor
        def _(pe):
            def mix(g):
                wait(pe, x1T_copied, g)
                pe.wait_ge(heads_ready, g + 1)
                for t in range(GT):
                    for k in range(KD):
                        last = nc.tensor.transpose(turned[:, k, P * t:P * t + P], heads_out[:, t, P * k:P * k + P], mem.ident[:])
                last.then_inc(aT_ready, 1)
                pe.wait_ge(aT_copied, g + 1)
                wait(pe, w_used, g)
                for t in range(GT):
                    for k in range(KD):
                        last = nc.tensor.matmul(mixed[:, t // 2, D * (t % 2):D * (t % 2) + D], aT[:, k, P * t:P * t + P],
                                                wo[:, k], start=k == 0, stop=k == KD - 1)
                last.then_inc(w_ready, 1)

            def first(g):
                pe.wait_ge(x1_staged, g + 1)
                for t in range(GT):
                    for k in range(KD):
                        last = nc.tensor.transpose(turned[:, k, P * t:P * t + P], x1[:, t, P * k:P * k + P], mem.ident[:])
                last.then_inc(x1T_ready, 1)
                pe.wait_ge(x1T_copied, g + 1)
                for m in range(KH):
                    wait(pe, f_used, KH * g + max(m - 1, 0))
                    for k in range(KD):
                        last = nc.tensor.matmul(filled[:, m % 2], wfc[:, k, P * m:P * m + P], x1T[:, k], start=k == 0, stop=k == KD - 1)
                    last.then_inc(f_ready, 1)

            def second(g):
                pe.wait_ge(h_ready, KH * (g + 1))
                wait(pe, y_copied, g)
                for t in range(GT):
                    for k in range(KH):
                        last = nc.tensor.matmul(spikes[:, t // 2, D * (t % 2):D * (t % 2) + D], hT[:, k, P * t:P * t + P],
                                                wproj[:, k], start=k == 0, stop=k == KH - 1)
                last.then_inc(y_ready, 1)

            pe.wait_ge(w_in, 3 * 16)
            mix(0)
            pe.wait_ge(net_in, 2 * 16)

            def round_of(g):
                first(g)
                mix(g + 1)
                second(g)

            run_rounds(pe, round_of, GROUPS - 1)
            first(GROUPS - 1)
            second(GROUPS - 1)


def linear_attention_and_gate(nc, io, mem, sem):
    ctx = ExitStack()
    with ctx:
        def sb(name, shape, dt=F32):
            return ctx.enter_context(nc.sbuf_tensor(name, shape, dt))

        def ps(name, shape):
            return ctx.enter_context(nc.psum_tensor(name, shape, F32))

        NH = 8
        W = NH * P
        wq, wk, wv, wg, wu = mem.l1q, mem.l1k, mem.l1v, mem.l1g, mem.l1u
        wd = sb("d_wd", [P, NH, D])
        wide = [room[:, W * i:W * i + W].rearrange("p (h i) -> p h i", i=P)
                for room, n in ((mem.attn[:].rearrange("p a t d -> p (a t d)"), 8), (mem.enc[:].rearrange("p t d -> p (t d)"), 2))
                for i in range(n)]
        norm_in, norm_out, norm_mlp = sb("norm_in", [P, KD]), sb("norm_out", [P, 1]), sb("norm_mlp", [P, KD])
        causal, keep = sb("causal", [P, P]), sb("keep", [P, TILES + 1])
        square = sb("square", [P, D])
        wv_high, wv_low = sb("wv_high", [P, KD, W], F32R), sb("wv_low", [P, KD, W], F32R)
        wo_high, wo_low, wd_high, wd_low = (sb(f"d_{n}", [P, NH, D], F32R) for n in ("wo_high", "wo_low", "wd_high", "wd_low"))
        hT_high, hT_low = sb("hT_high", [P, KD, P], F32R), sb("hT_low", [P, KD, P], F32R)
        wo = mem.enc[:, NH:2 * NH]
        onT_high, onT_low, gu_high, gu_low = (sb(n, [P, NH, P], F32R) for n in ("onT_high", "onT_low", "gu_high", "gu_low"))
        ms, rs = sb("ms", [P, 2]), sb("rs", [P, 2])
        oms, ors = sb("oms", [P, NH]), sb("ors", [P, NH])
        h, h2 = sb("h", [P, D]), sb("h2", [P, D])
        hT, h2T = sb("d_hT", [P, KD, P]), sb("d_h2T", [P, KD, P])
        qT, kT, kt, v_, at, on, state, gate, guT, wide_square = wide
        mid, res = sb("mid", [P, D]), sb("res", [P, 1, D])
        work = Names()
        work.held = sem("d_held")
        work.stats, work.moments = sb("d_stats", [P, 1, 6]), sb("d_moments", [P, 1, 2])
        work.var, work.rstd = sb("d_var", [P, 1]), sb("d_rstd", [P, 1])
        A, B, C, E = (ps(n, [P, 2, 512]) for n in "ABCE")
        heads_of = lambda bank: bank[:].rearrange("p a (h i) -> p (a h) i", i=P)
        names = ("w_in out_in out_scaled w_high ready ms_eps oms_eps ms2_eps ms_ready rs_ready h_ready hT_ready hT_copied q_ready q_out k_ready k_out "
                 "v_ready v_out kt_ready kt_out at_ready at_out o_ready o_squared oms_ready hT_split ors_ready on_ready "
                 "kv_ready kv_used state_ready onT_ready onT_copied onT_split wo_ready mid_ready "
                 "ms2_ready rs2_ready h2_ready h2T_ready h2T_copied g_ready g_out u_ready gu_ready gu_copied gu_split d_ready d_used "
                 "var_ready rstd_ready x_ready dve_s pool_held act_held").split()
        S = {n: sem(f"d_{n}") for n in names}

        def rounds(eng, side_by_side):
            run_rounds(eng, lambda c: side_by_side(c, True), TILES - 2)
            side_by_side(TILES - 2, False)

        block = ctx.enter_context(nc.Block())

        @block.sync
        def _(sp):
            for dst, src in ((norm_in, io.norm_in), (norm_out, io.norm_out), (norm_mlp, io.norm_mlp), (causal, io.causal),
                             (keep, io.keep)):
                sp.dma_start(dst[:], src).then_inc(S["w_in"], 16)
            sp.dma_start(wo[:], io.l1o).then_inc(S["out_in"], 16)
            sp.dma_start(wd[:], io.l1d).then_inc(S["out_in"], 16)

        @block.gpsimd
        def _(pool):
            def input_root(c):
                hold(pool, S["ms_ready"], c + 1, S["pool_held"])
                nc.gpsimd.tensor_scalar(ms[:, 0:1], ms[:, 0:1], 1e-5, None, ALU.add).then_inc(S["ms_eps"], 1)
                pool.wait_ge(S["ms_eps"], c + 1)
                nc.gpsimd.tensor_tensor(rs[:, 0:1], ms[:, 0:1], mem.minus_half[:, 0:1], ALU.pow).then_inc(S["rs_ready"], 1)

            def output_roots(c):
                hold(pool, S["oms_ready"], c + 1, S["pool_held"])
                nc.gpsimd.tensor_scalar(oms[:], oms[:], 1.0 / P, 1e-5, ALU.mult, ALU.add).then_inc(S["oms_eps"], 1)
                pool.wait_ge(S["oms_eps"], c + 1)
                nc.gpsimd.tensor_tensor(ors[:], oms[:], mem.minus_half[:, 0:NH], ALU.pow).then_inc(S["ors_ready"], 1)

            def net_root(c):
                hold(pool, S["ms2_ready"], c + 1, S["pool_held"])
                nc.gpsimd.tensor_scalar(ms[:, 1:2], ms[:, 1:2], 1e-5, None, ALU.add).then_inc(S["ms2_eps"], 1)
                pool.wait_ge(S["ms2_eps"], c + 1)
                nc.gpsimd.tensor_tensor(rs[:, 1:2], ms[:, 1:2], mem.minus_half[:, 0:1], ALU.pow).then_inc(S["rs2_ready"], 1)

            def final_root(c):
                pool.wait_ge(S["var_ready"], c + 1)
                nc.gpsimd.tensor_tensor(work.rstd[:], work.var[:], mem.minus_half[:, 0:1], ALU.pow).then_inc(S["rstd_ready"], 1)

            def side_by_side(c, more):
                if more:
                    input_root(c + 2)
                output_roots(c + 1)
                final_root(c)
                net_root(c + 1)

            input_root(0)
            output_roots(0)
            input_root(1)
            net_root(0)
            rounds(pool, side_by_side)
            final_root(TILES - 1)

        @block.scalar
        def _(act):
            a = nc.scalar.activation

            def square_input(c):
                xs = mem.xs[:, ds(c, 1), :].rearrange("p o d -> p (o d)")
                a(square[:], xs, ACT.Square, scale=D ** -0.5, accum_out=ms[:, 0:1]).then_inc(S["ms_ready"], 1)

            def norm_input(c):
                xs = mem.xs[:, ds(c, 1), :].rearrange("p o d -> p (o d)")
                wait(act, S["hT_ready"], c)
                hold(act, S["rs_ready"], c + 1, S["act_held"])
                a(h[:], xs, ACT.Copy, scale=rs[:, 0:1]).then_inc(S["h_ready"], 1)

            def turn_input(c):
                act.wait_ge(S["hT_ready"], c + 1)
                wait(act, S["v_ready"], c)
                a(hT[:], E[:, 0, 0:D].rearrange("p (k t) -> p k t", k=KD), ACT.Copy).then_inc(S["hT_copied"], 1)

            def queries(c):
                act.wait_ge(S["q_ready"], c + 1)
                wait(act, S["o_ready"], c)
                a(qT[:], heads_of(A), ACT.Copy).then_inc(S["q_out"], 1)

            def values(c):
                act.wait_ge(S["v_ready"], c + 1)
                wait(act, S["kv_ready"], c)
                a(v_[:], heads_of(C), ACT.Copy).then_inc(S["v_out"], 1)

            def keys(c):
                act.wait_ge(S["kt_ready"], c + 1)
                a(kt[:], heads_of(E), ACT.Copy).then_inc(S["kt_out"], 1)

            def norm_output(c):
                act.wait_ge(S["o_ready"], c + 1)
                wait(act, S["oms_ready"], c)
                a(wide_square[:], heads_of(B), ACT.Square).then_inc(S["o_squared"], 1)

            def turn_output(c):
                act.wait_ge(S["onT_ready"], c + 1)
                wait(act, S["wo_ready"], c)
                a(onT_high[:], heads_of(C), ACT.Copy).then_inc(S["onT_copied"], 1)

            def net_input(c):
                act.wait_ge(S["mid_ready"], c + 1)
                a(square[:], mid[:], ACT.Square, scale=D ** -0.5, accum_out=ms[:, 1:2]).then_inc(S["ms2_ready"], 1)
                act.wait_ge(S["rs2_ready"], c + 1)
                wait(act, S["h2T_ready"], c)
                a(h2[:], mid[:], ACT.Copy, scale=rs[:, 1:2]).then_inc(S["h2_ready"], 1)

            def turn_net_input(c):
                act.wait_ge(S["h2T_ready"], c + 1)
                wait(act, S["u_ready"], c)
                a(h2T[:], E[:, 1, 0:D].rearrange("p (k t) -> p k t", k=KD), ACT.Copy).then_inc(S["h2T_copied"], 1)

            def silu(c):
                act.wait_ge(S["g_ready"], c + 1)
                wait(act, S["gu_ready"], c)
                a(gate[:], heads_of(C), ACT.Silu).then_inc(S["g_out"], 1)

            def gated(c):
                act.wait_ge(S["gu_ready"], c + 1)
                wait(act, S["d_ready"], c)
                a(gu_high[:], guT[:], ACT.Copy).then_inc(S["gu_copied"], 1)

            square_input(0)
            norm_input(0)
            turn_input(0)
            queries(0)
            values(0)
            keys(0)
            square_input(1)
            norm_output(0)
            norm_input(1)
            turn_input(1)
            turn_output(0)
            queries(1)
            net_input(0)

            def side_by_side(c, more):
                values(c + 1)
                turn_net_input(c)
                silu(c)
                keys(c + 1)
                if more:
                    square_input(c + 2)
                gated(c)
                if more:
                    norm_input(c + 2)
                norm_output(c + 1)
                if more:
                    turn_input(c + 2)
                turn_output(c + 1)
                if more:
                    queries(c + 2)
                net_input(c + 1)

            rounds(act, side_by_side)
            turn_net_input(TILES - 1)
            silu(TILES - 1)
            gated(TILES - 1)

        @block.vector
        def _(dve):
            v = nc.vector

            def split_input(c):
                dve.wait_ge(S["hT_copied"], c + 1)
                wait(dve, S["v_ready"], c)
                v.tensor_copy(hT_high[:], hT[:]).then_inc(S["hT_split"], 1)
                dve.wait_ge(S["hT_split"], 2 * c + 1)
                v.tensor_tensor(hT_low[:], hT[:], hT_high[:].bitcast(F32), ALU.subtract).then_inc(S["hT_split"], 1)

            def attention(c):
                dve.wait_ge(S["k_ready"], c + 1)
                wait(dve, S["at_ready"], c)
                v.tensor_copy(kT[:], heads_of(B)).then_inc(S["k_out"], 1)
                dve.wait_ge(S["at_ready"], c + 1)
                wait(dve, S["o_ready"], c)
                v.tensor_tensor(at[:], heads_of(A), causal[:, :].unsqueeze(1).to_broadcast([P, NH, P]), ALU.mult).then_inc(S["at_out"], 1)

            def output(c):
                dve.wait_ge(S["o_squared"], c + 1)
                wait(dve, S["ors_ready"], c)
                v.reduce_sum(oms[:], wide_square[:], AX.X).then_inc(S["oms_ready"], 1)
                dve.wait_ge(S["kv_ready"], c + 1)
                v.tensor_tensor(state[:], state[:], heads_of(A), ALU.add).then_inc(S["kv_used"], 1)
                dve.wait_ge(S["kv_used"], c + 1)
                v.tensor_scalar(state[:], state[:], keep[:, ds(c + 1, 1)], None, ALU.mult).then_inc(S["state_ready"], 1)
                dve.wait_ge(S["ors_ready"], c + 1)
                wait(dve, S["onT_ready"], c)
                v.tensor_tensor(on[:], heads_of(B), ors[:, :].unsqueeze(2).to_broadcast([P, NH, P]), ALU.mult).then_inc(S["on_ready"], 1)

            def split_output(c):
                dve.wait_ge(S["onT_copied"], c + 1)
                wait(dve, S["wo_ready"], c)
                v.tensor_tensor(onT_low[:], heads_of(C), onT_high[:].bitcast(F32), ALU.subtract).then_inc(S["onT_split"], 1)

            def gated(c):
                dve.wait_ge(S["g_out"], c + 1)
                dve.wait_ge(S["u_ready"], c + 1)
                wait(dve, S["gu_split"], c)
                v.tensor_tensor(guT[:], gate[:], heads_of(E), ALU.mult).then_inc(S["gu_ready"], 1)
                dve.wait_ge(S["gu_copied"], c + 1)
                wait(dve, S["d_ready"], c)
                v.tensor_tensor(gu_low[:], guT[:], gu_high[:].bitcast(F32), ALU.subtract).then_inc(S["gu_split"], 1)

            def add_net(c):
                dve.wait_ge(S["d_ready"], c + 1)
                wait(dve, S["x_ready"], c)
                v.tensor_tensor(res[:, 0], mid[:], E[:, 1, 0:D], ALU.add).then_inc(S["d_used"], 1)

            def finish(c):
                LINKS = 3
                ch = Chain(dve, S["dve_s"], LINKS * c)
                xs = mem.xs[:, ds(c, 1), :]
                dve.wait_ge(S["h2_ready"], c + 1)
                dve.wait_ge(S["d_used"], c + 1)
                ch.link(v.tensor_tensor(res[:], res[:], xs, ALU.add))
                normalise_rows(dve, v, ch, work, res, xs, 1e-5, S["var_ready"], S["rstd_ready"], c + 1).then_inc(S["x_ready"], 1)
                assert ch.n == LINKS

            def middle(c):
                dve.wait_ge(S["wo_ready"], c + 1)
                xs = mem.xs[:, ds(c, 1), :].rearrange("p o d -> p (o d)")
                v.tensor_tensor(mid[:], xs, B[:, 0, 0:D], ALU.add).then_inc(S["mid_ready"], 1)

            def split(w, high, low):
                v.tensor_copy(high[:], w[:]).then_inc(S["w_high"], 1)
                splits[0] += 1
                dve.wait_ge(S["w_high"], splits[0])
                return v.tensor_tensor(low[:], w[:], high[:].bitcast(F32), ALU.subtract)

            splits = [0]
            dve.wait_ge(S["w_in"], 5 * 16)
            v.memset(state[:], 0.0).then_inc(S["ready"], 1)
            for w, norm in ((wq, norm_in), (wv, norm_in), (wk, norm_in)):
                for k in range(KD):
                    v.tensor_scalar(w[:, k], w[:, k], norm[:, k:k + 1], None, ALU.mult).then_inc(S["ready"], 1)
            dve.wait_ge(S["ready"], 7)
            split(wv, wv_high, wv_low).then_inc(S["ready"], 1)
            split_input(0)
            attention(0)
            for w in (wg, wu):
                for k in range(KD):
                    v.tensor_scalar(w[:, k], w[:, k], norm_mlp[:, k:k + 1], None, ALU.mult).then_inc(S["out_scaled"], 1)
            dve.wait_ge(S["out_in"], 2 * 16)
            v.tensor_scalar(wo[:], wo[:], norm_out[:, 0:1], None, ALU.mult).then_inc(S["out_scaled"], 1)
            dve.wait_ge(S["out_scaled"], 5)
            split(wo, wo_high, wo_low).then_inc(S["out_scaled"], 1)
            output(0)
            split_output(0)
            split_input(1)
            split(wd, wd_high, wd_low).then_inc(S["out_scaled"], 1)
            middle(0)

            def side_by_side(c, more):
                attention(c + 1)
                gated(c)
                output(c + 1)
                add_net(c)
                split_output(c + 1)
                if more:
                    split_input(c + 2)
                finish(c)
                middle(c + 1)

            rounds(dve, side_by_side)
            gated(TILES - 1)
            add_net(TILES - 1)
            finish(TILES - 1)

        @block.tensor
        def _(pe):
            mm, turn = nc.tensor.matmul, nc.tensor.transpose
            bank = lambda X, i: X[:, i // 4, P * (i % 4):P * (i % 4) + P]

            def start(c):
                pe.wait_ge(S["h_ready"], c + 1)
                for k in range(KD):
                    last = turn(E[:, 0, P * k:P * k + P], h[:, P * k:P * k + P], mem.ident[:])
                last.then_inc(S["hT_ready"], 1)

            def products(out, high, low, w_high, w_low, terms):
                for n, (left, right) in enumerate(terms):
                    first, final = n == 0, n == len(terms) - 1
                    mm(out, left(high), right(w_high), start=first, stop=False)
                    mm(out, left(high), right(w_low), start=False, stop=False)
                    last = mm(out, left(low), right(w_high), start=False, stop=final)
                return last

            def project(w, X, i):
                for k in range(KD):
                    last = mm(bank(X, i), w[:, k, P * i:P * i + P], hT[:, k], start=k == 0, stop=k == KD - 1)
                return last

            def queries(c, heads):
                if heads[0] == 0:
                    pe.wait_ge(S["hT_copied"], c + 1)
                    wait(pe, S["kv_used"], c)
                for i in heads:
                    last = project(wq, A, i)
                if heads[-1] == NH - 1:
                    last.then_inc(S["q_ready"], 1)

            def keys(c):
                wait(pe, S["mid_ready"], c)
                for i in range(NH):
                    last = project(wk, B, i)
                last.then_inc(S["k_ready"], 1)

            def values(c):
                pe.wait_ge(S["hT_split"], 2 * c + 2)
                for half in range(2):
                    cols = slice(512 * half, 512 * half + 512)
                    last = products(C[:, half], hT_high, hT_low, wv_high, wv_low,
                                    [(lambda x, k=k: x[:, k], lambda w, k=k: w[:, k, cols]) for k in range(KD)])
                last.then_inc(S["v_ready"], 1)

            def turn_keys(c):
                pe.wait_ge(S["k_out"], c + 1)
                for i in range(NH):
                    last = turn(bank(E, i), kT[:, i], mem.ident[:])
                last.then_inc(S["kt_ready"], 1)

            def scores(c):
                pe.wait_ge(S["q_out"], c + 1)
                for i in range(NH):
                    last = mm(bank(A, i), kT[:, i], qT[:, i], start=True, stop=True)
                last.then_inc(S["at_ready"], 1)

            def outputs(c):
                pe.wait_ge(S["at_out"], c + 1)
                pe.wait_ge(S["v_out"], c + 1)
                wait(pe, S["state_ready"], c)
                for i in range(NH):
                    mm(bank(B, i), at[:, i], v_[:, i], start=True, stop=False)
                    last = mm(bank(B, i), qT[:, i], state[:, i], start=False, stop=True)
                last.then_inc(S["o_ready"], 1)

            def keys_values(c):
                pe.wait_ge(S["kt_out"], c + 1)
                for i in range(NH):
                    last = mm(bank(A, i), kt[:, i], v_[:, i], start=True, stop=True)
                last.then_inc(S["kv_ready"], 1)

            def turn_output(c):
                pe.wait_ge(S["on_ready"], c + 1)
                for i in range(NH):
                    last = turn(bank(C, i), on[:, i], mem.ident[:])
                last.then_inc(S["onT_ready"], 1)

            by_head = [(lambda x, i=i: x[:, i], lambda w, i=i: w[:, i]) for i in range(NH)]

            def output_projection(c):
                pe.wait_ge(S["onT_split"], c + 1)
                products(B[:, 0, 0:D], onT_high, onT_low, wo_high, wo_low, by_head).then_inc(S["wo_ready"], 1)

            def turn_net_input(c):
                pe.wait_ge(S["h2_ready"], c + 1)
                wait(pe, S["d_used"], c)
                for k in range(KD):
                    last = turn(E[:, 1, P * k:P * k + P], h2[:, P * k:P * k + P], mem.ident[:])
                last.then_inc(S["h2T_ready"], 1)

            def net(c, w, X, done):
                for i in range(NH):
                    for k in range(KD):
                        last = mm(bank(X, i), w[:, k, P * i:P * i + P], h2T[:, k], start=k == 0, stop=k == KD - 1)
                last.then_inc(done, 1)

            def down(c):
                pe.wait_ge(S["gu_split"], c + 1)
                products(E[:, 1, 0:D], gu_high, gu_low, wd_high, wd_low, by_head).then_inc(S["d_ready"], 1)

            EARLY = 2
            start(0)
            pe.wait_ge(S["ready"], 8)
            queries(0, range(NH))
            values(0)
            keys(0)
            turn_keys(0)
            scores(0)
            outputs(0)
            keys_values(0)
            pe.wait_ge(S["kt_out"], 1)
            start(1)
            queries(1, range(EARLY))
            turn_output(0)
            queries(1, range(EARLY, NH))
            pe.wait_ge(S["out_scaled"], 6)
            output_projection(0)
            pe.wait_ge(S["out_scaled"], 7)

            def side_by_side(c, more):
                values(c + 1)
                turn_net_input(c)
                keys(c + 1)
                pe.wait_ge(S["v_out"], c + 2)
                pe.wait_ge(S["h2T_copied"], c + 1)
                net(c, wg, C, S["g_ready"])
                turn_keys(c + 1)
                scores(c + 1)
                pe.wait_ge(S["kt_out"], c + 2)
                net(c, wu, E, S["u_ready"])
                outputs(c + 1)
                keys_values(c + 1)
                pe.wait_ge(S["gu_ready"], c + 1)
                if more:
                    start(c + 2)
                down(c)
                if more:
                    queries(c + 2, range(EARLY))
                pe.wait_ge(S["g_out"], c + 1)
                turn_output(c + 1)
                if more:
                    queries(c + 2, range(EARLY, NH))
                output_projection(c + 1)

            rounds(pe, side_by_side)
            turn_net_input(TILES - 1)
            pe.wait_ge(S["h2T_copied"], TILES)
            net(TILES - 1, wg, C, S["g_ready"])
            net(TILES - 1, wu, E, S["u_ready"])
            down(TILES - 1)


NE, TOP = 8, 2
MAX_TILES = TOP * TILES + NE


def route(nc, io, mem, moe, sem):
    ctx = ExitStack()
    with ctx:
        def sb(name, shape, dt=F32):
            return ctx.enter_context(nc.sbuf_tensor(name, shape, dt))

        def ps(name, shape):
            return ctx.enter_context(nc.psum_tensor(name, shape, F32))

        I32 = mybir.dt.int32
        wg, bg = sb("r_wg", [P, KD, NE]), sb("r_bg", [P, NE])
        later, earlier = sb("later", [P, NE, NE]), sb("earlier", [P, NE, NE])
        below, ones = sb("below", [P, P]), sb("ones", [P, P])
        tile_numbers = sb("tile_numbers", [P, MAX_TILES])
        x, xT = sb("r_x", [P, 2, GT, D]), sb("r_xT", [P, 2, KD, 512])
        gate, top, total = sb("r_gate", [P, TILES, NE]), sb("r_top", [P, TILES]), sb("r_total", [P, TILES])
        above, same = sb("above", [P, TILES, NE, NE], BF16), sb("same", [P, TILES, NE, NE], BF16)
        rank = sb("rank", [P, TILES, NE])
        weights, chosen = sb("weights", [P, TILES, NE]), sb("chosen", [P, TILES, NE])
        counts = [sb(f"counts{i}", [P, TILES, NE]) for i in range(2)]
        used, first_tile, after_tile, start = (sb(n, [P, NE]) for n in ("used", "first_tile", "after_tile", "start"))
        pairs = sb("pairs", [P, NE, NE])
        slots, match = sb("slots", [P, TILES, NE]), sb("match", [P, TILES, NE])
        high, low = sb("high", [P, TILES]), sb("low", [P, TILES])
        passed, expert = sb("passed", [P, MAX_TILES, NE]), sb("expert", [P, MAX_TILES])
        turned = ps("r_turned", [P, 2, 2, 512])
        sums = ps("r_sums", [P, 2, 512])
        names = ("w_in x_ready xT_ready xT_copied logit_ready logit_out shifted exp_ready "
                 "counts_ready sums_ready slots_ready scattered dve_s").split()
        S = {n: sem(f"r_{n}") for n in names}
        LOADS = 7

        def rounds(eng, pair_of_groups):
            run_rounds(eng, pair_of_groups, GROUPS // 2 - 1)
            pair_of_groups(GROUPS // 2 - 1)

        def is_final(r, j):
            return isinstance(r, int) and 2 * r + j == GROUPS - 1

        block = ctx.enter_context(nc.Block())

        @block.sync
        def _(sp):
            for dst, src in ((wg, io.wg), (bg, io.bg), (later, io.later), (earlier, io.earlier), (below, io.below),
                             (ones, io.ones), (tile_numbers, io.tile_numbers)):
                sp.dma_start(dst[:], src).then_inc(S["w_in"], 16)
            for dst, src in ((moe.w1, io.w1), (moe.w3, io.w3), (moe.w2, io.w2), (moe.b1, io.b1), (moe.b3, io.b3), (moe.b2, io.b2)):
                sp.dma_start(dst[:], src).then_inc(moe.w_in, 16)

        @block.gpsimd
        def _(pool):
            pool.wait_ge(S["slots_ready"], 2)
            for t in range(TILES):
                for i in range(TOP):
                    at = bass.IndirectOffsetOnAxis(ap=moe.slot[:, i, t:t + 1], axis=0)
                    nc.gpsimd.indirect_dma_start(io.sorted_x, at, mem.xs[:, t, :], None).then_inc(S["scattered"], 16)
            pool.wait_ge(S["scattered"], 16 * TOP * TILES)

        @block.scalar
        def _(act):
            a = nc.scalar.activation

            def copy_x(g, j):
                wait(act, S["xT_ready"], g - 1)
                a(x[:, j], mem.xs[:, ds(GT * g, GT), :], ACT.Copy).then_inc(S["x_ready"], 1)

            copy_x(0, 0)

            def groups(r):
                for j in range(2):
                    g = 2 * r + j
                    if not is_final(r, j):
                        copy_x(g + 1, 1 - j)
                    act.wait_ge(S["xT_ready"], g + 1)
                    wait(act, S["logit_ready"], g - 1)
                    a(xT[:, j], turned[:, j], ACT.Copy).then_inc(S["xT_copied"], 1)

            rounds(act, groups)
            act.wait_ge(S["shifted"], 1)
            a(gate[:], gate[:], ACT.Exp).then_inc(S["exp_ready"], 1)

        @block.vector
        def _(dve):
            v = nc.vector
            dve.wait_ge(S["w_in"], 16 * LOADS)

            def groups(r):
                for j in range(2):
                    g = 2 * r + j
                    dve.wait_ge(S["logit_ready"], g + 1)
                    v.tensor_tensor(gate[:, ds(GT * g, GT), :], sums[:, j, 0:GT * NE].rearrange("p (t e) -> p t e", e=NE),
                                    bg[:, :].unsqueeze(1).to_broadcast([P, GT, NE]), ALU.add).then_inc(S["logit_out"], 1)

            rounds(dve, groups)
            ch = Chain(dve, S["dve_s"])
            dve.wait_ge(S["logit_out"], GROUPS)
            ch.link(v.reduce_max(top[:], gate[:], AX.X))
            v.tensor_tensor(gate[:], gate[:], top[:, :].unsqueeze(2).to_broadcast([P, TILES, NE]), ALU.subtract).then_inc(S["shifted"], 1)
            dve.wait_ge(S["exp_ready"], 1)
            ch.link(v.reduce_sum(total[:], gate[:], AX.X))
            ch.link(v.reciprocal(total[:], total[:]))
            ch.link(v.tensor_tensor(gate[:], gate[:], total[:, :].unsqueeze(2).to_broadcast([P, TILES, NE]), ALU.mult))
            other = gate[:, :, :].unsqueeze(2).to_broadcast([P, TILES, NE, NE])
            own = gate[:, :, :].unsqueeze(3).to_broadcast([P, TILES, NE, NE])
            ch.mark(v.tensor_tensor(above[:], other, own, ALU.is_gt))
            ch.link(v.tensor_tensor(same[:], other, own, ALU.is_equal))
            ch.link(v.tensor_tensor(same[:], same[:], later[:, :, :].unsqueeze(1).to_broadcast([P, TILES, NE, NE]), ALU.mult))
            ch.link(v.tensor_tensor(above[:], above[:], same[:], ALU.add))
            ch.link(v.reduce_sum(rank[:], above[:], AX.X))
            ch.link(v.tensor_scalar(chosen[:], rank[:], TOP - 0.5, None, ALU.is_lt))
            src, step = chosen, 1
            while step < TILES:
                dst = counts[0] if src is not counts[0] else counts[1]
                ch.mark(v.tensor_copy(dst[:, 0:step], src[:, 0:step]))
                ch.link(v.tensor_tensor(dst[:, step:], src[:, step:], src[:, 0:TILES - step], ALU.add))
                src, step = dst, 2 * step
            count = src
            v.tensor_copy(used[:], count[:, TILES - 1, :]).then_inc(S["counts_ready"], 1)
            dve.wait_ge(S["sums_ready"], 1)
            magic = 1.5 * 2 ** 23
            ch.link(v.tensor_scalar(used[:], sums[:, 0, 64:64 + NE], 1.0 / P, (P - 1.0) / P - 0.5 + 1.0 / 512, ALU.mult, ALU.add))
            ch.link(v.tensor_scalar(used[:], used[:], magic, magic, ALU.add, ALU.subtract))
            ch.link(v.tensor_tensor(pairs[:], earlier[:], used[:, :].unsqueeze(1).to_broadcast([P, NE, NE]), ALU.mult))
            ch.link(v.reduce_sum(first_tile[:], pairs[:], AX.X))
            ch.mark(v.tensor_tensor(after_tile[:], first_tile[:], used[:], ALU.add))
            ch.link(v.tensor_scalar(start[:], first_tile[:], float(P), -1.0, ALU.mult, ALU.add))
            ch.link(v.tensor_tensor(start[:], start[:], sums[:, 0, 0:NE], ALU.add))
            ch.link(v.tensor_tensor(slots[:], count[:], start[:, :].unsqueeze(1).to_broadcast([P, TILES, NE]), ALU.add))
            ch.link(v.tensor_tensor(slots[:], slots[:], chosen[:], ALU.mult))
            ch.mark(v.reduce_max(high[:], slots[:], AX.X))
            ch.link(v.reduce_sum(low[:], slots[:], AX.X))
            ch.mark(v.tensor_copy(moe.slot[:, 0, :], high[:]))
            ch.link(v.tensor_tensor(low[:], low[:], high[:], ALU.subtract))
            v.tensor_copy(moe.slot[:, 1, :], low[:]).then_inc(S["slots_ready"], 1)
            ch.link(v.tensor_tensor(passed[:], tile_numbers[:, :].unsqueeze(2).to_broadcast([P, MAX_TILES, NE]),
                                    after_tile[:, :].unsqueeze(1).to_broadcast([P, MAX_TILES, NE]), ALU.is_ge))
            ch.link(v.reduce_sum(expert[:], passed[:], AX.X))
            ch.link(v.tensor_scalar(expert[:], expert[:], NE - 1.0, None, ALU.min))
            v.tensor_copy(moe.expert[:], expert[:]).then_inc(S["slots_ready"], 1)
            ch.link(v.scalar_tensor_tensor(weights[:], rank[:], TOP - 0.5, gate[:], ALU.is_lt, ALU.mult))
            ch.link(v.tensor_tensor(match[:], slots[:], high[:, :].unsqueeze(2).to_broadcast([P, TILES, NE]), ALU.is_equal))
            ch.link(v.tensor_tensor(match[:], match[:], weights[:], ALU.mult))
            ch.link(v.reduce_sum(moe.weight[:, 0, :], match[:], AX.X))
            ch.link(v.tensor_tensor(match[:], weights[:], match[:], ALU.subtract))
            ch.link(v.reduce_sum(moe.weight[:, 1, :], match[:], AX.X))

        @block.tensor
        def _(pe):
            mm, turn = nc.tensor.matmul, nc.tensor.transpose
            pe.wait_ge(S["w_in"], 16 * LOADS)

            def turn_x(g, j):
                pe.wait_ge(S["x_ready"], g + 1)
                wait(pe, S["xT_copied"], g - 1)
                for t in range(GT):
                    for k in range(KD):
                        last = turn(turned[:, j, k, P * t:P * t + P], x[:, j, t, P * k:P * k + P], mem.ident[:])
                last.then_inc(S["xT_ready"], 1)

            turn_x(0, 0)

            def groups(r):
                for j in range(2):
                    g = 2 * r + j
                    if not is_final(r, j):
                        turn_x(g + 1, 1 - j)
                    pe.wait_ge(S["xT_copied"], g + 1)
                    wait(pe, S["logit_out"], g - 1)
                    for t in range(GT):
                        for k in range(KD):
                            last = mm(sums[:, j, NE * t:NE * t + NE], xT[:, j, k, P * t:P * t + P], wg[:, k], start=k == 0, stop=k == KD - 1)
                    last.then_inc(S["logit_ready"], 1)

            rounds(pe, groups)
            pe.wait_ge(S["counts_ready"], 1)
            mm(sums[:, 0, 0:NE], below[:], used[:], start=True, stop=True)
            mm(sums[:, 0, 64:64 + NE], ones[:], used[:], start=True, stop=True).then_inc(S["sums_ready"], 1)


def run_experts(nc, io, mem, moe, sem):
    ctx = ExitStack()
    with ctx:
        def sb(name, shape, dt=F32):
            return ctx.enter_context(nc.sbuf_tensor(name, shape, dt))

        def ps(name, shape):
            return ctx.enter_context(nc.psum_tensor(name, shape, F32))

        HID = 512
        KH = HID // P
        x, xT = sb("m_x", [P, 2, D]), sb("m_xT", [P, 2, KD, P])
        h1, h3, h, hT = (sb(n, [P, 2, HID]) for n in ("m_h1", "m_h3", "m_h", "m_hT"))
        y = sb("m_y", [P, 2, D])
        first, third, turned, small = (ps(f"m_{n}", [P, 2, 512]) for n in ("first", "third", "turned", "small"))
        names = ("xT_ready xT_copied h1_ready h1_out h3_ready h3_out product h_ready hT_ready hT_copied y_ready y_out").split()
        S = {n: sem(f"m_{n}") for n in names}
        x_in, stored = [sem(f"m_x_in{j}") for j in range(2)], [sem(f"m_stored{j}") for j in range(2)]
        ROUNDS = MAX_TILES // 2
        block = ctx.enter_context(nc.Block())

        @block.sync
        def _(sp):
            def tiles(r):
                for j in range(2):
                    n = 2 * r + j
                    wait(sp, S["xT_ready"], n - 1)
                    sp.dma_start(x[:, j, :], io.sorted_x[ds(P * n, P), :]).then_inc(x_in[j], 16)

            run_rounds(sp, tiles, ROUNDS)

        @block.gpsimd
        def _(pool):
            def tiles(r):
                for j in range(2):
                    n = 2 * r + j
                    pool.wait_ge(S["y_out"], n + 1)
                    pool.dma_start(io.sorted_y[ds(P * n, P), :], y[:, j, :]).then_inc(stored[j], 16)

            run_rounds(pool, tiles, ROUNDS)
            for j in range(2):
                pool.wait_ge(stored[j], 16 * ROUNDS)

        @block.scalar
        def _(act):
            a = nc.scalar.activation

            def copy_x(n, j):
                act.wait_ge(S["xT_ready"], n + 1)
                wait(act, S["h3_ready"], n - 1)
                a(xT[:, j], small[:, 1 - j, 0:D].rearrange("p (k t) -> p k t", k=KD), ACT.Copy).then_inc(S["xT_copied"], 1)

            def net(n, j):
                act.wait_ge(S["product"], n + 1)
                wait(act, S["hT_ready"], n - 1)
                a(h[:, j], h1[:, j], ACT.Silu).then_inc(S["h_ready"], 1)
                act.wait_ge(S["hT_ready"], n + 1)
                wait(act, S["y_ready"], n - 1)
                a(hT[:, j], turned[:, j], ACT.Copy).then_inc(S["hT_copied"], 1)

            def tiles(r, final=False):
                for j in range(2):
                    n = 2 * r + j
                    net(n, j)
                    if not final:
                        copy_x(n + 2, j)

            copy_x(0, 0)
            copy_x(1, 1)
            run_rounds(act, tiles, ROUNDS - 1)
            tiles(ROUNDS - 1, True)

        @block.vector
        def _(dve):
            v = nc.vector
            dve.wait_ge(moe.w_in, 16 * 6)

            def biases(e, n, j):
                dve.wait_ge(S["h1_ready"], n + 1)
                wait(dve, S["h_ready"], n - 1)
                v.tensor_tensor(h1[:, j], first[:, j], moe.b1[:, ds(e, 1), :].rearrange("p o n -> p (o n)"), ALU.add).then_inc(S["h1_out"], 1)
                dve.wait_ge(S["h3_ready"], n + 1)
                v.tensor_tensor(h3[:, j], third[:, j], moe.b3[:, ds(e, 1), :].rearrange("p o n -> p (o n)"), ALU.add).then_inc(S["h3_out"], 1)
                dve.wait_ge(S["h3_out"], n + 1)
                v.tensor_tensor(h1[:, j], h1[:, j], h3[:, j], ALU.mult).then_inc(S["product"], 1)

            def output(e, n, r, j):
                dve.wait_ge(S["y_ready"], n + 1)
                wait(dve, stored[j], 16 * r)
                v.tensor_tensor(y[:, j], small[:, j, D:2 * D], moe.b2[:, ds(e, 1), :].rearrange("p o n -> p (o n)"), ALU.add).then_inc(S["y_out"], 1)

            def expert_of(n):
                return dve.value_load(moe.expert[0:1, ds(n, 1)], min_val=0, max_val=NE - 1)

            def tiles(r, final=False):
                for j in range(2):
                    n = 2 * r + j
                    if not (final and j == 1):
                        biases(expert_of(n + 1), n + 1, 1 - j)
                    output(expert_of(n), n, r, j)

            biases(expert_of(0), 0, 0)
            run_rounds(dve, tiles, ROUNDS - 1)
            tiles(ROUNDS - 1, True)

        @block.tensor
        def _(pe):
            mm, turn = nc.tensor.matmul, nc.tensor.transpose
            pe.wait_ge(moe.w_in, 16 * 6)

            def expert_of(n):
                return pe.value_load(moe.expert[0:1, ds(n, 1)], min_val=0, max_val=NE - 1)

            def turn_x(n, r, j):
                pe.wait_ge(x_in[j], 16 * (r + 1))
                wait(pe, S["y_out"], n - 2)
                for k in range(KD):
                    last = turn(small[:, 1 - j, P * k:P * k + P], x[:, j, P * k:P * k + P], mem.ident[:])
                last.then_inc(S["xT_ready"], 1)

            def up(e, n, j, w, bank, free, done):
                if w is moe.w1:
                    pe.wait_ge(S["xT_copied"], n + 1)
                wait(pe, S[free], n - 1)
                for k in range(KD):
                    last = mm(bank[:, j], xT[:, j, k], w[:, ds(e, 1), k, :].rearrange("p o n -> p (o n)"), start=k == 0, stop=k == KD - 1)
                last.then_inc(S[done], 1)

            def turn_h(n, j):
                pe.wait_ge(S["h_ready"], n + 1)
                wait(pe, S["hT_copied"], n - 1)
                for k in range(KH):
                    last = turn(turned[:, j, P * k:P * k + P], h[:, j, P * k:P * k + P], mem.ident[:])
                last.then_inc(S["hT_ready"], 1)

            def down(e, n, j):
                pe.wait_ge(S["hT_copied"], n + 1)
                for k in range(KH):
                    last = mm(small[:, j, D:2 * D], hT[:, j, P * k:P * k + P], moe.w2[:, ds(e, 1), k, :].rearrange("p o n -> p (o n)"),
                              start=k == 0, stop=k == KH - 1)
                last.then_inc(S["y_ready"], 1)

            def tiles(r, final=False):
                for j in range(2):
                    n = 2 * r + j
                    more = not (final and j == 1)
                    if more:
                        e = expert_of(n + 1)
                        up(e, n + 1, 1 - j, moe.w1, first, "h1_out", "h1_ready")
                    turn_h(n, j)
                    if not final:
                        turn_x(n + 2, r + 1, j)
                    if more:
                        up(e, n + 1, 1 - j, moe.w3, third, "h3_out", "h3_ready")
                    down(expert_of(n), n, j)

            turn_x(0, 0, 0)
            turn_x(1, 0, 1)
            up(expert_of(0), 0, 0, moe.w1, first, "h1_out", "h1_ready")
            up(expert_of(0), 0, 0, moe.w3, third, "h3_out", "h3_ready")
            run_rounds(pe, tiles, ROUNDS - 1)
            tiles(ROUNDS - 1, True)


def combine(nc, io, mem, moe, sem):
    ctx = ExitStack()
    with ctx:
        def sb(name, shape, dt=F32):
            return ctx.enter_context(nc.sbuf_tensor(name, shape, dt))

        def ps(name, shape):
            return ctx.enter_context(nc.psum_tensor(name, shape, F32))

        wf, bf = sb("o_wf", [P, KD, D]), sb("o_bf", [P, D])
        RING = 4
        back = sb("back", [P, RING, GT, TOP, D])
        mix, mixT, out = sb("o_mix", [P, 2, GT, D]), sb("o_mixT", [P, 2, KD, 512]), sb("o_out", [P, 2, GT, D])
        work = Names()
        work.held = sem("o_held")
        work.stats, work.moments = sb("o_stats", [P, GT, 6]), sb("o_moments", [P, GT, 2])
        work.var, work.rstd = sb("o_var", [P, GT]), sb("o_rstd", [P, GT])
        turned, projected = ps("o_turned", [P, 2, 2, 512]), ps("o_projected", [P, 2, 2, 512])
        names = "w_in mix_ready mT_ready mT_copied f_ready f_used var_ready rstd_ready done dve_s dve_mix".split()
        S = {n: sem(f"o_{n}") for n in names}
        fetched, stored = [sem(f"o_fetched{j}") for j in range(RING)], [sem(f"o_stored{j}") for j in range(2)]
        tiles_of = lambda bank: bank.rearrange("p a (c d) -> p (a c) d", d=D)
        block = ctx.enter_context(nc.Block())

        @block.sync
        def _(sp):
            sp.dma_start(wf[:], io.wf).then_inc(S["w_in"], 16)
            sp.dma_start(bf[:], io.bf).then_inc(S["w_in"], 16)

            def groups(r):
                for j in range(2):
                    g = 2 * r + j
                    sp.wait_ge(S["done"], g + 1)
                    sp.dma_start(io.out[:, ds(GT * g, GT), :], out[:, j]).then_inc(stored[j], 16)

            run_rounds(sp, groups, GROUPS // 2)
            for j in range(2):
                sp.wait_ge(stored[j], 16 * GROUPS // 2)

        @block.gpsimd
        def _(pool):
            def root(g):
                pool.wait_ge(S["var_ready"], g + 1)
                nc.gpsimd.tensor_tensor(work.rstd[:], work.var[:], mem.minus_half[:, 0:GT], ALU.pow).then_inc(S["rstd_ready"], 1)

            for g in range(GROUPS):
                wait(pool, S["mix_ready"], g - RING + 1)
                for t in range(GT):
                    for i in range(TOP):
                        at = bass.IndirectOffsetOnAxis(ap=moe.slot[:, i, GT * g + t:GT * g + t + 1], axis=0)
                        nc.gpsimd.indirect_dma_start(back[:, g % RING, t, i, :], None, io.sorted_y, at).then_inc(fetched[g % RING], 16)
                if g >= 2:
                    root(g - 2)
            root(GROUPS - 2)
            root(GROUPS - 1)

        @block.scalar
        def _(act):
            def groups(r):
                for j in range(2):
                    g = 2 * r + j
                    act.wait_ge(S["mT_ready"], g + 1)
                    wait(act, S["f_ready"], g - 1)
                    nc.scalar.activation(mixT[:, j], turned[:, j], ACT.Copy).then_inc(S["mT_copied"], 1)

            run_rounds(act, groups, GROUPS // 2)

        @block.vector
        def _(dve):
            v = nc.vector
            LINKS = 4 + 1 + 8
            dve.wait_ge(S["w_in"], 32)

            def mixing(g, r, j, ch):
                dve.wait_ge(fetched[j], 16 * TOP * GT * (r + 1))
                wait(dve, S["mT_ready"], g - 1)
                for t in range(GT):
                    last = ch.mark(v.tensor_scalar(mix[:, j % 2, t], back[:, j, t, 0], moe.weight[:, 0, ds(GT * g + t, 1)], None, ALU.mult))
                dve.wait_ge(ch.sem, last)
                for t in range(GT):
                    last = v.scalar_tensor_tensor(mix[:, j % 2, t], back[:, j, t, 1], moe.weight[:, 1, ds(GT * g + t, 1)], mix[:, j % 2, t],
                                                  ALU.mult, ALU.add)
                last.then_inc(S["mix_ready"], 1)

            def finish(g, stores, j, ch):
                dve.wait_ge(S["f_ready"], g + 1)
                wait(dve, stored[j % 2], 16 * stores)
                v.tensor_tensor(out[:, j % 2], tiles_of(projected[:, j % 2]), bf[:, :].unsqueeze(1).to_broadcast([P, GT, D]), ALU.add).then_inc(S["f_used"], 1)
                dve.wait_ge(S["f_used"], g + 1)
                ch.link(v.tensor_tensor(out[:, j % 2], out[:, j % 2], mem.xs[:, ds(GT * g, GT), :], ALU.add))
                normalise_rows(dve, v, ch, work, out[:, j % 2], out[:, j % 2], 1e-5, S["var_ready"], S["rstd_ready"], g + 1).then_inc(S["done"], 1)

            def groups(r):
                for j in range(RING):
                    g = RING * r + j
                    ch = Chain(dve, S["dve_s"], LINKS * g)
                    more = g < GROUPS - 1
                    if more:
                        mixing(g + 1, r + (j + 1) // RING, (j + 1) % RING, ch)
                    finish(g, 2 * r + j // 2, j, ch)
                    assert ch.n == LINKS or not more, ch.n

            ch = Chain(dve, S["dve_mix"], 0)
            mixing(0, 0, 0, ch)
            for r in range(GROUPS // RING):
                groups(r)

        @block.tensor
        def _(pe):
            mm, turn = nc.tensor.matmul, nc.tensor.transpose
            pe.wait_ge(S["w_in"], 32)

            def groups(r):
                for j in range(2):
                    g = 2 * r + j
                    pe.wait_ge(S["mix_ready"], g + 1)
                    wait(pe, S["mT_copied"], g - 1)
                    for t in range(GT):
                        for k in range(KD):
                            last = turn(turned[:, j, k, P * t:P * t + P], mix[:, j, t, P * k:P * k + P], mem.ident[:])
                    last.then_inc(S["mT_ready"], 1)
                    pe.wait_ge(S["mT_copied"], g + 1)
                    wait(pe, S["f_used"], g - 1)
                    for t in range(GT):
                        for k in range(KD):
                            last = mm(tiles_of(projected[:, j])[:, t], mixT[:, j, k, P * t:P * t + P], wf[:, k], start=k == 0, stop=k == KD - 1)
                    last.then_inc(S["f_ready"], 1)

            run_rounds(pe, groups, GROUPS // 2)


def build(nc, a, out, upto=9):
    ctx = ExitStack()
    with ctx:
        sems = []

        def sem(name):
            sems.append(nc.alloc_semaphore(name=name))
            return sems[-1]

        io, mem = Names(), Names()
        io.x = a["L0_attn_x"].rearrange("b s d -> (b s) d")
        io.wq, io.wk, io.wv, io.wo = (a[f"L0_attn_W{n}"].rearrange("(k p) n -> p k n", p=P) for n in "qkvo")
        io.bq, io.bk = (a[f"L0_attn_b{n}"] for n in "qk")
        io.bv = a["L0_attn_bv"].partition_broadcast(P)
        io.rby = a["L0_attn_rby"].partition_broadcast(P)
        io.pos, io.powers, io.ident, io.delta = (a[n] for n in ("pos", "powers", "ident", "delta"))
        io.powers = io.powers.partition_broadcast(P)
        io.q_parts = nc.dram_tensor("q_parts", (PARTS, BATCH, D, SEQ), BF16, kind="Internal").ap()
        io.k_parts = nc.dram_tensor("k_parts", (PARTS, BATCH, D, SEQ), BF16, kind="Internal").ap()

        io.bo, io.gamma, io.beta = (a[n].partition_broadcast(P) for n in ("L0_attn_bo", "L0_attn_ln_gamma", "L0_attn_ln_beta"))
        io.wfc = a["L0_ffn_W_fc"].rearrange("(k p) n -> p k n", p=P)
        io.wproj = a["L0_ffn_W_proj"].rearrange("(k p) n -> p k n", p=P)

        io.norm_in, io.norm_out, io.norm_mlp = (a[f"L1_attn_{n}"] for n in ("attn_norm_w", "attn_out_norm_w", "mlp_norm_w"))
        io.l1q, io.l1k, io.l1v, io.l1o, io.l1g, io.l1u, io.l1d = (
            a[f"L1_attn_W{n}"].rearrange("(k p) n -> p k n", p=P) for n in ("q", "k", "v", "o", "gate", "up", "down"))
        io.causal, io.keep = a["causal"], a["keep"].partition_broadcast(P)

        io.w1, io.w3, io.w2 = (a[f"L1_ffn_W{n}"].rearrange("e (k p) n -> p e k n", p=P) for n in "132")
        io.b1, io.b3, io.b2 = (a[f"L1_ffn_b{n}"].rearrange("e n -> (e n)").partition_broadcast(P).rearrange("p (e n) -> p e n", e=NE) for n in "132")
        io.sorted_x = nc.dram_tensor("sorted_x", (MAX_TILES * P, D), F32, kind="Internal").ap()
        io.sorted_y = nc.dram_tensor("sorted_y", (MAX_TILES * P, D), F32, kind="Internal").ap()
        io.earlier, io.below, io.ones = a["earlier"], a["below"], a["ones"]
        io.tile_numbers = a["tile_numbers"].partition_broadcast(P)
        io.wg, io.wf = (a[f"L1_ffn_W{n}"].rearrange("(k p) n -> p k n", p=P) for n in "gf")
        io.bg, io.bf = (a[f"L1_ffn_b{n}"].partition_broadcast(P) for n in "gf")
        io.later = a["later"]
        io.out = out.rearrange("b s d -> (b s) d").rearrange("(t p) d -> p t d", p=P)

        def sb(c, name, shape, dt=F32):
            return c.enter_context(nc.sbuf_tensor(name, shape, dt))

        mem.xs = sb(ctx, "xs", [P, TILES, D])
        mem.ident = sb(ctx, "ident", [P, P])
        mem.minus_half = sb(ctx, "minus_half", [P, 8])
        mem.rby = sb(ctx, "rby", [P, 3])
        mem.logit_scale, mem.out_scale = sb(ctx, "logit_scale", [P, 1]), sb(ctx, "out_scale", [P, 1])
        first = ctx.enter_context(ExitStack())
        mem.enc = sb(first, "enc", [P, TPB, D])
        mem.attn = sb(first, "attn", [P, PAIRS, TPB, DK])
        heads = first.enter_context(ExitStack())
        mem.delta = sb(heads, "delta", [SHIFT, SEQ], BF16)
        mem.values = sb(heads, "values", [P, PAIRS, TPB, VW])
        mem.vstage = sb(heads, "vstage", [P, 2, TPB, 32])
        mem.qst = sb(heads, "qst", [P, 4, SEQ], BF16)
        mem.kst = sb(heads, "kst", [P, 4, SEQ], BF16)
        embed_and_project(nc, io, mem, sem)
        if upto < 2: return
        attend(nc, io, mem, sem)
        heads.close()
        if upto < 3: return
        mem.l1q, mem.l1k, mem.l1v, mem.l1g, mem.l1u = (sb(first, f"l1_w{n}", [P, KD, 4 * D]) for n in "qkvgu")
        mix_and_spike(nc, io, mem, sem)
        if upto < 4: return
        nc.clear_and_free_semaphores(sems)
        nc.all_engine_barrier()
        linear_attention_and_gate(nc, io, mem, sem)
        first.close()
        if upto < 5: return
        moe = Names()
        moe.slot = sb(ctx, "e_slot", [P, TOP, TILES], mybir.dt.uint32)
        moe.expert = sb(ctx, "e_expert", [P, MAX_TILES], mybir.dt.int32)
        moe.weight = sb(ctx, "e_weight", [P, TOP, TILES])
        nets = ctx.enter_context(ExitStack())
        moe.w1, moe.w3 = sb(nets, "e_w1", [P, NE, KD, 512]), sb(nets, "e_w3", [P, NE, KD, 512])
        moe.w2 = sb(nets, "e_w2", [P, NE, 4, D])
        moe.b1, moe.b3, moe.b2 = sb(nets, "e_b1", [P, NE, 512]), sb(nets, "e_b3", [P, NE, 512]), sb(nets, "e_b2", [P, NE, D])
        moe.w_in = sem("e_w_in")
        route(nc, io, mem, moe, sem)
        if upto < 6: return
        run_experts(nc, io, mem, moe, sem)
        nets.close()
        if upto < 7: return
        combine(nc, io, mem, moe, sem)


def layout(inputs):
    a = {n: np.ascontiguousarray(v) for n, v in inputs.items()}
    for n in ("L0_attn_Wq", "L0_attn_Wk", "L0_attn_Wv", "L0_attn_Wo", "L0_ffn_W_fc", "L0_ffn_W_proj"):
        a[n] = np.ascontiguousarray(a[n].T)
    for n in ("L0_attn_bq", "L0_attn_bk", "L1_attn_attn_norm_w", "L1_attn_attn_out_norm_w", "L1_attn_mlp_norm_w"):
        a[n] = np.ascontiguousarray(a[n].reshape(-1, P).T)
    a["pos"] = (np.arange(TPB)[None, :] * P + np.arange(P)[:, None]).astype(np.float32)
    a["powers"] = np.power(np.float32(10000.0), np.float32(2.0) * np.arange(0, D, 2, dtype=np.float32) / np.float32(D)).astype(np.float32)
    a["below"] = np.triu(np.ones((P, P), np.float32), 1)
    a["ones"] = np.ones((P, P), np.float32)
    a["tile_numbers"] = np.arange(MAX_TILES).astype(np.float32)
    a["earlier"] = np.ascontiguousarray(np.broadcast_to(np.tril(np.ones((NE, NE), np.float32), -1), (P, NE, NE)))
    a["later"] = np.ascontiguousarray(np.broadcast_to(np.triu(np.ones((8, 8), np.float32), 1), (P, 8, 8)))
    a["causal"] = np.triu(np.ones((P, P), np.float32))
    a["keep"] = (np.arange(TILES + 1) % TPB != 0).astype(np.float32)
    a["ident"] = np.eye(P, dtype=np.float32)
    a["delta"] = np.repeat(np.eye(SHIFT), P, axis=1).astype(mybir.dt.np(BF16))
    return {f"in_{n}": v for n, v in a.items()}


def kernel(**inputs):
    import concourse.bacc as bacc
    from concourse.bass_utils import run_bass_kernel_spmd

    nc = bacc.Bacc("TRN2", target_bir_lowering=False, num_devices=1)
    arrays = layout(inputs)
    a = {n[len("in_"):]: nc.dram_tensor(n, v.shape, mybir.dt.from_np(v.dtype), kind="ExternalInput").ap()
         for n, v in arrays.items()}
    out = nc.dram_tensor("out", (BATCH, SEQ, D), F32, kind="ExternalOutput").ap()
    build(nc, a, out)
    return run_bass_kernel_spmd(nc, [arrays], core_ids=[0]).results[0]["out"]
```
